# Optimizing a Trainium2 kernel written in Bass

```python
import numpy as np
import jax
import jax.numpy as jnp

def _softmax(x, axis=-1):
    return jax.nn.softmax(x, axis=axis)

def _gelu(x):
    return jax.nn.gelu(x, approximate=True)

def _silu(x):
    return jax.nn.silu(x)

def _sigmoid(x):
    return jax.nn.sigmoid(x)

def _layernorm(x, axis=-1, eps=1e-05):
    m = jnp.mean(x, axis=axis, keepdims=True)
    v = jnp.var(x, axis=axis, keepdims=True)
    return (x - m) / jnp.sqrt(v + eps)

def _scatter_add(tgt, idx, src, axis=0):
    return tgt.at[idx].add(src)

def _segment_sum(src, seg, n):
    return jax.ops.segment_sum(src, seg, n)
kernel_name = 'mk_adaln_d2_jaxref_r8_953294'

def setup_inputs(seed: int=0):
    np.random.seed(seed)
    _w = jnp.asarray

    def _L0_attn_setup():
        import jax, jax.numpy as jnp
        import numpy as np
        H, KV, HD, HID = (32, 8, 128, 512)
        THETA, FACTOR, HI_FF, LO_FF, ORIG_MAX = (500000.0, 8.0, 4.0, 1.0, 1024)

        def _llama3_inv_freq():
            inv = 1.0 / THETA ** (np.arange(0, HD, 2, dtype=np.float64) / HD)
            wavelen = 2.0 * np.pi / inv
            low_wl = ORIG_MAX / LO_FF
            high_wl = ORIG_MAX / HI_FF
            smooth = (ORIG_MAX / wavelen - LO_FF) / (HI_FF - LO_FF)
            scaled = np.where(wavelen > low_wl, inv / FACTOR, inv)
            mid = (wavelen <= low_wl) & (wavelen >= high_wl)
            scaled = np.where(mid, (1 - smooth) * inv / FACTOR + smooth * inv, scaled)
            return scaled.astype(np.float32)

        def _rope_cos_sin(T):
            inv = _llama3_inv_freq()
            pos = np.arange(T, dtype=np.float32)
            freqs = pos[:, None] * inv[None, :]
            emb = np.concatenate([freqs, freqs], axis=-1)
            return (jnp.asarray(np.cos(emb)), jnp.asarray(np.sin(emb)))

        def _rotate_half(x):
            x1, x2 = jnp.split(x, 2, axis=-1)
            return jnp.concatenate([-x2, x1], axis=-1)
        key = jax.random.key(seed)
        ks = jax.random.split(key, 5)
        s = 1.0 / np.sqrt(HID)
        return {'x': jax.random.normal(ks[0], (1, 256, HID), jnp.float32), 'wq': jax.random.normal(ks[1], (HID, H * HD), jnp.float32) * s, 'wk': jax.random.normal(ks[2], (HID, KV * HD), jnp.float32) * s, 'wv': jax.random.normal(ks[3], (HID, KV * HD), jnp.float32) * s, 'wo': jax.random.normal(ks[4], (H * HD, HID), jnp.float32) * s}
    _L0_attn_in = _L0_attn_setup()

    def _L0_ffn_setup():
        import jax, jax.numpy as jnp
        import numpy as np
        DIM = 512
        INTER = 128
        E = 16
        GROUPS = 4
        LIM = 2
        K = 2
        SHARED_INTER = 2 * INTER
        SCALE = 1.0
        key = jax.random.key(seed)
        ks = jax.random.split(key, 16)

        def n(k, shape, s=0.02):
            return jax.random.normal(k, shape, jnp.float32) * s
        return {'x': jax.random.normal(ks[0], (1, 256, DIM), jnp.float32), 'router_w': n(ks[1], (DIM, E)), 'router_b': n(ks[2], (E,)), 'router_bias': n(ks[3], (E,), 1.0), 'ew1': n(ks[4], (E, DIM, INTER)), 'eb1': n(ks[5], (E, INTER)), 'ew2': n(ks[6], (E, DIM, INTER)), 'eb2': n(ks[7], (E, INTER)), 'ew3': n(ks[8], (E, INTER, DIM)), 'eb3': n(ks[9], (E, DIM)), 'sw1': n(ks[10], (DIM, SHARED_INTER)), 'sb1': n(ks[11], (SHARED_INTER,)), 'sw2': n(ks[12], (DIM, SHARED_INTER)), 'sb2': n(ks[13], (SHARED_INTER,)), 'sw3': n(ks[14], (SHARED_INTER, DIM)), 'sb3': n(ks[15], (DIM,))}
    _L0_ffn_in = _L0_ffn_setup()
    _L0_c = _w((lambda *s: np.random.randn(*s).astype(np.float32) * 0.05)(2, 512))
    _L0_wmod = _w((lambda *s: np.random.randn(*s).astype(np.float32) * 0.05)(512, 6 * 512) * 512 ** (-0.5))

    def _L1_attn_setup():
        import jax, jax.numpy as jnp
        import numpy as np
        NEG_INF = -1e+30

        def rotary_pos_emb(x):
            B, T, H, D = x.shape
            exponents = (jnp.arange(0, D, 2)[:D // 2] // D).astype(jnp.float32)
            freqs = 1.0 / jnp.power(jnp.float32(1000.0), exponents)
            theta = jnp.arange(T, dtype=jnp.float32)[:, None] * freqs[None, :]
            cos = jnp.cos(theta)[None, :, None, :]
            sin = jnp.sin(theta)[None, :, None, :]
            xr = x.astype(jnp.float32).reshape(B, T, H, D // 2, 2)
            x0, x1 = (xr[..., 0], xr[..., 1])
            out = jnp.stack([x0 * cos - x1 * sin, x0 * sin + x1 * cos], axis=-1)
            return out.reshape(B, T, H, D).astype(x.dtype)

        def attention_fwd(x, wq, wk, wv, wo, n_heads=32):
            B, T, C = x.shape
            hd = C // n_heads
            xq = (x @ wq.T).reshape(B, T, n_heads, hd)
            xk = (x @ wk.T).reshape(B, T, n_heads, hd)
            xv = (x @ wv.T).reshape(B, T, n_heads, hd)
            xq = rotary_pos_emb(xq)
            xk = rotary_pos_emb(xk)
            scale = hd ** (-0.5)
            scores = jnp.einsum('bqhd,bkhd->bhqk', xq, xk) * scale
            causal = jnp.tril(jnp.ones((T, T), dtype=bool))
            scores = jnp.where(causal[None, None], scores, NEG_INF)
            probs = jax.nn.softmax(scores.astype(jnp.float32), axis=-1).astype(xq.dtype)
            out = jnp.einsum('bhqk,bkhd->bqhd', probs, xv).reshape(B, T, C)
            return out @ wo.T
        key = jax.random.key(seed)
        ks = jax.random.split(key, 5)
        B, T, C = (2, 256, 512)
        s = 0.02
        return {'x': jax.random.normal(ks[0], (B, T, C), jnp.float32), 'wq': jax.random.normal(ks[1], (C, C), jnp.float32) * s, 'wk': jax.random.normal(ks[2], (C, C), jnp.float32) * s, 'wv': jax.random.normal(ks[3], (C, C), jnp.float32) * s, 'wo': jax.random.normal(ks[4], (C, C), jnp.float32) * s}
    _L1_attn_in = _L1_attn_setup()

    def _L1_ffn_setup():
        import jax, jax.numpy as jnp
        import numpy as np
        import math
        E, DK, R = (8, 32, 16)
        SCALING = 16.0 / 16.0
        key = jax.random.key(seed)
        ks = jax.random.split(key, 7)
        Bt, S, Din, Dout = (4, 256, 512, 512)
        x = jax.random.normal(ks[0], (Bt, S, Din), jnp.float32)
        W = jax.random.normal(ks[1], (Dout, Din), jnp.float32) * 0.02
        b = jnp.zeros((Dout,), jnp.float32)
        Wq = jax.random.normal(ks[2], (E * DK, Din), jnp.float32) * 0.02
        Wk = jax.random.normal(ks[3], (E * DK, Din), jnp.float32) * 0.02
        A = jax.random.normal(ks[4], (E, R, Din), jnp.float32) * 0.02
        Bm = jax.random.normal(ks[5], (E, Dout, R), jnp.float32) * 0.02
        return {'x': x, 'W': W, 'b': b, 'Wq': Wq, 'Wk': Wk, 'A': A, 'Bm': Bm}
    _L1_ffn_in = _L1_ffn_setup()
    _L1_c = _w((lambda *s: np.random.randn(*s).astype(np.float32) * 0.05)(2, 512))
    _L1_wmod = _w((lambda *s: np.random.randn(*s).astype(np.float32) * 0.05)(512, 6 * 512) * 512 ** (-0.5))
    _d = {'L0_attn_x': _L0_attn_in['x'], 'L0_attn_wq': _L0_attn_in['wq'], 'L0_attn_wk': _L0_attn_in['wk'], 'L0_attn_wv': _L0_attn_in['wv'], 'L0_attn_wo': _L0_attn_in['wo'], 'L0_ffn_router_w': _L0_ffn_in['router_w'], 'L0_ffn_router_b': _L0_ffn_in['router_b'], 'L0_ffn_router_bias': _L0_ffn_in['router_bias'], 'L0_ffn_ew1': _L0_ffn_in['ew1'], 'L0_ffn_eb1': _L0_ffn_in['eb1'], 'L0_ffn_ew2': _L0_ffn_in['ew2'], 'L0_ffn_eb2': _L0_ffn_in['eb2'], 'L0_ffn_ew3': _L0_ffn_in['ew3'], 'L0_ffn_eb3': _L0_ffn_in['eb3'], 'L0_ffn_sw1': _L0_ffn_in['sw1'], 'L0_ffn_sb1': _L0_ffn_in['sb1'], 'L0_ffn_sw2': _L0_ffn_in['sw2'], 'L0_ffn_sb2': _L0_ffn_in['sb2'], 'L0_ffn_sw3': _L0_ffn_in['sw3'], 'L0_ffn_sb3': _L0_ffn_in['sb3'], 'L0_c': _L0_c, 'L0_wmod': _L0_wmod, 'L1_attn_wq': _L1_attn_in['wq'], 'L1_attn_wk': _L1_attn_in['wk'], 'L1_attn_wv': _L1_attn_in['wv'], 'L1_attn_wo': _L1_attn_in['wo'], 'L1_ffn_W': _L1_ffn_in['W'], 'L1_ffn_b': _L1_ffn_in['b'], 'L1_ffn_Wq': _L1_ffn_in['Wq'], 'L1_ffn_Wk': _L1_ffn_in['Wk'], 'L1_ffn_A': _L1_ffn_in['A'], 'L1_ffn_Bm': _L1_ffn_in['Bm'], 'L1_c': _L1_c, 'L1_wmod': _L1_wmod}
    _x0 = _d['L0_attn_x']
    _d['L0_attn_x'] = jax.random.normal(jax.random.fold_in(jax.random.key(seed), 1), (2, 512, 512), dtype=_x0.dtype)
    del _x0
    return _d

def reference(L0_attn_x, L0_attn_wq, L0_attn_wk, L0_attn_wv, L0_attn_wo, L0_ffn_router_w, L0_ffn_router_b, L0_ffn_router_bias, L0_ffn_ew1, L0_ffn_eb1, L0_ffn_ew2, L0_ffn_eb2, L0_ffn_ew3, L0_ffn_eb3, L0_ffn_sw1, L0_ffn_sb1, L0_ffn_sw2, L0_ffn_sb2, L0_ffn_sw3, L0_ffn_sb3, L0_c, L0_wmod, L1_attn_wq, L1_attn_wk, L1_attn_wv, L1_attn_wo, L1_ffn_W, L1_ffn_b, L1_ffn_Wq, L1_ffn_Wk, L1_ffn_A, L1_ffn_Bm, L1_c, L1_wmod):

    def _L0_attn_ref(x, wq, wk, wv, wo):
        import jax, jax.numpy as jnp
        import numpy as np
        H, KV, HD, HID = (32, 8, 128, 512)
        THETA, FACTOR, HI_FF, LO_FF, ORIG_MAX = (500000.0, 8.0, 4.0, 1.0, 1024)

        def _llama3_inv_freq():
            inv = 1.0 / THETA ** (np.arange(0, HD, 2, dtype=np.float64) / HD)
            wavelen = 2.0 * np.pi / inv
            low_wl = ORIG_MAX / LO_FF
            high_wl = ORIG_MAX / HI_FF
            smooth = (ORIG_MAX / wavelen - LO_FF) / (HI_FF - LO_FF)
            scaled = np.where(wavelen > low_wl, inv / FACTOR, inv)
            mid = (wavelen <= low_wl) & (wavelen >= high_wl)
            scaled = np.where(mid, (1 - smooth) * inv / FACTOR + smooth * inv, scaled)
            return scaled.astype(np.float32)

        def _rope_cos_sin(T):
            inv = _llama3_inv_freq()
            pos = np.arange(T, dtype=np.float32)
            freqs = pos[:, None] * inv[None, :]
            emb = np.concatenate([freqs, freqs], axis=-1)
            return (jnp.asarray(np.cos(emb)), jnp.asarray(np.sin(emb)))

        def _rotate_half(x):
            x1, x2 = jnp.split(x, 2, axis=-1)
            return jnp.concatenate([-x2, x1], axis=-1)
        B, T, _ = x.shape
        q = (x @ wq).reshape(B, T, H, HD).transpose(0, 2, 1, 3)
        k = (x @ wk).reshape(B, T, KV, HD).transpose(0, 2, 1, 3)
        v = (x @ wv).reshape(B, T, KV, HD).transpose(0, 2, 1, 3)
        cos, sin = _rope_cos_sin(T)
        q = q * cos + _rotate_half(q) * sin
        k = k * cos + _rotate_half(k) * sin
        rep = H // KV
        k = jnp.repeat(k, rep, axis=1)
        v = jnp.repeat(v, rep, axis=1)
        scores = jnp.einsum('bhtd,bhsd->bhts', q, k) * (1.0 / np.sqrt(HD))
        mask = jnp.tril(jnp.ones((T, T), dtype=bool))
        scores = jnp.where(mask, scores, -jnp.inf)
        att = jax.nn.softmax(scores, axis=-1)
        out = jnp.einsum('bhts,bhsd->bhtd', att, v)
        out = out.transpose(0, 2, 1, 3).reshape(B, T, H * HD)
        return out @ wo

    def _L0_ffn_ref(x, router_w, router_b, router_bias, ew1, eb1, ew2, eb2, ew3, eb3, sw1, sb1, sw2, sb2, sw3, sb3):
        import jax, jax.numpy as jnp
        import numpy as np
        DIM = 512
        INTER = 128
        E = 16
        GROUPS = 4
        LIM = 2
        K = 2
        SHARED_INTER = 2 * INTER
        SCALE = 1.0
        shape = x.shape
        xt = x.reshape(-1, DIM)
        T = xt.shape[0]
        logits = xt @ router_w + router_b
        scores = jax.nn.softmax(logits.astype(jnp.float32), axis=-1) + router_bias
        g = scores.reshape(T, GROUPS, E // GROUPS)
        _, gidx = jax.lax.top_k(g.max(axis=-1), LIM)
        keep = jnp.zeros((T, GROUPS), bool).at[jnp.arange(T)[:, None], gidx].set(True)
        masked = jnp.where(keep[:, :, None], g, -jnp.inf).reshape(T, E)
        _, idx = jax.lax.top_k(masked, K)
        vals = (jnp.take_along_axis(scores, idx, axis=1) * SCALE).astype(x.dtype)
        gate = jnp.zeros((T, E), x.dtype).at[jnp.arange(T)[:, None], idx].add(vals)

        def step(y, p):
            w1, b1, w2, b2, w3, b3, ge = p
            h = jax.nn.silu(xt @ w1 + b1) * (xt @ w2 + b2)
            return (y + ge[:, None] * (h @ w3 + b3), None)
        y, _ = jax.lax.scan(step, jnp.zeros_like(xt), (ew1, eb1, ew2, eb2, ew3, eb3, gate.T))
        z = jax.nn.silu(xt @ sw1 + sb1) * (xt @ sw2 + sb2) @ sw3 + sb3
        return (y + z).reshape(shape)

    def _L1_attn_ref(x, wq, wk, wv, wo):
        import jax, jax.numpy as jnp
        import numpy as np
        NEG_INF = -1e+30

        def rotary_pos_emb(x):
            B, T, H, D = x.shape
            exponents = (jnp.arange(0, D, 2)[:D // 2] // D).astype(jnp.float32)
            freqs = 1.0 / jnp.power(jnp.float32(1000.0), exponents)
            theta = jnp.arange(T, dtype=jnp.float32)[:, None] * freqs[None, :]
            cos = jnp.cos(theta)[None, :, None, :]
            sin = jnp.sin(theta)[None, :, None, :]
            xr = x.astype(jnp.float32).reshape(B, T, H, D // 2, 2)
            x0, x1 = (xr[..., 0], xr[..., 1])
            out = jnp.stack([x0 * cos - x1 * sin, x0 * sin + x1 * cos], axis=-1)
            return out.reshape(B, T, H, D).astype(x.dtype)

        def attention_fwd(x, wq, wk, wv, wo, n_heads=32):
            B, T, C = x.shape
            hd = C // n_heads
            xq = (x @ wq.T).reshape(B, T, n_heads, hd)
            xk = (x @ wk.T).reshape(B, T, n_heads, hd)
            xv = (x @ wv.T).reshape(B, T, n_heads, hd)
            xq = rotary_pos_emb(xq)
            xk = rotary_pos_emb(xk)
            scale = hd ** (-0.5)
            scores = jnp.einsum('bqhd,bkhd->bhqk', xq, xk) * scale
            causal = jnp.tril(jnp.ones((T, T), dtype=bool))
            scores = jnp.where(causal[None, None], scores, NEG_INF)
            probs = jax.nn.softmax(scores.astype(jnp.float32), axis=-1).astype(xq.dtype)
            out = jnp.einsum('bhqk,bkhd->bqhd', probs, xv).reshape(B, T, C)
            return out @ wo.T
        return attention_fwd(x, wq, wk, wv, wo)

    def _L1_ffn_ref(x, W, b, Wq, Wk, A, Bm):
        import jax, jax.numpy as jnp
        import numpy as np
        import math
        E, DK, R = (8, 32, 16)
        SCALING = 16.0 / 16.0
        Bt, S, Din = x.shape
        result = jnp.einsum('bsi,oi->bso', x, W) + b
        q = jnp.einsum('bsi,ni->bsn', x, Wq).reshape(Bt, S, E, DK)
        k = jnp.einsum('bsi,ni->bsn', x, Wk).reshape(Bt, S, E, DK)
        scores = jnp.einsum('bsed,bsed->bse', q, k) / math.sqrt(DK)
        w = jax.nn.softmax(scores, axis=-1)
        h = jnp.einsum('bsi,eri->bser', x, A)
        combined = jnp.einsum('bse,bser,eor->bso', w, h, Bm) * SCALING
        return result + combined
    x = L0_attn_x
    mod = (_silu(L0_c) @ L0_wmod).reshape(L0_c.shape[0], 6, 1, -1)
    sa, ca, ga, sb, cb, gb = (mod[:, 0], mod[:, 1], mod[:, 2], mod[:, 3], mod[:, 4], mod[:, 5])
    ga = (2 * (ga >= 0) - 1) * jnp.maximum(jnp.abs(ga), 0.25)
    gb = (2 * (gb >= 0) - 1) * jnp.maximum(jnp.abs(gb), 0.25)
    h = _layernorm(x, axis=-1) * (1 + ca) + sa
    x = x + ga * _L0_attn_ref(h, L0_attn_wq, L0_attn_wk, L0_attn_wv, L0_attn_wo)
    h = _layernorm(x, axis=-1) * (1 + cb) + sb
    x = x + gb * _L0_ffn_ref(h, L0_ffn_router_w, L0_ffn_router_b, L0_ffn_router_bias, L0_ffn_ew1, L0_ffn_eb1, L0_ffn_ew2, L0_ffn_eb2, L0_ffn_ew3, L0_ffn_eb3, L0_ffn_sw1, L0_ffn_sb1, L0_ffn_sw2, L0_ffn_sb2, L0_ffn_sw3, L0_ffn_sb3)
    mod = (_silu(L1_c) @ L1_wmod).reshape(L1_c.shape[0], 6, 1, -1)
    sa, ca, ga, sb, cb, gb = (mod[:, 0], mod[:, 1], mod[:, 2], mod[:, 3], mod[:, 4], mod[:, 5])
    ga = (2 * (ga >= 0) - 1) * jnp.maximum(jnp.abs(ga), 0.25)
    gb = (2 * (gb >= 0) - 1) * jnp.maximum(jnp.abs(gb), 0.25)
    h = _layernorm(x, axis=-1) * (1 + ca) + sa
    x = x + ga * _L1_attn_ref(h, L1_attn_wq, L1_attn_wk, L1_attn_wv, L1_attn_wo)
    h = _layernorm(x, axis=-1) * (1 + cb) + sb
    x = x + gb * _L1_ffn_ref(h, L1_ffn_W, L1_ffn_b, L1_ffn_Wq, L1_ffn_Wk, L1_ffn_A, L1_ffn_Bm)
    return x

_drawn_inputs = setup_inputs


def setup_inputs(seed=0):
    import zlib

    import numpy as np

    out = dict(_drawn_inputs(seed))
    spreads = {'L1_ffn_b': (0.0, 1.432)}
    factors = {'L0_ffn_router_w': 8.0,
     'L0_ffn_router_b': 8.0,
     'L0_ffn_ew1': 3.392,
     'L0_ffn_eb1': 8.0,
     'L0_ffn_ew2': 3.344,
     'L0_ffn_eb2': 8.0,
     'L0_ffn_ew3': 3.305,
     'L0_ffn_eb3': 4.102,
     'L0_ffn_sw1': 6.68,
     'L0_ffn_sb1': 8.0,
     'L0_ffn_sw2': 6.514,
     'L0_ffn_sb2': 8.0,
     'L0_ffn_sw3': 6.532,
     'L0_ffn_sb3': 8.0,
     'L1_attn_wq': 8.0,
     'L1_attn_wk': 8.0,
     'L1_attn_wv': 7.621,
     'L1_attn_wo': 7.712,
     'L1_ffn_Wq': 8.0,
     'L1_ffn_Wk': 8.0,
     'L1_ffn_A': 8.0,
     'L1_ffn_Bm': 8.0}
    for name, (base, spread) in spreads.items():
        noise = np.random.default_rng([zlib.crc32(name.encode()), seed]).standard_normal(out[name].shape)
        drawn = base * np.exp(spread * noise) if base else spread * noise
        out[name] = jnp.asarray(drawn.astype(out[name].dtype))
    for name, factor in factors.items():
        out[name] = (out[name] * factor).astype(out[name].dtype)
    return out
```

```python
from contextlib import ExitStack

import numpy as np

import concourse.bass as bass
from concourse import mybir

F32 = mybir.dt.float32
F32R = mybir.dt.float32r
BF16 = mybir.dt.bfloat16
ALU = mybir.AluOpType
ACT = mybir.ActivationFunctionType
AX_X = mybir.AxisListType.X

P = 128
B, T, D = 2, 512, 512
KT = D // P
TT = T // P
NT = B * TT
EPS = 1e-5

H0, KV0, HD0 = 32, 8, 128
REP = H0 // KV0
PAIRS = KV0 // 2
E0, INTER, GROUPS = 16, 128, 4
EX = E0 + 2
H1, HD1 = 32, 16
VW = HD1 + 1
E1, DK1, R1 = 8, 32, 16
NEG = -1e30



def rope_tables():
    theta, factor, hi_ff, lo_ff, orig = 500000.0, 8.0, 4.0, 1.0, 1024
    inv = 1.0 / theta ** (np.arange(0, HD0, 2, dtype=np.float64) / HD0)
    wavelen = 2.0 * np.pi / inv
    low_wl, high_wl = orig / lo_ff, orig / hi_ff
    smooth = (orig / wavelen - lo_ff) / (hi_ff - lo_ff)
    scaled = np.where(wavelen > low_wl, inv / factor, inv)
    mid = (wavelen <= low_wl) & (wavelen >= high_wl)
    scaled = np.where(mid, (1 - smooth) * inv / factor + smooth * inv, scaled).astype(np.float32)
    freqs = np.arange(T, dtype=np.float32)[:, None] * scaled[None, :]
    emb = np.concatenate([freqs, freqs], axis=-1)
    cos, sin = np.cos(emb).T, np.sin(emb).T
    sin = np.concatenate([sin[:HD0 // 2], -sin[HD0 // 2:]], axis=0)
    return np.stack([cos, sin], axis=1).astype(np.float32)


def rope1_tables():
    pos = np.arange(T, dtype=np.float32)
    both = np.stack([np.cos(pos), np.sin(pos)]).reshape(2, TT, P)
    both = np.stack([both * float(HD1) ** -0.5, both])
    return np.ascontiguousarray(both.transpose(3, 0, 1, 2)).astype(np.float32)


def pick_rows():
    n = 2 * KT * B
    return np.ascontiguousarray(np.broadcast_to(np.eye(n, dtype=np.float32)[:, :, None], (n, n, P)))



class Shared:
    pass


def semaphores(nc, scope):
    taken = []

    def give_back():
        nc.clear_and_free_semaphores(taken)
        nc.all_engine_barrier()

    scope.callback(give_back)

    def new(name):
        taken.append(nc.alloc_semaphore(name))
        return taken[-1]
    return new


def three_passes(pe, out, left, right, k, start, stop):
    (lh, ll), (rh, rl) = left, right
    pe.matmul(out, lh, rh, start=start, stop=False)
    pe.matmul(out, lh, rl, start=False, stop=False)
    return pe.matmul(out, ll, rh, start=False, stop=stop)


def passed(pool, g):
    pool.sem_inc(g.passed, 1)


class Chain:

    def __init__(self, eng, sem):
        self.eng, self.sem, self.n = eng, sem, 0

    def __call__(self, ins):
        self.n += 1
        ins.then_inc(self.sem, 1)
        self.eng.wait_ge(self.sem, self.n)


class Modulation:

    def __init__(self, nc, ctx, g, name, c_cols, wmod, banks):
        sb = lambda n, s: ctx.enter_context(nc.sbuf_tensor(f"{name}_{n}", s, F32))
        sem = lambda n: g.sem(f"{name}_{n}")
        self.g, self.c_cols, self.wmod_dram = g, c_cols, wmod
        self.c = sb("c", [P, KT, B])
        self.silu_c = sb("silu_c", [P, KT, B])
        self.wmod = sb("wmod", [P, KT, 6, D])
        self.gate = sb("gate", [P, 2, KT * B])
        self.sign = sb("sign", [P, 2, KT * B])
        self.mag = sb("mag", [P, 2, KT * B])
        self.gate_t = sb("gate_t", [2 * KT * B, P])
        self.mod_bank, self.turn_bank, self.row_banks = banks[0], banks[0], banks[1:3]
        (self.c_in, self.silu, self.cols, self.cols_sb, self.chain, self.turned, self.turned_sb, self.rows, self.rows_sb) = (
            sem(n) for n in ("c_in", "silu", "cols", "cols_sb", "chain", "turned", "turned_sb", "rows", "rows_sb"))
        self.w_in = [sem(f"w_in{m}") for m in range(6)]

    def load(self, sync, first=range(6)):
        sync.dma_start(self.c[:, :, :], self.c_cols).then_inc(self.c_in, 16)
        for m in first:
            sync.dma_start(self.wmod[:, :, m, :],
                           self.wmod_dram.rearrange("(k p) n -> p k n", p=P)[:, :, m * D:(m + 1) * D])\
                .then_inc(self.w_in[m], 16)

    def act(self, act):
        act.wait_ge(self.c_in, 16)
        act.activation(self.silu_c[:, :, :], self.c[:, :, :], ACT.Silu).then_inc(self.silu, 1)

    def pe(self, pe):
        g = self.g
        pe.wait_ge(self.silu, 1)
        for m in range(6):
            pe.wait_ge(self.w_in[m], 16)
            for j in range(KT):
                col = (m * KT + j) * B
                for k in range(KT):
                    mm = pe.matmul(self.mod_bank[:, col:col + B], self.wmod[:, k, m, j * P:(j + 1) * P],
                                   self.silu_c[:, k, :], start=(k == 0), stop=(k == KT - 1))
            mm.then_inc(self.cols, 1)

    def pe_rows(self, pe):
        g = self.g
        pe.wait_ge(self.chain, 6)
        pe.transpose(self.turn_bank[0:2 * KT * B, 0:P], self.gate[:, :, :].rearrange("p a n -> p (a n)"), g.ident[:, :])\
            .then_inc(self.turned, 1)
        pe.wait_ge(self.turned_sb, 1)
        for n in range(2 * B):
            which, b = n // B, n % B
            if n >= 2:
                pe.wait_ge(self.rows_sb, n - 1)
            for j in range(KT):
                mm = pe.matmul(self.row_banks[n % 2][:, j * P:(j + 1) * P],
                               g.pick[:, (which * KT + j) * B + b, :], self.gate_t[:, :],
                               start=True, stop=True)
            mm.then_inc(self.rows, 1)

    def dve_columns(self, dve, mod):
        link = Chain(dve, self.chain)
        cols = self.mod_bank[:, 0:6 * KT * B].rearrange("p (m n) -> p m n", m=6)
        dve.wait_ge(self.cols, 6)
        link(dve.tensor_copy(mod[:, :, :], cols))
        link(dve.tensor_scalar(mod[:, 1:5:3, :], mod[:, 1:5:3, :], 1.0, None, ALU.add))
        ga = mod[:, 2:6:3, :]
        link(dve.scalar_tensor_tensor(out=self.mag[:, :, :], in0=ga, scalar=-1.0, in1=ga,
                                      op0=ALU.mult, op1=ALU.max))
        link(dve.tensor_scalar(self.sign[:, :, :], ga, 0.0, 2.0, ALU.is_ge, ALU.mult))
        link(dve.tensor_scalar(self.mag[:, :, :], self.mag[:, :, :], 0.25, None, ALU.max))
        link(dve.scalar_tensor_tensor(out=self.gate[:, :, :], in0=self.sign[:, :, :], scalar=-1.0,
                                      in1=self.mag[:, :, :], op0=ALU.add, op1=ALU.mult))

    def dve_rows(self, dve, gate_rows):
        dve.wait_ge(self.turned, 1)
        dve.tensor_copy(self.gate_t[:, :], self.turn_bank[0:2 * KT * B, 0:P]).then_inc(self.turned_sb, 1)
        for n in range(2 * B):
            which, b = n // B, n % B
            dve.wait_ge(self.rows, n + 1)
            dve.tensor_copy(gate_rows[:, which, b, :], self.row_banks[n % 2][:, :]).then_inc(self.rows_sb, 1)


class Norm:

    def __init__(self, nc, ctx, g, name, scale, shift, gate=None, x_dram=None, mod_ready=None):
        sb = lambda n, s, t=F32: ctx.enter_context(nc.sbuf_tensor(f"{name}_{n}", s, t))
        sem = lambda n: g.sem(f"{name}_{n}")
        self.g, self.scale, self.shift, self.gate = g, scale, shift, gate
        self.x_dram, self.mod_ready = x_dram, mod_ready
        self.xn = sb("xn", [P, NT, D])
        self.hf = sb("hf", [P, KT, B * T])
        self.gy = sb("gy", [P, 2, D])
        self.stats = sb("stats", [P, NT, 6])
        self.mv = sb("mv", [P, NT, 2])
        self.var = sb("var", [P, NT])
        self.std = sb("std", [P, NT])
        self.rstd = sb("rstd", [P, NT])
        self.fix = sb("fix", [P, NT])
        (self.gated, self.summed, self.chain, self.var_ready, self.std_ready, self.normed, self.turned, self.affine, self.split_hi, self.split_lo) = (
            sem(n) for n in ("gated", "summed", "chain", "var_ready", "std_ready", "normed", "turned", "affine", "split_hi", "split_lo"))
        self.x_in = [sem(f"x_in{t}") for t in range(NT)] if x_dram is not None else None

    def load(self, sync, tiles=range(8)):
        for t in tiles:
            sync.dma_start(self.g.x[:, t, :], self.x_dram[t * P:(t + 1) * P, :]).then_inc(self.x_in[t], 16)

    def dve_stats(self, dve):
        g = self.g
        link = Chain(dve, self.chain)
        for b in range(B):
            tiles = range(b * TT, (b + 1) * TT)
            if self.gate is not None:
                for t in tiles:
                    if t >= 2:
                        dve.wait_ge(self.summed, t - 1)
                    dve.tensor_tensor(self.gy[:, t % 2, :], g.y[:, t, :], g.gate_rows[:, self.gate, b, :],
                                      ALU.mult).then_inc(self.gated, 1)
            for t in tiles:
                if self.gate is not None:
                    dve.wait_ge(self.summed, t + 1)
                else:
                    dve.wait_ge(self.x_in[t], 16)
                last = dve.bn_stats(self.stats[:, t, :], g.x[:, t, :])
            link(last)
            for t in tiles:
                last = dve.bn_aggr(self.mv[:, t, :], self.stats[:, t, :])
            link(last)
            h = slice(b * TT, (b + 1) * TT)
            dve.tensor_scalar(self.var[:, h], self.mv[:, h, 1], EPS, None, ALU.add).then_inc(self.var_ready, 1)
            dve.wait_ge(self.std_ready, b + 1)
            link(dve.reciprocal(self.rstd[:, h], self.std[:, h]))
            link(dve.tensor_tensor(self.fix[:, h], self.rstd[:, h], self.rstd[:, h], ALU.mult))
            link(dve.tensor_tensor(self.fix[:, h], self.fix[:, h], self.var[:, h], ALU.mult))
            link(dve.tensor_scalar(self.fix[:, h], self.fix[:, h], -0.5, 1.5, ALU.mult, ALU.add))
            link(dve.tensor_tensor(self.rstd[:, h], self.rstd[:, h], self.fix[:, h], ALU.mult))
            for t in tiles:
                dve.tensor_scalar(self.xn[:, t, :], g.x[:, t, :], self.mv[:, t, 0:1], self.rstd[:, t:t + 1],
                                  ALU.subtract, ALU.mult).then_inc(self.normed, 1)

    def dve_split(self, dve):
        g = self.g
        for b in range(B):
            for k in range(KT):
                dve.wait_ge(self.split_hi, b * KT + k + 1)
                cols = slice(b * T, (b + 1) * T)
                dve.tensor_tensor(g.hl[:, k, cols], self.hf[:, k, cols], g.hh[:, k, cols].bitcast(F32),
                                  ALU.subtract).then_inc(self.split_lo, 1)

    def act(self, act):
        g = self.g
        for b in range(B):
            h = slice(b * TT, (b + 1) * TT)
            act.wait_ge(self.var_ready, b + 1)
            act.activation(self.std[:, h], self.var[:, h], ACT.Sqrt).then_inc(self.std_ready, 1)
        if self.mod_ready is not None:
            act.wait_ge(*self.mod_ready)
        for b in range(B):
            for k in range(KT):
                act.wait_ge(self.turned, b * KT + k + 1)
                act.activation(self.hf[:, k, b * T:(b + 1) * T], g.bank[k][:, :], ACT.Identity,
                               scale=g.mod[:, self.scale, k * B + b:k * B + b + 1],
                               bias=g.mod[:, self.shift, k * B + b:k * B + b + 1]).then_inc(self.affine, 1)

    def pe(self, pe):
        g = self.g
        for b in range(B):
            pe.wait_ge(self.normed, (b + 1) * TT)
            for k in range(KT):
                if b:
                    pe.wait_ge(self.affine, k + 1)
                for t in range(TT):
                    mm = pe.transpose(g.bank[k][:, t * P:(t + 1) * P],
                                      self.xn[:, b * TT + t, k * P:(k + 1) * P], g.ident[:, :])
                mm.then_inc(self.turned, 1)

    def pool(self, pool):
        g = self.g
        if self.gate is not None:
            for t in range(NT):
                if self.x_in is not None:
                    pool.wait_ge(self.x_in[t], 16)
                pool.wait_ge(self.gated, t + 1)
                pool.tensor_tensor(g.x[:, t, :], g.x[:, t, :], self.gy[:, t % 2, :], ALU.add)\
                    .then_inc(self.summed, 1)
        for b in range(B):
            for k in range(KT):
                pool.wait_ge(self.affine, b * KT + k + 1)
                cols = slice(b * T, (b + 1) * T)
                pool.tensor_copy(g.hh[:, k, cols], self.hf[:, k, cols]).then_inc(self.split_hi, 1)



STEPS = 2 * B
KINDS = ("S", "T", "PV", "O", "OUT", "PROJ", "V")


def attention_order(more):
    ops = []

    def tail(s, u):
        n = u + 1
        seq = [("T", s, u, 0)] + ([("T", s, u, 1)] if n > 1 else [])
        for j in range(n):
            seq.append(("PV", s, u, j))
            if j + 2 < n:
                seq.append(("T", s, u, j + 2))
        return seq

    for s in range(STEPS):
        extra = {}
        if s + 1 < STEPS or more:
            for x, at in ((4, (0, 2)), (0, (1, 0)), (1, (1, 3)), (2, (2, 2)), (3, (3, 0))):
                extra.setdefault(at, []).append(("PROJ", s + 1, x))
        if s == 0 or (s == STEPS - 1 and more):
            for t, at in ((0, (1, 2)), (1, (2, 0)), (2, (2, 3)), (3, (3, 2))):
                extra.setdefault(at, []).append(("V", 1 if s == 0 else 0, t))
        for u in range(TT):
            before = (s, u - 1) if u else (s - 1, TT - 1)
            rest = tail(*before) if before[0] >= 0 else []
            due = (s, u - 2) if u >= 2 else (s - 1, u + 2)
            for h in range(REP):
                ops.append(("S", s, u, h))
                ops += rest[2 * h:2 * h + 2]
                if h == 1 and due[0] >= 0:
                    ops.append(("OUT", *due))
                ops += extra.get((u, h), [])
    s = STEPS - 1
    ops.append(("OUT", s, TT - 2))
    ops += tail(s, TT - 1)
    ops.append(("OUT", s, TT - 1))
    return ops


def late(ops, lags):
    due = [[] for _ in range(len(ops) + 16)]
    for at, op in enumerate(ops):
        for part, lag in lags.get(op[0], ()):
            due[at + lag].append((part, op))
    return [x for place in due for x in place]


def layer0_attention(nc, g, chunks, wv_chunks, rope):
    with ExitStack() as ctx:
        g.sem = semaphores(nc, ctx)
        sb = lambda n, s, t=F32: ctx.enter_context(nc.sbuf_tensor(f"a0_{n}", s, t))
        sem = lambda n: g.sem(f"a0_{n}")
        RAW = 4
        raw = sb("raw", [P, RAW, 512])
        wq = [sb(f"wq_{p}", [P, REP, KT, HD0], F32R) for p in ("hi", "lo")]
        wk = [sb(f"wk_{p}", [P, KT, HD0], F32R) for p in ("hi", "lo")]
        wv = [sb(f"wv_{p}", [P, KT, 2 * HD0], F32R) for p in ("hi", "lo")]
        wo = [sb(f"wo_{p}", [P, REP, D], F32R) for p in ("hi", "lo")]
        v = [sb(f"v_{p}", [P, B, TT, 2 * HD0], F32R) for p in ("hi", "lo")]
        qk = [sb(f"qk_{p}", [P, 2, REP + 1, T], F32R) for p in ("hi", "lo")]
        plain = sb("plain", [P, 2, T])
        by_cos = sb("by_cos", [P, T])
        by_sin = sb("by_sin", [P, T])
        turned = sb("turned", [P, T])
        probs = sb("probs", [P, 2, REP, T])
        pt = [sb(f"pt_{p}", [P, 2, REP * P], F32R) for p in ("hi", "lo")]
        o = [sb(f"o_{p}", [P, 2, REP * P], F32R) for p in ("hi", "lo")]
        table = sb("table", [P, 2, T])
        ring = REP * 2
        negmax = sb("negmax", [P, ring])
        rowsum = sb("rowsum", [P, ring])
        rsum = sb("rsum", [P, ring])
        score_banks, turn_banks, out_bank, mm_banks = g.bank[0:3], g.bank[3:5], g.bank[5], g.bank[6:8]

        raw_in = [sem(f"raw_in{r}") for r in range(RAW)]
        table_in = sem("table_in")
        names = ("raw_hi", "split", "scores", "maxed", "exped", "rsummed", "normed", "turned_mm", "pt_hi_done",
                 "pt_done", "pv", "o_hi_done", "o_done", "out_mm", "zeroed", "proj_mm", "rotated", "roped",
                 "qk_hi_done", "qk_done", "v_mm", "v_hi_done")
        s_ = {n: sem(n) for n in names}
        freed = [sem(f"freed{r}") for r in range(2)]

        full = attention_order(True)
        PER = {k: sum(op[0] == k for op in full) for k in KINDS}
        PER["O"] = STEPS * TT
        MM = ("PROJ", "V", "OUT")
        first_ops = [("PROJ", 0, 4), ("PROJ", 0, 0), ("V", 0, 0), ("PROJ", 0, 1), ("V", 0, 1), ("PROJ", 0, 2),
                     ("V", 0, 2), ("PROJ", 0, 3), ("V", 0, 3)]
        AHEAD = {"PROJ": REP + 1, "V": TT}
        MM_AHEAD = len(first_ops)
        MM_PER = sum(PER[k] for k in MM)

        W_AHEAD = [("K", 0), ("Q", 0), ("Vw", 0), ("Vw", 1), ("Q", 1), ("Q", 2), ("Q", 3)]

        def weight_order(more):
            ops = attention_order(more)
            at = {op: n for n, op in enumerate(ops)}
            out = [(0, ("O", h), 0) for h in range(REP)]
            for s in (0, 2):
                if s == 0 or more:
                    for x in (4, 0, 1, 2, 3):
                        what = ("K", 0) if x == 4 else ("Q", x)
                        out.append((at["PROJ", s + 1, x] + 4, what, (s // 2 + 1)))
            out += [(at["OUT", 1, TT - 1] + 1, ("O", h), 1) for h in range(REP)]
            if more:
                out += [(at["V", 1, 3] + 8 + n, ("Vw", n), 2) for n in range(2)]
            return sorted(out, key=lambda x: x[0])

        W_PER = len(weight_order(True))

        class Turn:

            def __init__(self, it, more=True, ahead=False):
                self.it, self.ahead, self.more = it, ahead, more
                self.ops = first_ops if ahead else attention_order(more)
                self.n = {}
                seen = {}
                m = -MM_AHEAD if ahead else 0
                for op in self.ops:
                    k = op[0]
                    self.n[op] = seen.get(k, 0)
                    seen[k] = self.n[op] + 1
                    if k == "PV" and op[2] == op[3]:
                        self.n["O", op[1], op[2]] = seen.get("O", 0)
                        seen["O"] = seen.get("O", 0) + 1
                    if k in MM:
                        self.n["MM", op] = m
                        m += 1
                self.weights = ([(0, w, 0) for w in W_AHEAD] if ahead else weight_order(more))
                for n, (_, w, kv) in enumerate(self.weights):
                    self.n["W", w, kv] = n - (len(W_AHEAD) if ahead else 0)

            def before(self, kind):
                if self.ahead:
                    return 0
                return self.it * PER[kind] + AHEAD.get(kind, 0)

            def done(self, *op):
                return self.before(op[0]) + (self.n[op] + 1)

            def bank(self, op):
                return self.n["MM", op] % 2

            def free(self, m):
                r = m % 2
                ahead = (MM_AHEAD + (1 if r else 0)) // 2
                n = m // 2 + 1 + ahead
                return freed[r], (n if self.ahead else self.it * (MM_PER // 2) + n)

            def evacuated(self, op):
                return self.free(self.n["MM", op])

            def chunk_in(self, c):
                r = c % RAW
                ahead = sum(x % RAW == r for x in range(-len(W_AHEAD), 0))
                n = c // RAW + 1 + ahead
                return raw_in[r], (n * 16 if self.ahead else self.it * (W_PER // RAW * 16) + n * 16)

            def split_count(self, c):
                n = c + 1 + len(W_AHEAD)
                return n if self.ahead else self.it * W_PER + n

        assert MM_PER % 2 == 0 and W_PER % RAW == 0 and PER["T"] % 2 == 0

        def project_source(tr, op):
            _, s, x = op
            kv = s // 2
            key = ("K", 0) if x == REP else ("Q", x)
            w = [t[:, :, :] if x == REP else t[:, x, :, :] for t in (wk, wq)[x < REP]]
            return w, key, kv


        def sync_turn(eng, tr):
            for n, (_, (what, which), kv) in enumerate(tr.weights):
                c = tr.n["W", (what, which), kv]
                if not (tr.ahead and c < RAW - len(W_AHEAD)):
                    eng.wait_ge(s_["split"], tr.split_count(c - RAW))
                if tr.ahead:
                    pair = 0
                else:
                    pair = tr.it
                if what == "Vw":
                    src = wv_chunks[(pair + kv // 2) * 2 + which]
                else:
                    row = {"K": 0, "Q": 1, "O": 1 + REP}[what] + which
                    src = chunks[(pair * 2 + kv) * (1 + 2 * REP) + row]
                eng.dma_start(raw[:, c % RAW, :], src).then_inc(raw_in[c % RAW], 16)

        def pool_split(eng, tr, what, which, kv):
            c = tr.n["W", (what, which), kv]
            if not tr.ahead:
                if what == "K":
                    eng.wait_ge(s_["proj_mm"], tr.done("PROJ", 2 * kv - 1, REP))
                elif what == "Q":
                    eng.wait_ge(s_["proj_mm"], tr.done("PROJ", 2 * kv - 1, which))
                elif what == "Vw":
                    eng.wait_ge(s_["v_mm"], tr.done("V", 1, TT - 1))
                elif kv == 0:
                    eng.wait_ge(s_["out_mm"], tr.before("OUT"))
                else:
                    eng.wait_ge(s_["out_mm"], tr.done("OUT", 1, TT - 1))
            dst = {"K": lambda t: t[:, :, :], "Q": lambda t: t[:, which, :, :],
                   "O": lambda t: t[:, which, :], "Vw": lambda t: t[:, 2 * which:2 * which + 2, :]}[what]
            hi, lo = (dst(t) for t in {"K": wk, "Q": wq, "O": wo, "Vw": wv}[what])
            src = raw[:, c % RAW, :]
            if what != "O":
                src = src.rearrange("p (k n) -> p k n", k=2 if what == "Vw" else KT)
            eng.wait_ge(*tr.chunk_in(c))
            passed(eng, g)
            eng.tensor_copy(hi, src).then_inc(s_["raw_hi"], 1)
            eng.wait_ge(s_["raw_hi"], tr.split_count(c))
            eng.tensor_tensor(lo, src, hi.bitcast(F32), ALU.subtract).then_inc(s_["split"], 1)

        def pool_rope(eng, tr, op):
            _, s, x = op
            slot = s % 2
            eng.wait_ge(s_["rotated"], tr.done(*op))
            if not tr.ahead or tr.n[op]:
                eng.wait_ge(s_["qk_done"], tr.done(*op) - 1)
            eng.tensor_tensor(turned[:, :], by_cos[:, :], by_sin[:, :], ALU.add).then_inc(s_["roped"], 1)
            if not tr.ahead:
                eng.wait_ge(s_["scores"], tr.before("S") + (s - 1) * TT * REP)
            eng.wait_ge(s_["roped"], tr.done(*op))
            passed(eng, g)
            eng.tensor_copy(qk[0][:, slot, x, :], turned[:, :]).then_inc(s_["qk_hi_done"], 1)
            eng.wait_ge(s_["qk_hi_done"], tr.done(*op))
            eng.tensor_tensor(qk[1][:, slot, x, :], turned[:, :], qk[0][:, slot, x, :].bitcast(F32),
                              ALU.subtract).then_inc(s_["qk_done"], 1)

        def pool_turn(eng, tr):
            work = late(tr.ops, {"PROJ": [("rope", 2)]})
            at = {op: n for n, op in enumerate(tr.ops)}
            items = [(at[op] + 2, 1, ("rope", op)) for _, op in work]
            items += [(n, 0, ("split", w)) for n, *w in tr.weights]
            for _, _, (kind, what) in sorted(items, key=lambda x: x[:2]):
                if kind == "rope":
                    pool_rope(eng, tr, what)
                else:
                    (name, which), kv = what
                    pool_split(eng, tr, name, which, kv)

        def pe_turn(eng, tr):
            for op in tr.ops:
                kind = op[0]
                if kind in MM:
                    m = tr.n["MM", op]
                    bank = mm_banks[m % 2]
                    if not (tr.ahead and m < 2 - MM_AHEAD):
                        eng.wait_ge(*tr.free(m - 2))
                if kind == "PROJ":
                    _, s, x = op
                    b = s % B
                    w, key, kv = project_source(tr, op)
                    if tr.ahead:
                        eng.wait_ge(s_["split"], tr.split_count(tr.n["W", key, 0]))
                    elif s > 1:
                        eng.wait_ge(s_["split"], tr.split_count(tr.n["W", key, kv]))
                    cols = slice(b * T, (b + 1) * T)
                    for k in range(KT):
                        mm = three_passes(eng, bank[:, :], [t[:, k, :] for t in w],
                                          [t[:, k, cols] for t in (g.hh, g.hl)], k, k == 0, k == KT - 1)
                    mm.then_inc(s_["proj_mm"], 1)
                elif kind == "V":
                    _, b, t = op
                    if tr.ahead:
                        eng.wait_ge(s_["split"], tr.split_count(tr.n["W", ("Vw", 1), 0]))
                    elif b == 0:
                        eng.wait_ge(s_["split"], tr.split_count(tr.n["W", ("Vw", 1), 2]))
                    cols = slice(b * T + t * P, b * T + (t + 1) * P)
                    for k in range(KT):
                        mm = three_passes(eng, bank[:, 0:2 * HD0], [x[:, k, cols] for x in (g.hh, g.hl)],
                                          [x[:, k, :] for x in wv], k, k == 0, k == KT - 1)
                    mm.then_inc(s_["v_mm"], 1)
                elif kind == "OUT":
                    _, s, u = op
                    eng.wait_ge(s_["o_done"], tr.before("O") + tr.n["O", s, u] + 1)
                    eng.wait_ge(s_["split"], tr.split_count(tr.n["W", ("O", REP - 1), s // 2]))
                    slot = tr.n["O", s, u] % 2
                    for h in range(REP):
                        mm = three_passes(eng, bank[:, :], [t[:, slot, h * P:(h + 1) * P] for t in o],
                                          [t[:, h, :] for t in wo], h, h == 0, h == REP - 1)
                    mm.then_inc(s_["out_mm"], 1)
                elif kind == "S":
                    _, s, u, h = op
                    n = tr.n[op]
                    eng.wait_ge(s_["exped"], tr.before("S") + max(n - 2, 0))
                    if s == 0:
                        if u == 0 and h == 0:
                            eng.wait_ge(s_["qk_done"], tr.before("PROJ"))
                    elif u == 0:
                        eng.wait_ge(s_["qk_done"], tr.done("PROJ", s, h))
                    width = max(2 * P, (u + 1) * P)
                    q = [t[:, s % 2, h, u * P:(u + 1) * P] for t in qk]
                    kk = [t[:, s % 2, REP, 0:width] for t in qk]
                    bank = score_banks[n % 3]
                    three_passes(eng, bank[:, 0:width], q, kk, 0, True, False)
                    eng.matmul(bank[:, u * P:(u + 1) * P], g.eye16[:, :], g.mask[:, :], start=False, stop=True)\
                       .then_inc(s_["scores"], 1)
                elif kind == "T":
                    _, s, u, j = op
                    n = tr.n[op]
                    if j == 0:
                        eng.wait_ge(s_["normed"], tr.done("S", s, u, REP - 1))
                    eng.wait_ge(s_["pt_done"], tr.before("T") + max(n - 1, 0))
                    unit = s * TT + u
                    for h in range(REP):
                        mm = eng.transpose(turn_banks[n % 2][:, h * P:(h + 1) * P],
                                           probs[:, unit % 2, h, j * P:(j + 1) * P], g.ident[:, :])
                    mm.then_inc(s_["turned_mm"], 1)
                elif kind == "PV":
                    _, s, u, j = op
                    slot = tr.n["T", s, u, j] % 2
                    b, kv = s % B, s // 2
                    eng.wait_ge(s_["pt_done"], tr.done("T", s, u, j))
                    if j == 0:
                        if u == 0 and s == 0:
                            eng.wait_ge(*tr.free(-2))
                            eng.wait_ge(*tr.free(-1))
                        elif u == 0 and s == 1:
                            eng.wait_ge(*tr.evacuated(("V", 1, TT - 2)))
                            eng.wait_ge(*tr.evacuated(("V", 1, TT - 1)))
                        eng.wait_ge(s_["o_done"], tr.before("O") + tr.n["O", s, u])
                    three_passes(eng, out_bank[:, :], [t[:, b, j, kv * HD0:(kv + 1) * HD0] for t in v],
                                 [t[:, slot, :] for t in pt], 0, j == 0, j == u).then_inc(s_["pv"], 1)

        def act_turn(eng, tr):
            lags = {"S": [("exp", 1)], "T": [("hi", 0)], "PV": [("hi", 0)], "PROJ": [("copy", 0)], "V": [("hi", 0)]}
            for part, op in late(tr.ops, lags):
                kind = op[0]
                if kind == "PROJ":
                    n, slot = tr.n[op], (tr.n[op] + (1 if not tr.ahead else 0)) % 2
                    eng.wait_ge(s_["proj_mm"], tr.done(*op))
                    if not (tr.ahead and n < 2):
                        eng.wait_ge(s_["rotated"], tr.done(*op) - 2)
                    eng.activation(plain[:, slot, :], mm_banks[tr.bank(op)][:, :], ACT.Copy,
                                   scale=float(HD0) ** -0.5 if op[2] < REP else 1.0)\
                       .then_inc(freed[tr.bank(op)], 1)
                elif kind == "V":
                    _, b, t = op
                    eng.wait_ge(s_["v_mm"], tr.done(*op))
                    if not tr.ahead:
                        eng.wait_ge(s_["pv"], tr.done("PV", 2, TT - 1, TT - 1) if b == 0 else tr.before("PV"))
                    eng.activation(v[0][:, b, t, :], mm_banks[tr.bank(op)][:, 0:2 * HD0], ACT.Copy)\
                       .then_inc(s_["v_hi_done"], 1)
                elif kind == "S":
                    _, s, u, h = op
                    n, unit = tr.n[op], s * TT + u
                    w = (u + 1) * P
                    eng.wait_ge(s_["maxed"], tr.done(*op))
                    if h == 0:
                        if unit >= 2:
                            s2, u2 = divmod(unit - 2, TT)
                            eng.wait_ge(s_["turned_mm"], tr.done("T", s2, u2, u2))
                        else:
                            eng.wait_ge(s_["turned_mm"], tr.before("T"))
                    eng.activation(probs[:, unit % 2, h, 0:w], score_banks[n % 3][:, 0:w], ACT.Exp,
                                   bias=negmax[:, n % ring:n % ring + 1],
                                   accum_out=rowsum[:, n % ring:n % ring + 1]).then_inc(s_["exped"], 1)
                elif kind == "T":
                    n = tr.n[op]
                    eng.wait_ge(s_["turned_mm"], tr.done(*op))
                    if n >= 2:
                        eng.wait_ge(s_["pv"], tr.before("PV") + (n - 1))
                    else:
                        eng.wait_ge(s_["pv"], tr.before("PV"))
                    eng.activation(pt[0][:, n % 2, :], turn_banks[n % 2][:, :], ACT.Copy)\
                       .then_inc(s_["pt_hi_done"], 1)
                elif kind == "PV" and op[2] == op[3]:
                    k = tr.n["O", op[1], op[2]]
                    eng.wait_ge(s_["pv"], tr.done(*op))
                    eng.wait_ge(s_["out_mm"], tr.before("OUT") + max(k - 1, 0))
                    eng.activation(o[0][:, k % 2, :], out_bank[:, :], ACT.Copy).then_inc(s_["o_hi_done"], 1)

        def dve_turn(eng, tr):
            lags = {"S": [("max", 0), ("norm", 3)], "T": [("lo", 1)], "PV": [("lo", 1)], "PROJ": [("rotate", 1)],
                    "V": [("lo", 1)], "OUT": [("add", 1)]}
            for part, op in late(tr.ops, lags):
                kind = op[0]
                if kind == "PROJ":
                    n, slot = tr.n[op], (tr.n[op] + (1 if not tr.ahead else 0)) % 2
                    eng.wait_ge(*tr.evacuated(op))
                    if not (tr.ahead and n == 0):
                        eng.wait_ge(s_["roped"], tr.done(*op) - 1)
                    half = HD0 // 2
                    eng.tensor_tensor(by_cos[:, :], plain[:, slot, :], table[:, 0, :], ALU.mult)
                    for a, z in ((0, half), (half, 0)):
                        last = eng.tensor_tensor(by_sin[z:z + half, :], plain[a:a + half, slot, :],
                                                 table[a:a + half, 1, :], ALU.mult)
                    last.then_inc(s_["rotated"], 1)
                elif kind == "V":
                    _, b, t = op
                    eng.wait_ge(s_["v_hi_done"], tr.done(*op))
                    eng.tensor_tensor(v[1][:, b, t, :], mm_banks[tr.bank(op)][:, 0:2 * HD0],
                                      v[0][:, b, t, :].bitcast(F32), ALU.subtract)\
                       .then_inc(freed[tr.bank(op)], 1)
                elif part == "max":
                    _, s, u, h = op
                    n = tr.n[op]
                    eng.wait_ge(s_["scores"], tr.done(*op))
                    eng.tensor_reduce(negmax[:, n % ring:n % ring + 1], score_banks[n % 3][:, 0:(u + 1) * P],
                                      AX_X, ALU.max, negate=True).then_inc(s_["maxed"], 1)
                elif part == "norm":
                    _, s, u, h = op
                    n, unit = tr.n[op], s * TT + u
                    eng.wait_ge(s_["exped"], tr.done(*op))
                    eng.reciprocal(rsum[:, n % ring:n % ring + 1], rowsum[:, n % ring:n % ring + 1])\
                       .then_inc(s_["rsummed"], 1)
                    eng.wait_ge(s_["rsummed"], tr.done(*op))
                    p_ = probs[:, unit % 2, h, 0:(u + 1) * P]
                    eng.tensor_scalar(p_, p_, rsum[:, n % ring:n % ring + 1], None, ALU.mult)\
                       .then_inc(s_["normed"], 1)
                elif kind == "T":
                    n = tr.n[op]
                    eng.wait_ge(s_["pt_hi_done"], tr.done(*op))
                    eng.tensor_tensor(pt[1][:, n % 2, :], turn_banks[n % 2][:, :], pt[0][:, n % 2, :].bitcast(F32),
                                      ALU.subtract).then_inc(s_["pt_done"], 1)
                elif kind == "PV" and op[2] == op[3]:
                    k = tr.n["O", op[1], op[2]]
                    eng.wait_ge(s_["o_hi_done"], tr.before("O") + (k + 1))
                    eng.tensor_tensor(o[1][:, k % 2, :], out_bank[:, :], o[0][:, k % 2, :].bitcast(F32),
                                      ALU.subtract).then_inc(s_["o_done"], 1)
                elif kind == "OUT":
                    _, s, u = op
                    y = g.y[:, (s % B) * TT + u, :]
                    eng.wait_ge(s_["out_mm"], tr.done(*op))
                    eng.wait_ge(*(tr.evacuated(("OUT", s - 2, u)) if s >= 2 else tr.free(-1)))
                    eng.tensor_tensor(y, mm_banks[tr.bank(op)][:, :], y, ALU.add)\
                       .then_inc(freed[tr.bank(op)], 1)

        def turns(eng, body):
            body(eng, Turn(-1, ahead=True))
            body(eng, Turn(0))
            with eng.Fori(1, PAIRS - 1) as it:
                body(eng, Turn(it))
            body(eng, Turn(PAIRS - 1, more=False))

        block = ctx.enter_context(nc.Block())

        @block.sync
        def _(sync):
            sync.dma_start(table[:, :, :], rope).then_inc(table_in, 16)
            turns(sync, sync_turn)

        @block.gpsimd
        def _(pool):
            turns(pool, pool_turn)

        @block.tensor
        def _(pe):
            turns(pe, pe_turn)

        @block.scalar
        def _(act):
            turns(act, act_turn)

        @block.vector
        def _(dve):
            dve.memset(g.y[:, :, :], 0.0).then_inc(s_["zeroed"], 1)
            dve.wait_ge(s_["zeroed"], 1)
            dve.wait_ge(table_in, 16)
            turns(dve, dve_turn)



class Router:

    def __init__(self, nc, ctx, g, norm, bank, w, b, bias, descend):
        sb = lambda n, s: ctx.enter_context(nc.sbuf_tensor(f"r_{n}", s, F32))
        sem = lambda n: g.sem(f"r_{n}")
        self.g, self.norm, self.bank = g, norm, bank
        self.srcs = (w, b, bias, descend)
        self.w = sb("w", [P, KT, E0])
        self.b, self.bias, self.descend = (sb(n, [P, E0]) for n in ("b", "bias", "descend"))
        self.e, self.p, self.q, self.hit, self.kept = (sb(n, [P, NT, E0]) for n in ("e", "p", "q", "hit", "kept"))
        self.one, self.two = sb("one", [P, NT]), sb("two", [P, NT])
        self.gmax, self.keep, self.ghit, self.gq = (sb(n, [P, NT, GROUPS]) for n in ("gmax", "keep", "ghit", "gq"))
        self.loaded, self.logits, self.chain, self.shifted, self.exped = (
            sem(n) for n in ("loaded", "logits", "chain", "shifted", "exped"))

    def load(self, eng):
        for dst, src in zip((self.w[:, :, :], self.b[:, :], self.bias[:, :], self.descend[:, :]), self.srcs):
            eng.dma_start(dst, src).then_inc(self.loaded, 16)

    def pe(self, pe):
        pe.wait_ge(self.loaded, 64)
        for t in range(NT):
            if t % TT == 0:
                pe.wait_ge(self.norm.affine, (t // TT + 1) * KT)
            for k in range(KT):
                mm = pe.matmul(self.bank[:, t * E0:(t + 1) * E0], self.norm.hf[:, k, t * P:(t + 1) * P],
                               self.w[:, k, :], start=(k == 0), stop=(k == KT - 1))
        mm.then_inc(self.logits, 1)

    def act(self, act):
        act.wait_ge(self.shifted, 1)
        act.activation(self.e[:, :, :], self.e[:, :, :], ACT.Exp).then_inc(self.exped, 1)

    def dve(self, dve):
        g = self.g
        link = Chain(dve, self.chain)
        over = lambda x, n: x.unsqueeze(2).to_broadcast([P, NT, n])
        each = lambda x, n: x.unsqueeze(1).to_broadcast([P, NT, n])
        dve.wait_ge(self.logits, 1)
        dve.wait_ge(self.loaded, 64)
        link(dve.tensor_tensor(self.e[:, :, :], self.bank[:, 0:NT * E0].rearrange("p (t e) -> p t e", e=E0),
                               each(self.b[:, :], E0), ALU.add))
        link(dve.tensor_reduce(self.one[:, :], self.e[:, :, :], AX_X, ALU.max))
        dve.tensor_tensor(self.e[:, :, :], self.e[:, :, :], over(self.one[:, :], E0), ALU.subtract)\
           .then_inc(self.shifted, 1)
        dve.wait_ge(self.exped, 1)
        link(dve.tensor_reduce(self.one[:, :], self.e[:, :, :], AX_X, ALU.add))
        link(dve.reciprocal(self.two[:, :], self.one[:, :]))
        link(dve.tensor_tensor(self.p[:, :, :], self.e[:, :, :], over(self.two[:, :], E0), ALU.mult))
        link(dve.tensor_tensor(self.p[:, :, :], self.p[:, :, :], each(self.bias[:, :], E0), ALU.add))

        def best_two(values, work, hit, kept, n):
            for turn in range(2):
                src = values if turn == 0 else work
                link(dve.tensor_reduce(self.one[:, :], src, AX_X, ALU.max))
                link(dve.tensor_tensor(hit, src, over(self.one[:, :], n), ALU.is_equal))
                link(dve.tensor_tensor(hit, hit, each(self.descend[:, 0:n], n), ALU.mult))
                link(dve.tensor_reduce(self.two[:, :], hit, AX_X, ALU.max))
                link(dve.tensor_tensor(hit, hit, over(self.two[:, :], n), ALU.is_equal))
                if turn == 0:
                    link(dve.tensor_copy(kept, hit))
                    link(dve.scalar_tensor_tensor(out=work, in0=hit, scalar=NEG, in1=src,
                                                  op0=ALU.mult, op1=ALU.add))
                else:
                    link(dve.tensor_tensor(kept, kept, hit, ALU.add))

        link(dve.tensor_reduce(self.gmax[:, :, :].rearrange("p t a -> p (t a)"),
                               self.p[:, :, :].rearrange("p t (a e) -> p (t a) e", a=GROUPS), AX_X, ALU.max))
        best_two(self.gmax[:, :, :], self.gq[:, :, :], self.ghit[:, :, :], self.keep[:, :, :], GROUPS)
        wide = self.keep[:, :, :].rearrange("p t a -> p (t a)").unsqueeze(2).to_broadcast(
            [P, NT * GROUPS, E0 // GROUPS])
        by_group = lambda x: x[:, :, :].rearrange("p t (a e) -> p (t a) e", a=GROUPS)
        link(dve.tensor_tensor(by_group(self.q), by_group(self.p), wide, ALU.mult))
        link(dve.tensor_scalar(self.keep[:, :, :], self.keep[:, :, :], -1.0, -NEG, ALU.add, ALU.mult))
        link(dve.tensor_tensor(by_group(self.q), by_group(self.q), wide, ALU.add))
        best_two(self.q[:, :, :], self.q[:, :, :], self.hit[:, :, :], self.kept[:, :, :], E0)
        link(dve.tensor_tensor(g.gates[:, :, 0:E0], self.p[:, :, :], self.kept[:, :, :], ALU.mult))
        link(dve.memset(g.gates[:, :, E0:EX], 1.0))


def layer0_experts(nc, g, chunks, biases, b3, meanwhile):
    with ExitStack() as ctx:
        g.sem = semaphores(nc, ctx)
        sb = lambda n, s, t=F32: ctx.enter_context(nc.sbuf_tensor(f"e0_{n}", s, t))
        sem = lambda n: g.sem(f"e0_{n}")
        TURNS, RAW, CH = EX // 2, 3, 3
        raw = sb("raw", [P, RAW, 512])
        w12 = [sb(f"w12_{p}", [P, 2, 2, KT, INTER], F32R) for p in ("hi", "lo")]
        w3 = [sb(f"w3_{p}", [P, 2, D], F32R) for p in ("hi", "lo")]
        bias = sb("bias", [P, EX, 2])
        bias_now = sb("bias_now", [P, 2, 2])
        gate_now = sb("gate_now", [P, NT, 2])
        b3_rows = sb("b3", [EX, D])
        gates_t = sb("gates_t", [EX, NT * P])
        silu = sb("silu", [P, B, T])
        prod = sb("prod", [P, B, T])
        pr = [sb(f"prod_{p}", [P, B, T], F32R) for p in ("hi", "lo")]
        raw_in = [sem(f"raw_in{r}") for r in range(RAW)]
        names = ("small_in", "raw_hi", "split", "turned", "turned_sb", "up_mm", "silu_done", "prod_done", "prod_hi",
                 "prod_lo", "down_mm", "added", "bias_set", "gate_set")
        s_ = {n: sem(n) for n in names}
        UPS, DOWNS = 2 * B, 2 * NT
        order = [("H", 0, 0), ("H", 0, 1), ("Y", 0, 0), ("H", 1, 0), ("Y", 0, 1), ("H", 1, 1), ("Y", 1, 0),
                 ("Y", 1, 1)]

        def tiles(p, b):
            return [((p * B + b) * TT + t, b * TT + t) for t in range(TT)]

        def load_expert(eng, row, n, first):
            for c in range(CH):
                if not first:
                    eng.wait_ge(s_["split"], (n - 1) * CH + (c + 1))
                eng.dma_start(raw[:, c, :], chunks[row * CH + c]).then_inc(raw_in[c], 16)

        def split_expert(eng, p, n, used):
            for c in range(CH):
                used(c)
                if c < 2:
                    hi, lo = (t[:, p, c, :, :] for t in w12)
                    src = raw[:, c, :].rearrange("p (k n) -> p k n", k=KT)
                else:
                    hi, lo = (t[:, p, :] for t in w3)
                    src = raw[:, c, :]
                eng.wait_ge(raw_in[c], (n + 1) * 16)
                passed(eng, g)
                eng.tensor_copy(hi, src).then_inc(s_["raw_hi"], 1)
                eng.wait_ge(s_["raw_hi"], n * CH + (c + 1))
                eng.tensor_tensor(lo, src, hi.bitcast(F32), ALU.subtract).then_inc(s_["split"], 1)

        def pool_products(eng, it, p):
            for b in range(B):
                n = it * UPS + (p * B + b)
                eng.wait_ge(s_["prod_done"], n + 1)
                k = it * DOWNS + ((p - 1) * B + b + 1) * TT
                if p:
                    eng.wait_ge(s_["down_mm"], k)
                else:
                    eng.wait_ge(s_["down_mm"], it * DOWNS)
                passed(eng, g)
                eng.tensor_copy(pr[0][:, b, :], prod[:, b, :]).then_inc(s_["prod_hi"], 1)
                eng.wait_ge(s_["prod_hi"], n + 1)
                eng.tensor_tensor(pr[1][:, b, :], prod[:, b, :], pr[0][:, b, :].bitcast(F32), ALU.subtract)\
                   .then_inc(s_["prod_lo"], 1)

        def pool_turn(eng, it, more):
            eng.wait_ge(s_["silu_done"], it * UPS)
            eng.wait_ge(s_["small_in"], 32)
            passed(eng, g)
            eng.tensor_copy(bias_now[:, :, :], bias[:, bass.ds(it * 2, 2), :]).then_inc(s_["bias_set"], 1)

            def used_second(c):
                eng.wait_ge(*((s_["up_mm"], it * UPS) if c < 2 else (s_["down_mm"], it * DOWNS)))

            def used_first(c):
                eng.wait_ge(*((s_["up_mm"], it * UPS + B) if c < 2 else (s_["down_mm"], it * DOWNS + NT)))

            split_expert(eng, 1, it * 2 + 1, used_second)
            pool_products(eng, it, 0)
            if more:
                pool_products_first = pool_products(eng, it, 1) if False else None
                split_expert(eng, 0, it * 2 + 2, used_first)
            pool_products(eng, it, 1)

        def pe_turn(eng, it, more):
            for kind, p, b in order:
                if kind == "H":
                    n = it * UPS + (p * B + b)
                    if b == 0:
                        eng.wait_ge(s_["split"], it * 2 * CH + (p * CH + 2))
                    if p:
                        eng.wait_ge(s_["prod_done"], n - 1)
                    else:
                        eng.wait_ge(s_["prod_done"], it * UPS)
                    cols = slice(b * T, (b + 1) * T)
                    for c in range(2):
                        for k in range(KT):
                            mm = three_passes(eng, g.bank[2 * b + c][:, :], [t[:, p, c, k, :] for t in w12],
                                              [t[:, k, cols] for t in (g.hh, g.hl)], k, k == 0, k == KT - 1)
                    mm.then_inc(s_["up_mm"], 1)
                else:
                    if b == 0:
                        eng.wait_ge(s_["split"], it * 2 * CH + (p + 1) * CH)
                    eng.wait_ge(s_["prod_lo"], it * UPS + (p * B + b + 1))
                    for (k, t) in tiles(p, b):
                        eng.wait_ge(s_["added"], it * DOWNS + (k + NT - 3))
                        three_passes(eng, g.bank[4 + t % 4][:, :], [x[:, b, (t % TT) * P:(t % TT + 1) * P] for x in pr],
                                     [x[:, p, :] for x in w3], 0, True, True).then_inc(s_["down_mm"], 1)

        def act_turn(eng, it, more):
            eng.wait_ge(s_["bias_set"], it + 1)
            for kind, p, b in order:
                if kind == "H":
                    n = it * UPS + (p * B + b)
                    eng.wait_ge(s_["up_mm"], n + 1)
                    if p:
                        eng.wait_ge(s_["prod_done"], n - 1)
                    else:
                        eng.wait_ge(s_["prod_done"], it * UPS)
                    eng.activation(silu[:, b, :], g.bank[2 * b][:, :], ACT.Silu, bias=bias_now[:, p, 0:1])\
                       .then_inc(s_["silu_done"], 1)

        def dve_turn(eng, it, more):
            eng.wait_ge(s_["added"], it * DOWNS + NT)
            eng.tensor_copy(gate_now[:, :, :], g.gates[:, :, bass.ds(it * 2, 2)]).then_inc(s_["gate_set"], 1)
            eng.wait_ge(s_["gate_set"], it + 1)
            eng.wait_ge(s_["bias_set"], it + 1)
            for kind, p, b in order:
                if kind == "H":
                    n = it * UPS + (p * B + b)
                    eng.wait_ge(s_["silu_done"], n + 1)
                    if p:
                        eng.wait_ge(s_["prod_lo"], n - 1)
                    else:
                        eng.wait_ge(s_["prod_lo"], it * UPS)
                    eng.scalar_tensor_tensor(out=prod[:, b, :], in0=g.bank[2 * b + 1][:, :],
                                             scalar=bias_now[:, p, 1:2], in1=silu[:, b, :],
                                             op0=ALU.add, op1=ALU.mult).then_inc(s_["prod_done"], 1)
                else:
                    for (k, t) in tiles(p, b):
                        eng.wait_ge(s_["down_mm"], it * DOWNS + (k + 1))
                        eng.wait_ge(s_["added"], it * DOWNS + (k + 1))
                        eng.scalar_tensor_tensor(out=g.y[:, t, :], in0=g.bank[4 + t % 4][:, :],
                                                 scalar=gate_now[:, t, p:p + 1], in1=g.y[:, t, :],
                                                 op0=ALU.mult, op1=ALU.add).then_inc(s_["added"], 1)

        def turns(eng, body):
            body(eng, 0, True)
            with eng.Fori(1, TURNS - 1) as it:
                body(eng, it, True)
            body(eng, TURNS - 1, False)

        block = ctx.enter_context(nc.Block())

        @block.sync
        def _(sync):
            sync.dma_start(bias[:, :, :], biases).then_inc(s_["small_in"], 16)
            sync.dma_start(b3_rows[:, :], b3).then_inc(s_["small_in"], 16)
            load_expert(sync, 0, 0, True)

            def body(eng, it, more):
                load_expert(eng, it * 2 + 1, it * 2 + 1, False)
                if more:
                    load_expert(eng, it * 2 + 2, it * 2 + 2, False)
            turns(sync, body)

        @block.gpsimd
        def _(pool):
            split_expert(pool, 0, 0, lambda c: None)
            turns(pool, pool_turn)

        @block.tensor
        def _(pe):
            for t in range(NT):
                mm = pe.transpose(g.bank[t // TT][0:EX, (t % TT) * P:(t % TT + 1) * P], g.gates[:, t, :],
                                  g.ident[:, :])
            mm.then_inc(s_["turned"], 1)
            pe.wait_ge(s_["turned_sb"], 2)
            pe.wait_ge(s_["small_in"], 32)
            for t in range(NT):
                if t >= TT:
                    pe.wait_ge(s_["added"], t - TT + 1)
                pe.matmul(g.bank[4 + t % 4][:, :], gates_t[:, t * P:(t + 1) * P], b3_rows[:, :],
                          start=True, stop=True).then_inc(s_["turned"], 1)
            turns(pe, pe_turn)

        @block.scalar
        def _(act):
            meanwhile(act)
            turns(act, act_turn)

        @block.vector
        def _(dve):
            dve.wait_ge(s_["turned"], 1)
            for n in range(2):
                dve.tensor_copy(gates_t[:, n * TT * P:(n + 1) * TT * P], g.bank[n][0:EX, :]).then_inc(s_["turned_sb"], 1)
            for t in range(NT):
                dve.wait_ge(s_["turned"], t + 2)
                dve.tensor_copy(g.y[:, t, :], g.bank[4 + t % 4][:, :]).then_inc(s_["added"], 1)
            turns(dve, dve_turn)



SLOT = 64
STACK = ((0, 2), (0, 1))


def split_weights(pool, g, raw, raw_in, hi_sem, split_sem, items, n=0):
    for hi, lo, view in items:
        src = view(raw[:, n % raw.shape[1], :])
        pool.wait_ge(raw_in[n % raw.shape[1]], (n // raw.shape[1] + 1) * 16)
        pool.tensor_copy(hi, src).then_inc(hi_sem, 1)
        pool.wait_ge(hi_sem, n + 1)
        pool.tensor_tensor(lo, src, hi.bitcast(F32), ALU.subtract).then_inc(split_sem, 1)
        n += 1


def load_weights(sync, raw, raw_in, split_sem, sources):
    ring = raw.shape[1]
    for n, src in enumerate(sources):
        if n >= ring:
            sync.wait_ge(split_sem, n - ring + 1)
        sync.dma_start(raw[:, n % ring, :], src).then_inc(raw_in[n % ring], 16)


def layer1_projections(nc, g, weights, rope1):
    with ExitStack() as ctx:
        g.sem = semaphores(nc, ctx)
        sb = lambda n, s, t=F32: ctx.enter_context(nc.sbuf_tensor(f"p1_{n}", s, t))
        sem = lambda n: g.sem(f"p1_{n}")
        RAW = 2
        raw = sb("raw", [P, RAW, 512])
        w = [sb(f"w_{p}", [P, 3, KT, D], F32R) for p in ("hi", "lo")]
        trig = sb("trig", [P, 2, 2, TT])
        by_cos, by_sin = (sb(n, [P, 2, D]) for n in ("by_cos", "by_sin"))
        raw_in = [sem(f"raw_in{r}") for r in range(RAW)]
        s_ = {n: sem(n) for n in ("trig_in", "raw_hi", "split", "mm", "cos_done",
                                                    "v_done", "even", "odd", "ones")}
        freed = [sem(f"freed{r}") for r in range(4)]
        pieces = [(t, c) for t in range(NT) for c in range(3)]
        rotated = [(t, c) for t, c in pieces if c < 2]
        block = ctx.enter_context(nc.Block())

        @block.sync
        def _(sync):
            sync.dma_start(trig[:, :, :, :], rope1).then_inc(s_["trig_in"], 16)
            load_weights(sync, raw, raw_in, s_["split"], [weights[c * KT + k] for c in range(3) for k in range(KT)])

        @block.gpsimd
        def _(pool):
            items = [(w[0][:, c, k, :], w[1][:, c, k, :], lambda r: r) for c in range(3) for k in range(KT)]
            split_weights(pool, g, raw, raw_in, s_["raw_hi"], s_["split"], items)
            pair = lambda x: x.rearrange("p (i two) -> p i two", two=2)
            for n, (t, c) in enumerate(rotated):
                dst = pair((g.q1 if c == 0 else g.k1)[:, t, :])
                cos, sin = pair(by_cos[:, n % 2, :]), pair(by_sin[:, n % 2, :])
                pool.wait_ge(s_["cos_done"], n + 1)
                m = pieces.index((t, c))
                pool.wait_ge(freed[m % 4], m // 4 + 1)
                pool.tensor_tensor(dst[:, :, 0], cos[:, :, 0], sin[:, :, 1], ALU.subtract).then_inc(s_["even"], 1)
                pool.tensor_tensor(dst[:, :, 1], cos[:, :, 1], sin[:, :, 0], ALU.add).then_inc(s_["odd"], 1)

        @block.tensor
        def _(pe):
            for n, (t, c) in enumerate(pieces):
                if n < 3:
                    pe.wait_ge(s_["split"], (c + 1) * KT)
                if n >= 4:
                    pe.wait_ge(freed[n % 4], n // 4)
                for k in range(KT):
                    mm = three_passes(pe, g.bank[n % 4][:, :], [x[:, k, t * P:(t + 1) * P] for x in (g.hh, g.hl)],
                                      [x[:, c, k, :] for x in w], k, k == 0, k == KT - 1)
                mm.then_inc(s_["mm"], 1)

        @block.scalar
        def _(act):
            act.wait_ge(s_["trig_in"], 16)
            for n, (t, c) in enumerate(pieces):
                if c == 2:
                    continue
                r = rotated.index((t, c))
                act.wait_ge(s_["mm"], n + 1)
                if r >= 2:
                    act.wait_ge(s_["odd"], r - 1)
                act.activation(by_cos[:, r % 2, :], g.bank[n % 4][:, :], ACT.Copy,
                               scale=trig[:, c, 0, t % TT:t % TT + 1]).then_inc(s_["cos_done"], 1)

        @block.vector
        def _(dve):
            dve.memset(g.v1[:, :, :, HD1:VW], 1.0).then_inc(s_["ones"], 1)
            dve.wait_ge(s_["trig_in"], 16)
            for n, (t, c) in enumerate(pieces):
                bank = g.bank[n % 4]
                dve.wait_ge(s_["mm"], n + 1)
                if c == 2:
                    dve.tensor_copy(g.v1[:, t, :, 0:HD1], bank[:, :].rearrange("p (h d) -> p h d", h=H1))\
                       .then_inc(freed[n % 4], 1)
                    continue
                r = rotated.index((t, c))
                dve.wait_ge(s_["cos_done"], r + 1)
                if r >= 2:
                    dve.wait_ge(s_["odd"], r - 1)
                dve.tensor_scalar(by_sin[:, r % 2, :], bank[:, :], trig[:, c, 1, t % TT:t % TT + 1], None, ALU.mult)\
                   .then_inc(freed[n % 4], 1)


def layer1_attention(nc, g, b):
    with ExitStack() as ctx:
        g.sem = semaphores(nc, ctx)
        sb = lambda n, s, t=F32: ctx.enter_context(nc.sbuf_tensor(f"a1{b}_{n}", s, t))
        sem = lambda n: g.sem(f"a1{b}_{n}")
        PR = H1 // 2
        stack = sb("stack", [P, 2, H1, 4, HD1], F32R)
        turned = [sb(n, [P, PR, T], F32R) for n in ("q", "k")]
        probs = sb("probs", [P, 2, TT, T])
        BLOCKS = TT * (TT + 1) // 2
        pt = sb("pt", [P, 2, BLOCKS, P])
        negmax = sb("negmax", [P, 2, TT])
        rsum = sb("rsum", [P, 2, TT, 4])
        names = ("hi", "lo", "turn", "taken_a", "taken_v", "scores", "maxed", "exped", "pt_mm", "pt_a", "pt_v",
                 "pv", "rsummed", "normed")
        s_ = {n: sem(n) for n in names}
        score_banks, turn_banks, out_banks = g.bank[0:3], g.bank[3:6], g.bank[6:8]
        stacks = [(t, c) for t in range(TT) for c in range(2)]
        GROUPS_T = [[(0, 0), (1, 0), (1, 1)], [(2, 0), (2, 1), (2, 2)], [(3, 0), (3, 1), (3, 2), (3, 3)]]
        FIRST = [0, 3, 6]
        where = {ub: FIRST[n] + m for n, grp in enumerate(GROUPS_T) for m, ub in enumerate(grp)}
        HG = 4

        block = ctx.enter_context(nc.Block())

        def copies(c, n, lo):
            s = stack[:, n % 2, :, :, :]
            if c == 0:
                return s[:, :, lo:4:2, :]
            return s[:, :, 2 * lo:2 * lo + 2, :]

        def source(t, c):
            return (g.q1 if c == 0 else g.k1)[:, b * TT + t, :].rearrange("p (h d) -> p h d", h=H1)\
                .unsqueeze(2).to_broadcast([P, H1, 2, HD1])

        @block.gpsimd
        def _(pool):
            for n, (t, c) in enumerate(stacks):
                if n >= 2:
                    pool.wait_ge(s_["turn"], 4 * (n - 1))
                pool.tensor_copy(copies(c, n, 0), source(t, c)).then_inc(s_["hi"], 1)

        @block.tensor
        def _(pe):
            for n, (t, c) in enumerate(stacks):
                pe.wait_ge(s_["lo"], n + 1)
                flat = stack[:, n % 2, :, :, :].rearrange("p h a d -> p (h a d)").bitcast(F32)
                for q in range(4):
                    m = 4 * n + q
                    if m >= 8:
                        pe.wait_ge((s_["taken_a"], s_["taken_v"])[m % 2], (m - 8) // 2 + 1)
                    for r in range(4):
                        mm = pe.transpose(g.bank[m % 8][:, r * P:(r + 1) * P],
                                          flat[:, (q * 4 + r) * P:(q * 4 + r + 1) * P], g.ident[:, :])
                    mm.then_inc(s_["turn"], 1)
            pe.wait_ge(s_["taken_a"], 16)
            pe.wait_ge(s_["taken_v"], 16)

            def score(h, u):
                n = h * TT + u
                if n >= 3:
                    pe.wait_ge(s_["exped"], n - 2)
                rows = slice(SLOT * (h % 2), SLOT * (h % 2 + 1))
                w = max(2, u + 1) * P
                bank = score_banks[n % 3]
                pe.matmul(bank[:, 0:w], turned[0][rows, h // 2, u * P:(u + 1) * P], turned[1][rows, h // 2, 0:w],
                          start=True, stop=False)
                pe.matmul(bank[:, u * P:(u + 1) * P], g.eye16[:, :], g.mask[:, :], start=False, stop=True)\
                    .then_inc(s_["scores"], 1)

            def turn(h, n):
                pe.wait_ge(s_["exped"], h * TT + (2, 3, 4)[n])
                if h:
                    pe.wait_ge(*((s_["pt_a"], h) if n == 0 else (s_["pt_v"], 2 * (h - 1) + n)))
                for m, (u, j) in enumerate(GROUPS_T[n]):
                    mm = pe.transpose(turn_banks[n][:, m * P:(m + 1) * P], probs[:, h % 2, u, j * P:(j + 1) * P],
                                      g.ident[:, :])
                mm.then_inc(s_["pt_mm"], 1)

            def values(h, us):
                grp = h // HG
                if us[0] == 0:
                    pe.wait_ge(s_["pt_a"], h + 1)
                    if h % HG == 0 and grp >= 2:
                        pe.wait_ge(s_["normed"], grp - 1)
                for u in us:
                    if u >= 2:
                        pe.wait_ge(s_["pt_v"], 2 * h + u - 1)
                    out = out_banks[grp % 2][:, (u * HG + h % HG) * VW:(u * HG + h % HG + 1) * VW]
                    for j in range(u + 1):
                        mm = pe.matmul(out, pt[:, h % 2, where[u, j], :], g.v1[:, b * TT + j, h, :],
                                       start=(j == 0), stop=(j == u))
                mm.then_inc(s_["pv"], 1)

            for h in range(H1 + 1):
                if h < H1:
                    score(h, 0)
                if h:
                    turn(h - 1, 0)
                if h < H1:
                    score(h, 1)
                if h:
                    turn(h - 1, 1)
                if h < H1:
                    score(h, 2)
                if h:
                    turn(h - 1, 2)
                    values(h - 1, (0, 1))
                if h < H1:
                    score(h, 3)
                if h:
                    values(h - 1, (2, 3))

        @block.scalar
        def _(act):
            for n, (t, c) in enumerate(stacks):
                for q in range(0, 4, 2):
                    m = 4 * n + q
                    act.wait_ge(s_["turn"], m + 1)
                    act.activation(turned[c][:, q * 4:q * 4 + 4, t * P:(t + 1) * P],
                                   g.bank[m % 8][:, :].rearrange("p (a x) -> p a x", a=4), ACT.Copy)\
                       .then_inc(s_["taken_a"], 1)

            def exps(h):
                for u in range(TT):
                    n = h * TT + u
                    act.wait_ge(s_["maxed"], n + 1)
                    if h >= 2 and u == 0:
                        act.wait_ge(s_["pt_mm"], 3 * (h - 1))
                    act.activation(probs[:, h % 2, u, 0:(u + 1) * P], score_banks[n % 3][:, 0:(u + 1) * P],
                                   ACT.Exp, bias=negmax[:, h % 2, u:u + 1]).then_inc(s_["exped"], 1)
                    if u == 0 and h:
                        act.wait_ge(s_["pt_mm"], 3 * (h - 1) + 1)
                        if h >= 3:
                            act.wait_ge(s_["pv"], 2 * (h - 2))
                        act.activation(pt[:, (h - 1) % 2, 0:3, :],
                                       turn_banks[0][:, 0:3 * P].rearrange("p (a x) -> p a x", a=3), ACT.Copy)\
                           .then_inc(s_["pt_a"], 1)
            for h in range(H1):
                exps(h)
            act.wait_ge(s_["pt_mm"], 3 * (H1 - 1) + 1)
            act.wait_ge(s_["pv"], 2 * (H1 - 2))
            act.activation(pt[:, (H1 - 1) % 2, 0:3, :], turn_banks[0][:, 0:3 * P].rearrange("p (a x) -> p a x", a=3),
                           ACT.Copy).then_inc(s_["pt_a"], 1)

        @block.vector
        def _(dve):
            for n, (t, c) in enumerate(stacks):
                dve.wait_ge(s_["hi"], n + 1)
                hi = stack[:, n % 2, :, 0:1, :].bitcast(F32).to_broadcast([P, H1, 2, HD1])
                dve.tensor_tensor(copies(c, n, 1), source(t, c), hi, ALU.subtract).then_inc(s_["lo"], 1)
                for q in range(1, 4, 2):
                    m = 4 * n + q
                    dve.wait_ge(s_["turn"], m + 1)
                    dve.tensor_copy(turned[c][:, q * 4:q * 4 + 4, t * P:(t + 1) * P],
                                    g.bank[m % 8][:, :].rearrange("p (a x) -> p a x", a=4)).then_inc(s_["taken_v"], 1)

            def take(h, n):
                dve.wait_ge(s_["pt_mm"], 3 * h + n + 1)
                if n == 1 and h >= 2:
                    dve.wait_ge(s_["pv"], 2 * (h - 1))
                k = len(GROUPS_T[n])
                dve.tensor_copy(pt[:, h % 2, FIRST[n]:FIRST[n] + k, :],
                                turn_banks[n][:, 0:k * P].rearrange("p (a x) -> p a x", a=k)).then_inc(s_["pt_v"], 1)

            def finish(grp):
                out = out_banks[grp % 2][:, 0:TT * HG * VW].rearrange("p (u h d) -> p u h d", u=TT, h=HG)
                dve.wait_ge(s_["pv"], 2 * HG * (grp + 1))
                dve.reciprocal(rsum[:, grp % 2, :, :], out[:, :, :, HD1]).then_inc(s_["rsummed"], 1)
                dve.wait_ge(s_["rsummed"], grp + 1)
                dst = g.q1[:, b * TT:(b + 1) * TT, grp * HG * HD1:(grp + 1) * HG * HD1]\
                    .rearrange("p u (h d) -> p u h d", h=HG)
                dve.tensor_tensor(dst, out[:, :, :, 0:HD1],
                                  rsum[:, grp % 2, :, :].unsqueeze(3).to_broadcast([P, TT, HG, HD1]), ALU.mult)\
                   .then_inc(s_["normed"], 1)

            for h in range(H1 + 1):
                for u in range(TT):
                    if h < H1:
                        n = h * TT + u
                        dve.wait_ge(s_["scores"], n + 1)
                        dve.tensor_reduce(negmax[:, h % 2, u:u + 1], score_banks[n % 3][:, 0:(u + 1) * P], AX_X,
                                          ALU.max, negate=True).then_inc(s_["maxed"], 1)
                    if h and u in (2, 3):
                        take(h - 1, u - 1)
                if h >= 2 and (h - 1) % HG == 0:
                    finish((h - 1) // HG - 1)
            finish(H1 // HG - 1)


def layer1_output(nc, g, weights):
    with ExitStack() as ctx:
        g.sem = semaphores(nc, ctx)
        sb = lambda n, s, t=F32: ctx.enter_context(nc.sbuf_tensor(f"o1_{n}", s, t))
        sem = lambda n: g.sem(f"o1_{n}")
        RAW = 4
        raw = sb("raw", [P, RAW, 512])
        w = [sb(f"w_{p}", [P, KT, D], F32R) for p in ("hi", "lo")]
        o = [sb(f"o_{p}", [P, KT, B * T], F32R) for p in ("hi", "lo")]
        raw_in = [sem(f"raw_in{r}") for r in range(RAW)]
        s_ = {n: sem(n) for n in ("raw_hi", "split", "turn", "hi", "lo", "mm", "out")}
        block = ctx.enter_context(nc.Block())

        @block.sync
        def _(sync):
            load_weights(sync, raw, raw_in, s_["split"], [weights[3 * KT + k] for k in range(KT)])

        @block.gpsimd
        def _(pool):
            split_weights(pool, g, raw, raw_in, s_["raw_hi"], s_["split"],
                          [(w[0][:, k, :], w[1][:, k, :], lambda r: r) for k in range(KT)])

        @block.tensor
        def _(pe):
            def turn(t):
                if t >= 2:
                    pe.wait_ge(s_["lo"], t - 1)
                for k in range(KT):
                    mm = pe.transpose(g.bank[t % 2][:, k * P:(k + 1) * P], g.q1[:, t, k * P:(k + 1) * P], g.ident[:, :])
                mm.then_inc(s_["turn"], 1)

            turn(0)
            turn(1)
            for t in range(NT):
                if t + 2 < NT:
                    turn(t + 2)
                pe.wait_ge(s_["lo"], t + 1)
                if t == 0:
                    pe.wait_ge(s_["split"], KT)
                if t >= 4:
                    pe.wait_ge(s_["out"], t - 3)
                for k in range(KT):
                    mm = three_passes(pe, g.bank[2 + t % 4][:, :], [x[:, k, t * P:(t + 1) * P] for x in o],
                                      [x[:, k, :] for x in w], k, k == 0, k == KT - 1)
                mm.then_inc(s_["mm"], 1)

        @block.scalar
        def _(act):
            for t in range(NT):
                act.wait_ge(s_["turn"], t + 1)
                act.activation(o[0][:, :, t * P:(t + 1) * P], g.bank[t % 2][:, :].rearrange("p (k x) -> p k x", k=KT),
                               ACT.Copy).then_inc(s_["hi"], 1)

        @block.vector
        def _(dve):
            def out(t):
                dve.wait_ge(s_["mm"], t + 1)
                dve.tensor_copy(g.y[:, t, :], g.bank[2 + t % 4][:, :]).then_inc(s_["out"], 1)

            for t in range(NT):
                dve.wait_ge(s_["hi"], t + 1)
                dve.tensor_tensor(o[1][:, :, t * P:(t + 1) * P], g.bank[t % 2][:, :].rearrange("p (k x) -> p k x", k=KT),
                                  o[0][:, :, t * P:(t + 1) * P].bitcast(F32), ALU.subtract).then_inc(s_["lo"], 1)
                if t >= 2:
                    out(t - 2)
            out(NT - 2)
            out(NT - 1)



def layer1_experts(nc, g, norm, weights, a_w, b_w, bias_row, out_dram):
    with ExitStack() as ctx:
        g.sem = semaphores(nc, ctx)
        sb = lambda n, s, t=F32: ctx.enter_context(nc.sbuf_tensor(f"l1_{n}", s, t))
        sem = lambda n: g.sem(f"l1_{n}")
        RAW, ER = 2, E1 * R1
        raw = sb("raw", [P, RAW, 512])
        w = [sb(f"w_{p}", [P, 2, KT, D], F32R) for p in ("hi", "lo")]
        bw = [sb(f"b_{p}", [P, D], F32R) for p in ("hi", "lo")]
        aw = sb("aw", [P, KT, ER])
        bias = sb("bias", [P, D])
        k_sb = sb("k_sb", [P, 2, E1 * DK1])
        qk = sb("qk", [P, 2, E1 * DK1])
        sc, ex, wt = (sb(n, [P, 2, E1]) for n in ("sc", "ex", "wt"))
        mx, sm, rs = (sb(n, [P, 2]) for n in ("mx", "sm", "rs"))
        wh = sb("wh", [P, 2, ER])
        wht = [sb(f"wht_{p}", [P, 2, P], F32R) for p in ("hi", "lo")]
        biased = sb("biased", [P, 2, D])
        gated = sb("gated", [P, 2, D])
        final = sb("final", [P, 2, D])
        raw_in = [sem(f"raw_in{r}") for r in range(RAW)]
        names = ("small_in", "raw_hi", "split", "res_mm", "qk_mm", "a_mm", "k_copied", "chain", "scored", "exped",
                 "rs", "wt", "weighted", "turned", "t_hi", "t_lo", "b_mm", "biased", "gated", "final")
        s_ = {n: sem(n) for n in names}
        stored = [sem(f"stored{r}") for r in range(2)]
        block = ctx.enter_context(nc.Block())

        @block.sync
        def _(sync):
            for dst, src in ((aw[:, :, :], a_w), (bias[:, :], bias_row)):
                sync.dma_start(dst, src).then_inc(s_["small_in"], 16)
            load_weights(sync, raw, raw_in, s_["split"], [weights[(4 + c) * KT + k] for c in (1, 0) for k in range(KT)] + [b_w])
            for t in range(NT):
                sync.wait_ge(s_["final"], t + 1)
                sync.dma_start(out_dram[t * P:(t + 1) * P, :], final[:, t % 2, :]).then_inc(stored[t % 2], 16)
            for slot in stored:
                sync.wait_ge(slot, 16 * (NT // 2))

        @block.gpsimd
        def _(pool):
            items = [(w[0][:, c, k, :], w[1][:, c, k, :], lambda r: r) for c in (1, 0) for k in range(KT)]
            items.append((bw[0][:, :], bw[1][:, :], lambda r: r))
            split_weights(pool, g, raw, raw_in, s_["raw_hi"], s_["split"], items)
            for t in range(NT):
                pool.wait_ge(s_["biased"], t + 1)
                if t >= 2:
                    pool.wait_ge(s_["final"], t - 1)
                pool.tensor_tensor(gated[:, t % 2, :], biased[:, t % 2, :], g.gate_rows[:, 1, t // TT, :], ALU.mult)\
                    .then_inc(s_["gated"], 1)
                pool.wait_ge(s_["gated"], t + 1)
                if t >= 2:
                    pool.wait_ge(stored[t % 2], 16 * (t // 2))
                pool.tensor_tensor(final[:, t % 2, :], gated[:, t % 2, :], g.x[:, t, :], ALU.add).then_inc(s_["final"], 1)

        @block.tensor
        def _(pe):
            def front(t):
                cols = slice(t * P, (t + 1) * P)
                if t == 0:
                    pe.wait_ge(s_["split"], KT)
                if t >= 2:
                    pe.wait_ge(s_["scored"], t - 1)
                for k in range(KT):
                    mm = three_passes(pe, g.bank[3 + t % 2][:, :], [x[:, k, cols] for x in (g.hh, g.hl)],
                                      [x[:, 1, k, :] for x in w], k, k == 0, k == KT - 1)
                mm.then_inc(s_["qk_mm"], 1)
                pe.wait_ge(s_["small_in"], 32)
                if t >= 2:
                    pe.wait_ge(s_["weighted"], t - 1)
                for k in range(KT):
                    mm = pe.matmul(g.bank[5 + t % 2][:, 0:ER], norm.hf[:, k, cols], aw[:, k, :],
                                   start=(k == 0), stop=(k == KT - 1))
                mm.then_inc(s_["a_mm"], 1)
                if t == 0:
                    pe.wait_ge(s_["split"], 2 * KT)
                if t >= 3:
                    pe.wait_ge(s_["biased"], t - 2)
                for k in range(KT):
                    mm = three_passes(pe, g.bank[t % 3][:, :], [x[:, k, cols] for x in (g.hh, g.hl)],
                                      [x[:, 0, k, :] for x in w], k, k == 0, False)

            front(0)
            for t in range(NT):
                if t + 1 < NT:
                    front(t + 1)
                pe.wait_ge(s_["weighted"], t + 1)
                if t >= 1:
                    pe.wait_ge(s_["t_lo"], t)
                pe.transpose(g.bank[7][:, 0:P], wh[:, t % 2, :], g.ident[:, :]).then_inc(s_["turned"], 1)
                pe.wait_ge(s_["t_lo"], t + 1)
                if t == 0:
                    pe.wait_ge(s_["split"], 2 * KT + 1)
                three_passes(pe, g.bank[t % 3][:, :], [x[:, t % 2, :] for x in wht], [x[:, :] for x in bw],
                             0, False, True).then_inc(s_["b_mm"], 1)

        @block.scalar
        def _(act):
            for t in range(NT):
                act.wait_ge(s_["qk_mm"], t + 1)
                if t >= 2:
                    act.wait_ge(s_["scored"], t - 1)
                act.activation(k_sb[:, t % 2, :], g.bank[3 + t % 2][:, E1 * DK1:2 * E1 * DK1], ACT.Copy)\
                    .then_inc(s_["k_copied"], 1)
                act.wait_ge(s_["chain"], 3 * t + 3)
                act.activation(ex[:, t % 2, :], sc[:, t % 2, :], ACT.Exp, bias=mx[:, t % 2:t % 2 + 1],
                               scale=float(DK1) ** -0.5, accum_out=sm[:, t % 2:t % 2 + 1]).then_inc(s_["exped"], 1)
                act.wait_ge(s_["turned"], t + 1)
                if t >= 2:
                    act.wait_ge(s_["b_mm"], t - 1)
                act.activation(wht[0][:, t % 2, :], g.bank[7][:, 0:P], ACT.Copy).then_inc(s_["t_hi"], 1)

        @block.vector
        def _(dve):
            dve.wait_ge(s_["small_in"], 32)

            def last(t):
                dve.wait_ge(s_["t_hi"], t + 1)
                dve.tensor_tensor(wht[1][:, t % 2, :], g.bank[7][:, 0:P], wht[0][:, t % 2, :].bitcast(F32),
                                  ALU.subtract).then_inc(s_["t_lo"], 1)
                dve.wait_ge(s_["b_mm"], t + 1)
                if t >= 2:
                    dve.wait_ge(s_["gated"], t - 1)
                dve.tensor_tensor(biased[:, t % 2, :], g.bank[t % 3][:, :], bias[:, :], ALU.add).then_inc(s_["biased"], 1)

            for t in range(NT):
                p = t % 2
                dve.wait_ge(s_["k_copied"], t + 1)
                dve.tensor_tensor(qk[:, p, :], g.bank[3 + p][:, 0:E1 * DK1], k_sb[:, p, :], ALU.mult).then_inc(s_["scored"], 1)
                dve.wait_ge(s_["scored"], t + 1)
                dve.tensor_reduce(sc[:, p, :], qk[:, p, :].rearrange("p (e d) -> p e d", e=E1), AX_X, ALU.add)\
                   .then_inc(s_["chain"], 1)
                dve.wait_ge(s_["chain"], 3 * t + 1)
                dve.tensor_reduce(mx[:, p:p + 1], sc[:, p, :], AX_X, ALU.max, negate=True).then_inc(s_["chain"], 1)
                dve.wait_ge(s_["chain"], 3 * t + 2)
                dve.tensor_scalar(mx[:, p:p + 1], mx[:, p:p + 1], float(DK1) ** -0.5, None, ALU.mult).then_inc(s_["chain"], 1)
                dve.wait_ge(s_["exped"], t + 1)
                dve.reciprocal(rs[:, p:p + 1], sm[:, p:p + 1]).then_inc(s_["rs"], 1)
                dve.wait_ge(s_["rs"], t + 1)
                dve.tensor_scalar(wt[:, p, :], ex[:, p, :], rs[:, p:p + 1], None, ALU.mult).then_inc(s_["wt"], 1)
                dve.wait_ge(s_["wt"], t + 1)
                dve.wait_ge(s_["a_mm"], t + 1)
                if t >= 2:
                    dve.wait_ge(s_["turned"], t - 1)
                dve.tensor_tensor(wh[:, p, :].rearrange("p (e r) -> p e r", e=E1),
                                  g.bank[5 + p][:, 0:ER].rearrange("p (e r) -> p e r", e=E1),
                                  wt[:, p, :].unsqueeze(2).to_broadcast([P, E1, R1]), ALU.mult).then_inc(s_["weighted"], 1)
                last(t)



def build(nc, a, out, upto=99):
    with ExitStack() as ctx:
        sb = lambda n, s, t=F32: ctx.enter_context(nc.sbuf_tensor(n, s, t))
        g = Shared()
        g.bank = [ctx.enter_context(nc.psum_tensor(f"bank{i}", [P, 512], F32)) for i in range(8)]
        g.y = sb("y", [P, NT, D])

        def operands(scope, name):
            g.hh, g.hl = (scope.enter_context(nc.sbuf_tensor(f"h_{p}_{name}", [P, KT, B * T], F32R))
                          for p in ("hi", "lo"))

        g.mod = sb("mod", [P, 6, KT * B])
        g.ident = sb("ident", [P, P])
        g.eye16 = sb("eye16", [P, P], BF16)
        g.mask = sb("mask", [P, P], BF16)
        g.passed = ctx.enter_context(nc.semaphore("passed"))
        g.ready = ctx.enter_context(nc.semaphore("ready"))
        dbg = lambda: None

        part = ctx.enter_context(ExitStack())
        operands(part, "attention0")
        with ExitStack() as ph:
            sem = g.sem = semaphores(nc, ph)
            g.x = ph.enter_context(nc.sbuf_tensor("x_first", [P, NT, D], F32))
            g.gate_rows = ph.enter_context(nc.sbuf_tensor("gate_rows_first", [P, 2, B, D], F32))
            g.pick = ph.enter_context(nc.sbuf_tensor("pick", [2 * KT * B, 2 * KT * B, P], F32))
            mod = Modulation(nc, ph, g, "m0", a["c0"], a["L0_wmod"], g.bank[5:8])
            norm = Norm(nc, ph, g, "n0", 1, 0, x_dram=a["x"], mod_ready=(mod.chain, 2))
            zeroed, eyed = sem("zeroed"), sem("eyed")
            stored, stored_rows = sem("stored"), sem("rows_stored")
            block = ph.enter_context(nc.Block())

            @block.sync
            def _(sync):
                mod.load(sync, (0, 1))
                norm.load(sync)
                for m in range(2, 6):
                    sync.dma_start(mod.wmod[:, :, m, :],
                                   a["L0_wmod"].rearrange("(k p) n -> p k n", p=P)[:, :, m * D:(m + 1) * D])\
                        .then_inc(mod.w_in[m], 16)
                sync.wait_ge(mod.rows_sb, 2 * B)
                sync.dma_start(a["gate_rows"][0], g.gate_rows[:, :, :, :]).then_inc(stored_rows, 16)
                sync.wait_ge(stored_rows, 16)

            @block.gpsimd
            def _(pool):
                pool.memset(g.ident[:, :], 0.0).then_inc(zeroed, 1)
                pool.memset(g.eye16[:, :], 0.0).then_inc(zeroed, 1)
                pool.memset(g.mask[:, :], 0.0).then_inc(zeroed, 1)
                pool.wait_ge(zeroed, 3)
                for eye in (g.ident, g.eye16):
                    pool.affine_select(out=eye[:, :], in_=eye[:, :], compare_op=ALU.not_equal, fill=1.0,
                                       base=0, pattern=[[-1, P]], channel_multiplier=1).then_inc(eyed, 1)
                pool.affine_select(out=g.mask[:, :], in_=g.mask[:, :], compare_op=ALU.is_ge, fill=NEG,
                                   base=0, pattern=[[-1, P]], channel_multiplier=1).then_inc(g.ready, 1)
                norm.pool(pool)

            @block.scalar
            def _(act):
                act.dma_start(g.pick[:, :, :], a["pick"]).then_inc(stored, 16)
                mod.act(act)
                norm.act(act)

            @block.tensor
            def _(pe):
                pe.wait_ge(eyed, 2)
                pe.wait_ge(stored, 16)
                mod.pe(pe)
                norm.pe(pe)
                mod.pe_rows(pe)

            @block.vector
            def _(dve):
                norm.dve_stats(dve)
                mod.dve_columns(dve, g.mod)
                norm.dve_split(dve)
                mod.dve_rows(dve, g.gate_rows)
        if upto == 0:
            return dump(nc, g, out, g.hh, [[g.hh[:, k, t * P:(t + 1) * P] for k in range(KT)] for t in range(NT)])
        layer0_attention(nc, g, a["chunks"], a["wv_chunks"], a["rope"])
        if upto == 1:
            return dump(nc, g, out, g.y, [[g.y[:, t, k * P:(k + 1) * P] for k in range(KT)] for t in range(NT)])
        part.close()

        g.x = sb("x", [P, NT, D])
        g.gate_rows = sb("gate_rows", [P, 2, B, D])
        part = ctx.enter_context(ExitStack())
        g.gates = part.enter_context(nc.sbuf_tensor("gates", [P, NT, EX], F32))
        operands(part, "experts")
        with ExitStack() as ph:
            sem = g.sem = semaphores(nc, ph)
            norm = Norm(nc, ph, g, "n1", 4, 3, gate=0, x_dram=a["x"])
            router = Router(nc, ph, g, norm, g.bank[4], a["router_w"], a["router_b"], a["router_bias"], a["descend"])
            rows_in = sem("rows_in")
            block = ph.enter_context(nc.Block())

            @block.sync
            def _(sync):
                sync.dma_start(g.gate_rows[:, :, :, :], a["gate_rows"][0]).then_inc(rows_in, 16)
                norm.load(sync)

            @block.gpsimd
            def _(pool):
                norm.pool(pool)

            @block.scalar
            def _(act):
                router.load(act)
                norm.act(act)
                router.act(act)

            @block.tensor
            def _(pe):
                norm.pe(pe)
                router.pe(pe)

            @block.vector
            def _(dve):
                dve.wait_ge(rows_in, 16)
                norm.dve_stats(dve)
                norm.dve_split(dve)
                router.dve(dve)
        if upto == 2:
            return dump(nc, g, out, g.gates, [[g.gates[:, t, 0:16] for k in range(1)] for t in range(NT)])

        layer0_experts(nc, g, a["expert_chunks"], a["expert_biases"], a["expert_b3"], lambda act: None)
        if upto == 3:
            return dump(nc, g, out, g.y, [[g.y[:, t, k * P:(k + 1) * P] for k in range(KT)] for t in range(NT)])
        part.close()

        gate_rows1 = sb("gate_rows1", [P, 2, B, D])
        qkv = ctx.enter_context(ExitStack())
        g.q1 = qkv.enter_context(nc.sbuf_tensor("q1", [P, NT, D], F32))
        g.v1 = qkv.enter_context(nc.sbuf_tensor("v1", [P, NT, H1, VW], F32))
        g.k1 = g.y
        part = ctx.enter_context(ExitStack())
        operands(part, "attention1")
        with ExitStack() as ph:
            g.sem = semaphores(nc, ph)
            pick = ph.enter_context(nc.sbuf_tensor("pick1", [2 * KT * B, 2 * KT * B, P], F32))
            picked = g.sem("picked")
            g.pick = pick
            mod = Modulation(nc, ph, g, "m1", a["c1"], a["L1_wmod"], g.bank[5:8])
            norm = Norm(nc, ph, g, "n2", 1, 0, gate=1, mod_ready=(mod.chain, 2))
            block = ph.enter_context(nc.Block())

            @block.sync
            def _(sync):
                mod.load(sync)

            @block.gpsimd
            def _(pool):
                norm.pool(pool)

            @block.scalar
            def _(act):
                act.dma_start(pick[:, :, :], a["pick"]).then_inc(picked, 16)
                mod.act(act)
                norm.act(act)

            @block.tensor
            def _(pe):
                pe.wait_ge(picked, 16)
                mod.pe(pe)
                norm.pe(pe)
                mod.pe_rows(pe)

            @block.vector
            def _(dve):
                norm.dve_stats(dve)
                mod.dve_columns(dve, g.mod)
                norm.dve_split(dve)
                mod.dve_rows(dve, gate_rows1)
        g.gate_rows = gate_rows1
        if upto == 4:
            return dump(nc, g, out, g.hh, [[g.hh[:, k, t * P:(t + 1) * P] for k in range(KT)] for t in range(NT)])
        layer1_projections(nc, g, a["l1_chunks"], a["rope1"])
        part.close()
        for b in range(B):
            layer1_attention(nc, g, b)
        layer1_output(nc, g, a["l1_chunks"])
        if upto == 5:
            return dump(nc, g, out, g.y, [[g.y[:, t, k * P:(k + 1) * P] for k in range(KT)] for t in range(NT)])
        qkv.close()

        operands(ctx, "experts1")
        g.sem = semaphores(nc, ctx)
        norm = Norm(nc, ctx, g, "n3", 4, 3, gate=0)
        with nc.Block() as block:
            @block.gpsimd
            def _(pool):
                norm.pool(pool)

            @block.scalar
            def _(act):
                norm.act(act)

            @block.tensor
            def _(pe):
                norm.pe(pe)

            @block.vector
            def _(dve):
                norm.dve_stats(dve)
                norm.dve_split(dve)
        if upto == 6:
            return dump(nc, g, out, g.hh, [[g.hh[:, k, t * P:(t + 1) * P] for k in range(KT)] for t in range(NT)])
        layer1_experts(nc, g, norm, a["l1_chunks"], a["lora_a"], a["lora_b"], a["l1_bias"], out)


def dump(nc, g, out, src, tiles):
    with nc.semaphore("dumped") as s, nc.Block() as block:
        @block.sync
        def _(sync):
            n = 0
            for t in range(NT):
                for k, v in enumerate(tiles[t]):
                    sync.dma_start(out[t * P:(t + 1) * P, k * P:k * P + v.shape[1]],
                                   v.bitcast(F32) if src.dtype == F32R else v).then_inc(s, 16)
                    n += 16
            sync.wait_ge(s, n)


def lay_out(i):
    n = lambda k: np.asarray(i[k])
    a = {}
    a["x"] = np.ascontiguousarray(n("L0_attn_x").reshape(B * T, D))
    a["L0_wmod"], a["L1_wmod"] = n("L0_wmod"), n("L1_wmod")
    for l in (0, 1):
        a[f"c{l}"] = np.ascontiguousarray(n(f"L{l}_c").reshape(B, KT, P).transpose(2, 1, 0))
    a["pick"] = pick_rows()
    a["rope"] = rope_tables()
    kt = lambda w: w.reshape(KT, P, w.shape[1]).transpose(1, 0, 2)
    wq, wk, wv, wo = (n(f"L0_attn_w{c}") for c in "qkvo")
    chunks = np.empty((KV0, 1 + 2 * REP, P, 512), np.float32)
    for kv in range(KV0):
        chunks[kv, 0] = kt(wk[:, kv * HD0:(kv + 1) * HD0]).reshape(P, 512)
        for r in range(REP):
            h = kv * REP + r
            chunks[kv, 1 + r] = kt(wq[:, h * HD0:(h + 1) * HD0]).reshape(P, 512)
            chunks[kv, 1 + REP + r] = wo[h * HD0:(h + 1) * HD0]
    a["chunks"] = chunks.reshape(KV0 * (1 + 2 * REP), P, 512)
    wvc = np.empty((PAIRS, 2, P, 512), np.float32)
    for pr in range(PAIRS):
        w = kt(wv[:, pr * 2 * HD0:(pr + 1) * 2 * HD0])
        for c in range(2):
            wvc[pr, c] = w[:, 2 * c:2 * c + 2].reshape(P, 512)
    a["wv_chunks"] = wvc.reshape(PAIRS * 2, P, 512)
    f = lambda k: n("L0_ffn_" + k)
    a["router_w"] = np.ascontiguousarray(kt(f("router_w")))
    for k in ("router_b", "router_bias"):
        a[k] = np.ascontiguousarray(np.broadcast_to(f(k), (P, E0)))
    a["descend"] = np.ascontiguousarray(np.broadcast_to(np.arange(E0, 0, -1, dtype=np.float32), (P, E0)))
    ec = np.empty((EX, 3, P, 512), np.float32)
    eb = np.empty((P, EX, 2), np.float32)
    b3 = np.zeros((EX, D), np.float32)
    for e in range(E0):
        ec[e, 0], ec[e, 1] = (kt(f(k)[e]).reshape(P, 512) for k in ("ew1", "ew2"))
        ec[e, 2] = f("ew3")[e]
        eb[:, e, 0], eb[:, e, 1] = f("eb1")[e], f("eb2")[e]
    b3[:E0], b3[E0] = f("eb3"), f("sb3")
    for m in range(2):
        c = slice(m * INTER, (m + 1) * INTER)
        ec[E0 + m, 0], ec[E0 + m, 1] = (kt(f(k)[:, c]).reshape(P, 512) for k in ("sw1", "sw2"))
        ec[E0 + m, 2] = f("sw3")[c]
        eb[:, E0 + m, 0], eb[:, E0 + m, 1] = f("sb1")[c], f("sb2")[c]
    l1 = [n(f"L1_attn_w{c}").T for c in "qkvo"] + [n("L1_ffn_W").T, np.concatenate(
        [n("L1_ffn_Wq").T, n("L1_ffn_Wk").T], axis=1)]
    a["l1_chunks"] = np.ascontiguousarray(np.stack(l1).reshape(6 * KT, P, D))
    a["lora_a"] = np.ascontiguousarray(kt(n("L1_ffn_A").reshape(E1 * R1, D).T))
    a["lora_b"] = np.ascontiguousarray(n("L1_ffn_Bm").transpose(0, 2, 1).reshape(E1 * R1, D))
    a["l1_bias"] = np.ascontiguousarray(np.broadcast_to(n("L1_ffn_b"), (P, D)))
    a["rope1"] = rope1_tables()
    a["expert_chunks"], a["expert_biases"], a["expert_b3"] = ec.reshape(EX * 3, P, 512), eb, b3
    return a


def program(nc, arrays, upto=99):
    a = {k: nc.dram_tensor(f"in_{k}", v.shape, mybir.dt.from_np(v.dtype), kind="ExternalInput").ap()
         for k, v in arrays.items()}
    a["gate_rows"] = nc.dram_tensor("gate_rows_scratch", (2, P, 2, B, D), F32, kind="Internal").ap()
    out = nc.dram_tensor("out", (B * T, D), F32, kind="ExternalOutput").ap()
    build(nc, a, out, upto)


def kernel(**inputs):
    import concourse.bacc as _bacc
    from concourse.bass_utils import run_bass_kernel_spmd as _run

    nc = _bacc.Bacc("TRN2", target_bir_lowering=False, num_devices=1)
    arrays = lay_out(inputs)
    program(nc, arrays)
    r = _run(nc, [{f"in_{k}": v for k, v in arrays.items()}], core_ids=[0])
    return r.results[0]["out"].reshape(B, T, D)
```

```python
from contextlib import ExitStack

import numpy as np

import concourse.bass as bass
from concourse import mybir

F32 = mybir.dt.float32
F32R = mybir.dt.float32r
BF16 = mybir.dt.bfloat16
ALU = mybir.AluOpType
ACT = mybir.ActivationFunctionType
AX_X = mybir.AxisListType.X

P = 128
B, T, D = 2, 512, 512
KT = D // P
TT = T // P
NT = B * TT
EPS = 1e-5

H0, KV0, HD0 = 32, 8, 128
REP = H0 // KV0
PAIRS = KV0 // 2
E0, INTER, GROUPS = 16, 128, 4
EX = E0 + 2
H1, HD1 = 32, 16
VW = HD1 + 1
E1, DK1, R1 = 8, 32, 16
NEG = -1e30



def rope_tables():
    theta, factor, hi_ff, lo_ff, orig = 500000.0, 8.0, 4.0, 1.0, 1024
    inv = 1.0 / theta ** (np.arange(0, HD0, 2, dtype=np.float64) / HD0)
    wavelen = 2.0 * np.pi / inv
    low_wl, high_wl = orig / lo_ff, orig / hi_ff
    smooth = (orig / wavelen - lo_ff) / (hi_ff - lo_ff)
    scaled = np.where(wavelen > low_wl, inv / factor, inv)
    mid = (wavelen <= low_wl) & (wavelen >= high_wl)
    scaled = np.where(mid, (1 - smooth) * inv / factor + smooth * inv, scaled).astype(np.float32)
    freqs = np.arange(T, dtype=np.float32)[:, None] * scaled[None, :]
    emb = np.concatenate([freqs, freqs], axis=-1)
    cos, sin = np.cos(emb).T, np.sin(emb).T
    sin = np.concatenate([sin[:HD0 // 2], -sin[HD0 // 2:]], axis=0)
    return np.stack([cos, sin], axis=1).astype(np.float32)


def rope1_tables():
    pos = np.arange(T, dtype=np.float32)
    both = np.stack([np.cos(pos), np.sin(pos)]).reshape(2, TT, P)
    both = np.stack([both * float(HD1) ** -0.5, both])
    return np.ascontiguousarray(both.transpose(3, 0, 1, 2)).astype(np.float32)



class Shared:
    pass


def semaphores(nc, scope):
    taken = []

    def give_back():
        nc.clear_and_free_semaphores(taken)
        nc.all_engine_barrier()

    scope.callback(give_back)

    def new(name):
        taken.append(nc.alloc_semaphore(name))
        return taken[-1]
    return new


def three_passes(pe, out, left, right, k, start, stop):
    (lh, ll), (rh, rl) = left, right
    pe.matmul(out, lh, rh, start=start, stop=False)
    pe.matmul(out, lh, rl, start=False, stop=False)
    return pe.matmul(out, ll, rh, start=False, stop=stop)


def passed(pool, g):
    pool.sem_inc(g.passed, 1)


class Chain:

    def __init__(self, eng, sem):
        self.eng, self.sem, self.n = eng, sem, 0

    def __call__(self, ins):
        self.n += 1
        ins.then_inc(self.sem, 1)
        self.eng.wait_ge(self.sem, self.n)


class Modulation:

    ORDER = (0, 1, 2, 5, 3, 4)
    SLOTS = 4
    TURNED = (0, 1, 4, 5)

    def __init__(self, nc, ctx, g, name, c_cols, wmod, banks):
        sb = lambda n, s: ctx.enter_context(nc.sbuf_tensor(f"{name}_{n}", s, F32))
        sem = lambda n: g.sem(f"{name}_{n}")
        self.g, self.c_cols, self.wmod_dram = g, c_cols, wmod
        self.row_banks, self.col_banks = banks[0:2], banks[2:4]
        self.c = sb("c", [P, KT, B])
        self.silu_c = sb("silu_c", [P, KT, B])
        self.wmod = sb("wmod", [P, 6, KT, D])
        self.row = sb("row", [B, self.SLOTS, D])
        self.c_in, self.silu, self.row_mm, self.row_out, self.cols, self.chain = (
            sem(n) for n in ("c_in", "silu", "row_mm", "row_out", "cols", "chain"))
        self.w_in = [sem(f"w_in{n}") for n in range(6)]

    def load_c(self, queue):
        queue.dma_start(self.c[:, :, :], self.c_cols).then_inc(self.c_in, 16)

    def load(self, queue, n):
        m = self.ORDER[n]
        queue.dma_start(self.wmod[:, m, :, :], self.wmod_dram.rearrange("(k p) n -> p k n", p=P)[:, :, m * D:(m + 1) * D])\
             .then_inc(self.w_in[n], 16)

    def act(self, act):
        act.wait_ge(self.c_in, 16)
        act.activation(self.silu_c[:, :, :], self.c[:, :, :], ACT.Silu).then_inc(self.silu, 1)

    def pe_rows(self, pe, ns):
        for n in ns:
            if n == 0:
                pe.wait_ge(self.silu, 1)
            pe.wait_ge(self.w_in[n], 16)
            if n >= 2:
                pe.wait_ge(self.row_out, n - 1)
            for k in range(KT):
                mm = pe.matmul(self.row_banks[n % 2][0:B, :], self.silu_c[:, k, :], self.wmod[:, self.ORDER[n], k, :],
                               start=(k == 0), stop=(k == KT - 1))
            mm.then_inc(self.row_mm, 1)

    def pe_columns(self, pe, ns):
        for n in ns:
            at = self.TURNED.index(n)
            pe.wait_ge(self.row_out, n + 1)
            for j in range(KT):
                col = (at % 2 * KT + j) * B
                mm = pe.transpose(self.col_banks[at // 2][:, col:col + B], self.row[0:B, n % self.SLOTS, j * P:(j + 1) * P],
                                  self.g.ident[0:B, 0:B])
            mm.then_inc(self.cols, 1)

    def dve_rows(self, dve, ns):
        for n in ns:
            dve.wait_ge(self.row_mm, n + 1)
            if n == self.SLOTS:
                dve.wait_ge(self.cols, 2)
            dve.tensor_copy(self.row[0:B, n % self.SLOTS, :], self.row_banks[n % 2][0:B, :]).then_inc(self.row_out, 1)

    def dve_columns(self, dve, pair):
        link = self.link = self.link if pair else Chain(dve, self.chain)
        dve.wait_ge(self.cols, 2 * pair + 2)
        mod, m = self.g.mod, 3 * pair
        link(dve.tensor_copy(mod[:, m:m + 2, :], self.col_banks[pair][:, 0:2 * KT * B].rearrange("p (m n) -> p m n", m=2)))
        link(dve.tensor_scalar(mod[:, m + 1, :], mod[:, m + 1, :], 1.0, None, ALU.add))

    def dve_gates(self, dve, gate):
        link, raw = self.link, self.row[0:B, 2:4, :]
        dve.wait_ge(self.row_out, 4)
        link(dve.tensor_scalar(gate[0:B, :, :], raw, 0.0, 2.0, ALU.is_ge, ALU.mult))
        link(dve.scalar_tensor_tensor(out=raw, in0=raw, scalar=-1.0, in1=raw, op0=ALU.mult, op1=ALU.max))
        link(dve.tensor_scalar(raw, raw, 0.25, None, ALU.max))
        link(dve.scalar_tensor_tensor(out=gate[0:B, :, :], in0=gate[0:B, :, :], scalar=-1.0, in1=raw,
                                      op0=ALU.add, op1=ALU.mult))


class GateRows:

    def __init__(self, nc, ctx, g, name, gate, whichs, banks):
        self.g, self.gate, self.banks, self.whichs = g, gate, banks, whichs
        self.out = ctx.enter_context(nc.sbuf_tensor(f"{name}_out", [P, len(whichs), B, D], F32))
        self.rows, self.rows_out = (g.sem(f"{name}_{n}") for n in ("rows", "rows_out"))
        self.pieces = [(n, b) for n in range(len(whichs)) for b in range(B)]

    def pe(self, pe):
        for m, (n, b) in enumerate(self.pieces):
            if m >= 2:
                pe.wait_ge(self.rows_out, m - 1)
            pe.matmul(self.banks[m % 2][:, :], self.g.pick[0:B, b, :], self.gate[0:B, self.whichs[n], :],
                      start=True, stop=True).then_inc(self.rows, 1)

    def dve(self, dve):
        for m, (n, b) in enumerate(self.pieces):
            dve.wait_ge(self.rows, m + 1)
            dve.tensor_copy(self.out[:, n, b, :], self.banks[m % 2][:, :]).then_inc(self.rows_out, 1)


class Norm:

    def __init__(self, nc, ctx, g, name, scale, shift, gate=None, x_dram=None, mod_ready=None):
        sb = lambda n, s, t=F32: ctx.enter_context(nc.sbuf_tensor(f"{name}_{n}", s, t))
        sem = lambda n: g.sem(f"{name}_{n}")
        self.g, self.scale, self.shift, self.gate = g, scale, shift, gate
        self.x_dram, self.mod_ready = x_dram, mod_ready
        self.xn = sb("xn", [P, NT, D])
        self.hf = sb("hf", [P, KT, B * T])
        self.gy = sb("gy", [P, 2, D])
        self.stats = sb("stats", [P, NT, 6])
        self.mv = sb("mv", [P, NT, 2])
        self.var = sb("var", [P, NT])
        self.std = sb("std", [P, NT])
        self.rstd = sb("rstd", [P, NT])
        self.fix = sb("fix", [P, NT])
        (self.gated, self.summed, self.chain, self.var_ready, self.std_ready, self.normed, self.turned, self.affine, self.split_hi, self.split_lo) = (
            sem(n) for n in ("gated", "summed", "chain", "var_ready", "std_ready", "normed", "turned", "affine", "split_hi", "split_lo"))
        self.x_in = [sem(f"x_in{t}") for t in range(NT)] if x_dram is not None else None

    def load(self, sync, tiles=range(8)):
        for t in tiles:
            sync.dma_start(self.g.x[:, t, :], self.x_dram[t * P:(t + 1) * P, :]).then_inc(self.x_in[t], 16)

    def dve_stats(self, dve):
        g = self.g
        link = Chain(dve, self.chain)
        for b in range(B):
            tiles = range(b * TT, (b + 1) * TT)
            if self.gate is not None:
                for t in tiles:
                    if t % TT == 0:
                        dve.wait_ge(self.gate.rows_out, b + 1)
                    if t >= 2:
                        dve.wait_ge(self.summed, t - 1)
                    dve.tensor_tensor(self.gy[:, t % 2, :], g.y[:, t, :], self.gate.out[:, 0, b, :],
                                      ALU.mult).then_inc(self.gated, 1)
            for t in tiles:
                if self.gate is not None:
                    dve.wait_ge(self.summed, t + 1)
                else:
                    dve.wait_ge(self.x_in[t], 16)
                last = dve.bn_stats(self.stats[:, t, :], g.x[:, t, :])
            link(last)
            for t in tiles:
                last = dve.bn_aggr(self.mv[:, t, :], self.stats[:, t, :])
            link(last)
            h = slice(b * TT, (b + 1) * TT)
            dve.tensor_scalar(self.var[:, h], self.mv[:, h, 1], EPS, None, ALU.add).then_inc(self.var_ready, 1)
            dve.wait_ge(self.std_ready, b + 1)
            link(dve.reciprocal(self.rstd[:, h], self.std[:, h]))
            link(dve.tensor_tensor(self.fix[:, h], self.rstd[:, h], self.rstd[:, h], ALU.mult))
            link(dve.tensor_tensor(self.fix[:, h], self.fix[:, h], self.var[:, h], ALU.mult))
            link(dve.tensor_scalar(self.fix[:, h], self.fix[:, h], -0.5, 1.5, ALU.mult, ALU.add))
            link(dve.tensor_tensor(self.rstd[:, h], self.rstd[:, h], self.fix[:, h], ALU.mult))
            for t in tiles:
                dve.tensor_scalar(self.xn[:, t, :], g.x[:, t, :], self.mv[:, t, 0:1], self.rstd[:, t:t + 1],
                                  ALU.subtract, ALU.mult).then_inc(self.normed, 1)

    def dve_split(self, dve):
        g = self.g
        for b in range(B):
            for k in range(KT):
                dve.wait_ge(self.split_hi, b * KT + k + 1)
                cols = slice(b * T, (b + 1) * T)
                dve.tensor_tensor(g.hl[:, k, cols], self.hf[:, k, cols], g.hh[:, k, cols].bitcast(F32),
                                  ALU.subtract).then_inc(self.split_lo, 1)

    def act(self, act):
        g = self.g
        for b in range(B):
            h = slice(b * TT, (b + 1) * TT)
            act.wait_ge(self.var_ready, b + 1)
            act.activation(self.std[:, h], self.var[:, h], ACT.Sqrt).then_inc(self.std_ready, 1)
        if self.mod_ready is not None:
            act.wait_ge(*self.mod_ready)
        for b in range(B):
            for k in range(KT):
                act.wait_ge(self.turned, b * KT + k + 1)
                act.activation(self.hf[:, k, b * T:(b + 1) * T], g.bank[k][:, :], ACT.Identity,
                               scale=g.mod[:, self.scale, k * B + b:k * B + b + 1],
                               bias=g.mod[:, self.shift, k * B + b:k * B + b + 1]).then_inc(self.affine, 1)
                if b * KT + k:
                    self.act_hi(act, b * KT + k - 1)
        self.act_hi(act, B * KT - 1)

    def pe(self, pe):
        g = self.g
        for b in range(B):
            pe.wait_ge(self.normed, (b + 1) * TT)
            for k in range(KT):
                if b:
                    pe.wait_ge(self.affine, k + 1)
                for t in range(TT):
                    mm = pe.transpose(g.bank[k][:, t * P:(t + 1) * P],
                                      self.xn[:, b * TT + t, k * P:(k + 1) * P], g.ident[:, :])
                mm.then_inc(self.turned, 1)

    def act_hi(self, act, n):
        b, k = divmod(n, KT)
        cols = slice(b * T, (b + 1) * T)
        act.wait_ge(self.affine, n + 1)
        act.activation(self.g.hh[:, k, cols], self.hf[:, k, cols], ACT.Copy).then_inc(self.split_hi, 1)

    def pool(self, pool):
        g = self.g
        if self.gate is not None:
            for t in range(NT):
                if self.x_in is not None:
                    pool.wait_ge(self.x_in[t], 16)
                pool.wait_ge(self.gated, t + 1)
                pool.tensor_tensor(g.x[:, t, :], g.x[:, t, :], self.gy[:, t % 2, :], ALU.add)\
                    .then_inc(self.summed, 1)



TAIL_CUTS = (0, 0, 2, 7, 8)
OUT_AT = 1
PROJ_AT = ((0, 3), (1, 0), (1, 3), (2, 0), (3, 2))
V_AT = ((1, 0), (2, 0), (2, 0), (2, 1))
STEPS = 2 * B
KINDS = ("S", "T", "PV", "O", "OUT", "PROJ", "V")


def attention_order(more):
    ops = []

    def tail(s, u):
        n = u + 1
        seq = [("T", s, u, 0)] + ([("T", s, u, 1)] if n > 1 else [])
        for j in range(n):
            seq.append(("PV", s, u, j))
            if j + 2 < n:
                seq.append(("T", s, u, j + 2))
        return seq

    for s in range(STEPS):
        extra = {}
        if s + 1 < STEPS or more:
            for x, at in zip((4, 0, 1, 2, 3), PROJ_AT):
                extra.setdefault(at, []).append(("PROJ", s + 1, x))
        if s == 0 or (s == STEPS - 1 and more):
            for t, at in enumerate(V_AT):
                extra.setdefault(at, []).append(("V", 1 if s == 0 else 0, t))
        for u in range(TT):
            before = (s, u - 1) if u else (s - 1, TT - 1)
            rest = tail(*before) if before[0] >= 0 else []
            due = (s, u - 2) if u >= 2 else (s - 1, u + 2)
            for h in range(REP):
                ops.append(("S", s, u, h))
                if h == OUT_AT and due[0] >= 0:
                    ops.append(("OUT", *due))
                ops += rest[TAIL_CUTS[h]:TAIL_CUTS[h + 1]][:2]
                ops += extra.get((u, h), [])
                ops += rest[TAIL_CUTS[h]:TAIL_CUTS[h + 1]][2:]
    s = STEPS - 1
    ops.append(("OUT", s, TT - 2))
    ops += tail(s, TT - 1)
    ops.append(("OUT", s, TT - 1))
    return ops


def late(ops, lags):
    due = [[] for _ in range(len(ops) + 16)]
    for at, op in enumerate(ops):
        for part, lag in lags.get(op[0], ()):
            due[at + lag].append((part, op))
    return [x for place in due for x in place]


def layer0_attention(nc, g, chunks, wv_chunks, rope):
    with ExitStack() as ctx:
        g.sem = semaphores(nc, ctx)
        sb = lambda n, s, t=F32: ctx.enter_context(nc.sbuf_tensor(f"a0_{n}", s, t))
        sem = lambda n: g.sem(f"a0_{n}")
        RAW = 4
        raw = sb("raw", [P, RAW, 512])
        wq = [sb(f"wq_{p}", [P, REP, KT, HD0], F32R) for p in ("hi", "lo")]
        wk = [sb(f"wk_{p}", [P, KT, HD0], F32R) for p in ("hi", "lo")]
        wv = [sb(f"wv_{p}", [P, KT, 2 * HD0], F32R) for p in ("hi", "lo")]
        wo = [sb(f"wo_{p}", [P, REP, D], F32R) for p in ("hi", "lo")]
        v = [sb(f"v_{p}", [P, B, TT, 2 * HD0], F32R) for p in ("hi", "lo")]
        qk = [sb(f"qk_{p}", [P, 2, REP + 1, T], F32R) for p in ("hi", "lo")]
        plain = sb("plain", [P, 2, T])
        by_cos = sb("by_cos", [P, T])
        by_sin = sb("by_sin", [P, T])
        turned = sb("turned", [P, 2, T])
        probs = sb("probs", [P, 2, REP, T])
        pt = [sb(f"pt_{p}", [P, 2, REP * P], F32R) for p in ("hi", "lo")]
        o = [sb(f"o_{p}", [P, 2, REP * P], F32R) for p in ("hi", "lo")]
        table = sb("table", [P, 2, T])
        ring = REP * 2
        negmax = sb("negmax", [P, ring])
        rowsum = sb("rowsum", [P, ring])
        rsum = sb("rsum", [P, ring])
        score_banks, turn_banks, out_bank, mm_banks = g.bank[0:3], g.bank[3:5], g.bank[5], g.bank[6:8]

        raw_in = [sem(f"raw_in{r}") for r in range(RAW)]
        table_in = sem("table_in")
        names = ("raw_hi", "split", "scores", "maxed", "exped", "rsummed", "normed", "turned_mm", "pt_hi_done",
                 "pt_done", "pv", "o_hi_done", "o_done", "out_mm", "zeroed", "proj_mm", "rotated", "roped",
                 "qk_hi_done", "qk_done", "v_mm", "v_hi_done")
        s_ = {n: sem(n) for n in names}
        freed = [sem(f"freed{r}") for r in range(2)]

        full = attention_order(True)
        PER = {k: sum(op[0] == k for op in full) for k in KINDS}
        PER["O"] = STEPS * TT
        MM = ("PROJ", "V", "OUT")
        first_ops = [("PROJ", 0, 4), ("PROJ", 0, 0), ("V", 0, 0), ("PROJ", 0, 1), ("V", 0, 1), ("PROJ", 0, 2),
                     ("V", 0, 2), ("PROJ", 0, 3), ("V", 0, 3)]
        AHEAD = {"PROJ": REP + 1, "V": TT}
        MM_AHEAD = len(first_ops)
        MM_PER = sum(PER[k] for k in MM)

        W_AHEAD = [("K", 0), ("Q", 0), ("Vw", 0), ("Vw", 1), ("Q", 1), ("Q", 2), ("Q", 3)]

        def weight_order(more):
            ops = attention_order(more)
            at = {op: n for n, op in enumerate(ops)}
            out = [(2 + 4 * h, ("O", h), 0) for h in range(REP)]
            for s in (0, 2):
                if s == 0 or more:
                    for x in (4, 0, 1, 2, 3):
                        what = ("K", 0) if x == 4 else ("Q", x)
                        out.append((at["PROJ", s + 1, x] + 4, what, (s // 2 + 1)))
            out += [(at["OUT", 1, TT - 1] + 1 + 2 * h, ("O", h), 1) for h in range(REP)]
            if more:
                out += [(at["V", 1, 3] + 8 + n, ("Vw", n), 2) for n in range(2)]
            return sorted(out, key=lambda x: x[0])

        W_PER = len(weight_order(True))

        class Turn:

            def __init__(self, it, more=True, ahead=False):
                self.it, self.ahead, self.more = it, ahead, more
                self.ops = first_ops if ahead else attention_order(more)
                self.n = {}
                seen = {}
                m = -MM_AHEAD if ahead else 0
                for op in self.ops:
                    k = op[0]
                    self.n[op] = seen.get(k, 0)
                    seen[k] = self.n[op] + 1
                    if k == "PV" and op[2] == op[3]:
                        self.n["O", op[1], op[2]] = seen.get("O", 0)
                        seen["O"] = seen.get("O", 0) + 1
                    if k in MM:
                        self.n["MM", op] = m
                        m += 1
                self.weights = ([(0, w, 0) for w in W_AHEAD] if ahead else weight_order(more))
                for n, (_, w, kv) in enumerate(self.weights):
                    self.n["W", w, kv] = n - (len(W_AHEAD) if ahead else 0)

            def before(self, kind):
                if self.ahead:
                    return 0
                return self.it * PER[kind] + AHEAD.get(kind, 0)

            def done(self, *op):
                return self.before(op[0]) + (self.n[op] + 1)

            def bank(self, op):
                return self.n["MM", op] % 2

            def free(self, m):
                r = m % 2
                ahead = (MM_AHEAD + (1 if r else 0)) // 2
                n = m // 2 + 1 + ahead
                return freed[r], (n if self.ahead else self.it * (MM_PER // 2) + n)

            def evacuated(self, op):
                return self.free(self.n["MM", op])

            def chunk_in(self, c):
                r = c % RAW
                ahead = sum(x % RAW == r for x in range(-len(W_AHEAD), 0))
                n = c // RAW + 1 + ahead
                return raw_in[r], (n * 16 if self.ahead else self.it * (W_PER // RAW * 16) + n * 16)

            def split_count(self, c):
                n = c + 1 + len(W_AHEAD)
                return n if self.ahead else self.it * W_PER + n

        assert MM_PER % 2 == 0 and W_PER % RAW == 0 and PER["T"] % 2 == 0

        def project_source(tr, op):
            _, s, x = op
            kv = s // 2
            key = ("K", 0) if x == REP else ("Q", x)
            w = [t[:, :, :] if x == REP else t[:, x, :, :] for t in (wk, wq)[x < REP]]
            return w, key, kv


        def sync_turn(eng, tr):
            for n, (_, (what, which), kv) in enumerate(tr.weights):
                c = tr.n["W", (what, which), kv]
                if not (tr.ahead and c < RAW - len(W_AHEAD)):
                    eng.wait_ge(s_["split"], tr.split_count(c - RAW))
                if tr.ahead:
                    pair = 0
                else:
                    pair = tr.it
                if what == "Vw":
                    src = wv_chunks[(pair + kv // 2) * 2 + which]
                else:
                    row = {"K": 0, "Q": 1, "O": 1 + REP}[what] + which
                    src = chunks[(pair * 2 + kv) * (1 + 2 * REP) + row]
                eng.dma_start(raw[:, c % RAW, :], src).then_inc(raw_in[c % RAW], 16)

        def chunk_views(tr, what, which, kv):
            c = tr.n["W", (what, which), kv]
            dst = {"K": lambda t: t[:, :, :], "Q": lambda t: t[:, which, :, :],
                   "O": lambda t: t[:, which, :], "Vw": lambda t: t[:, 2 * which:2 * which + 2, :]}[what]
            hi, lo = (dst(t) for t in {"K": wk, "Q": wq, "O": wo, "Vw": wv}[what])
            src = raw[:, c % RAW, :]
            if what != "O":
                src = src.rearrange("p (k n) -> p k n", k=2 if what == "Vw" else KT)
            return c, hi, lo, src

        def act_split(eng, tr, what, which, kv):
            c, hi, lo, src = chunk_views(tr, what, which, kv)
            if not tr.ahead:
                if what == "K":
                    eng.wait_ge(s_["proj_mm"], tr.done("PROJ", 2 * kv - 1, REP))
                elif what == "Q":
                    eng.wait_ge(s_["proj_mm"], tr.done("PROJ", 2 * kv - 1, which))
                elif what == "Vw":
                    eng.wait_ge(s_["v_mm"], tr.done("V", 1, TT - 1))
                elif kv == 0:
                    eng.wait_ge(s_["out_mm"], tr.before("OUT"))
                else:
                    eng.wait_ge(s_["out_mm"], tr.done("OUT", 1, TT - 1))
            eng.wait_ge(*tr.chunk_in(c))
            eng.activation(hi, src, ACT.Copy).then_inc(s_["raw_hi"], 1)

        def pool_split(eng, tr, what, which, kv):
            c, hi, lo, src = chunk_views(tr, what, which, kv)
            eng.wait_ge(s_["raw_hi"], tr.split_count(c))
            eng.tensor_tensor(lo, src, hi.bitcast(F32), ALU.subtract).then_inc(s_["split"], 1)

        def rope_slot(tr, op):
            return (tr.n[op] + (0 if tr.ahead else 1)) % 2

        def pool_rope(eng, tr, op):
            eng.wait_ge(s_["rotated"], tr.done(*op))
            if not tr.ahead or tr.n[op] >= 2:
                eng.wait_ge(s_["qk_done"], tr.done(*op) - 2)
            eng.tensor_tensor(turned[:, rope_slot(tr, op), :], by_cos[:, :], by_sin[:, :], ALU.add).then_inc(s_["roped"], 1)

        def act_rope(eng, tr, op):
            _, s, x = op
            if not tr.ahead:
                eng.wait_ge(s_["scores"], tr.before("S") + (s - 1) * TT * REP)
            eng.wait_ge(s_["roped"], tr.done(*op))
            eng.activation(qk[0][:, s % 2, x, :], turned[:, rope_slot(tr, op), :], ACT.Copy)\
               .then_inc(s_["qk_hi_done"], 1)

        def pool_rope_lo(eng, tr, op):
            _, s, x = op
            eng.wait_ge(s_["qk_hi_done"], tr.done(*op))
            eng.tensor_tensor(qk[1][:, s % 2, x, :], turned[:, rope_slot(tr, op), :], qk[0][:, s % 2, x, :].bitcast(F32),
                              ALU.subtract).then_inc(s_["qk_done"], 1)

        def with_weights(tr, pieces):
            items = [(at, 1, part, op) for at, part, op in pieces]
            items += [(n, 0, "split", w) for n, *w in tr.weights]
            return [x[2:] for x in sorted(items, key=lambda x: x[:2])]

        def pool_turn(eng, tr):
            work = [(n + lag, part, op) for n, op in enumerate(tr.ops) if op[0] == "PROJ"
                    for part, lag in (("rope", 2), ("lo", 4))]
            for part, op in with_weights(tr, work):
                if part == "split":
                    pool_split(eng, tr, *op[0], op[1])
                elif part == "rope":
                    pool_rope(eng, tr, op)
                else:
                    pool_rope_lo(eng, tr, op)

        def pe_turn(eng, tr):
            for op in tr.ops:
                kind = op[0]
                if kind in MM:
                    m = tr.n["MM", op]
                    bank = mm_banks[m % 2]
                    if not (tr.ahead and m < 2 - MM_AHEAD):
                        eng.wait_ge(*tr.free(m - 2))
                if kind == "PROJ":
                    _, s, x = op
                    b = s % B
                    w, key, kv = project_source(tr, op)
                    if tr.ahead:
                        eng.wait_ge(s_["split"], tr.split_count(tr.n["W", key, 0]))
                    elif s > 1:
                        eng.wait_ge(s_["split"], tr.split_count(tr.n["W", key, kv]))
                    cols = slice(b * T, (b + 1) * T)
                    for k in range(KT):
                        mm = three_passes(eng, bank[:, :], [t[:, k, :] for t in w],
                                          [t[:, k, cols] for t in (g.hh, g.hl)], k, k == 0, k == KT - 1)
                    mm.then_inc(s_["proj_mm"], 1)
                elif kind == "V":
                    _, b, t = op
                    if tr.ahead:
                        eng.wait_ge(s_["split"], tr.split_count(tr.n["W", ("Vw", 1), 0]))
                    elif b == 0:
                        eng.wait_ge(s_["split"], tr.split_count(tr.n["W", ("Vw", 1), 2]))
                    cols = slice(b * T + t * P, b * T + (t + 1) * P)
                    for k in range(KT):
                        mm = three_passes(eng, bank[:, 0:2 * HD0], [x[:, k, cols] for x in (g.hh, g.hl)],
                                          [x[:, k, :] for x in wv], k, k == 0, k == KT - 1)
                    mm.then_inc(s_["v_mm"], 1)
                elif kind == "OUT":
                    _, s, u = op
                    eng.wait_ge(s_["o_done"], tr.before("O") + tr.n["O", s, u] + 1)
                    eng.wait_ge(s_["split"], tr.split_count(tr.n["W", ("O", REP - 1), s // 2]))
                    slot = tr.n["O", s, u] % 2
                    for h in range(REP):
                        mm = three_passes(eng, bank[:, :], [t[:, slot, h * P:(h + 1) * P] for t in o],
                                          [t[:, h, :] for t in wo], h, h == 0, h == REP - 1)
                    mm.then_inc(s_["out_mm"], 1)
                elif kind == "S":
                    _, s, u, h = op
                    n = tr.n[op]
                    eng.wait_ge(s_["exped"], tr.before("S") + max(n - 2, 0))
                    if s == 0:
                        if u == 0 and h == 0:
                            eng.wait_ge(s_["qk_done"], tr.before("PROJ"))
                    elif u == 0:
                        eng.wait_ge(s_["qk_done"], tr.done("PROJ", s, h))
                    width = max(2 * P, (u + 1) * P)
                    q = [t[:, s % 2, h, u * P:(u + 1) * P] for t in qk]
                    kk = [t[:, s % 2, REP, 0:width] for t in qk]
                    bank = score_banks[n % 3]
                    three_passes(eng, bank[:, 0:width], q, kk, 0, True, False)
                    eng.matmul(bank[:, u * P:(u + 1) * P], g.eye16[:, :], g.mask[:, :], start=False, stop=True)\
                       .then_inc(s_["scores"], 1)
                elif kind == "T":
                    _, s, u, j = op
                    n = tr.n[op]
                    if j == 0:
                        eng.wait_ge(s_["normed"], tr.done("S", s, u, REP - 1))
                    eng.wait_ge(s_["pt_done"], tr.before("T") + max(n - 1, 0))
                    unit = s * TT + u
                    for h in range(REP):
                        mm = eng.transpose(turn_banks[n % 2][:, h * P:(h + 1) * P],
                                           probs[:, unit % 2, h, j * P:(j + 1) * P], g.ident[:, :])
                    mm.then_inc(s_["turned_mm"], 1)
                elif kind == "PV":
                    _, s, u, j = op
                    slot = tr.n["T", s, u, j] % 2
                    b, kv = s % B, s // 2
                    eng.wait_ge(s_["pt_done"], tr.done("T", s, u, j))
                    if j == 0:
                        if u == 0 and s == 0:
                            eng.wait_ge(*tr.free(-2))
                            eng.wait_ge(*tr.free(-1))
                        elif u == 0 and s == 1:
                            eng.wait_ge(*tr.evacuated(("V", 1, TT - 2)))
                            eng.wait_ge(*tr.evacuated(("V", 1, TT - 1)))
                        eng.wait_ge(s_["o_done"], tr.before("O") + tr.n["O", s, u])
                    three_passes(eng, out_bank[:, :], [t[:, b, j, kv * HD0:(kv + 1) * HD0] for t in v],
                                 [t[:, slot, :] for t in pt], 0, j == 0, j == u).then_inc(s_["pv"], 1)

        def act_turn(eng, tr):
            lags = {"S": [("exp", 0)], "T": [("hi", 0)], "PV": [("hi", 0)],
                    "PROJ": [("copy", 1), ("turned", 4)], "V": [("hi", 0)]}
            pieces = sorted((n + lag, m, part, op) for n, op in enumerate(tr.ops)
                            for m, (part, lag) in enumerate(lags.get(op[0], ())))
            for part, op in with_weights(tr, [(n, part, op) for n, _, part, op in pieces]):
                kind = op[0]
                if part == "split":
                    act_split(eng, tr, *op[0], op[1])
                elif part == "turned":
                    act_rope(eng, tr, op)
                elif kind == "PROJ":
                    n, slot = tr.n[op], rope_slot(tr, op)
                    eng.wait_ge(s_["proj_mm"], tr.done(*op))
                    if not (tr.ahead and n < 2):
                        eng.wait_ge(s_["rotated"], tr.done(*op) - 2)
                    eng.activation(plain[:, slot, :], mm_banks[tr.bank(op)][:, :], ACT.Copy,
                                   scale=float(HD0) ** -0.5 if op[2] < REP else 1.0)\
                       .then_inc(freed[tr.bank(op)], 1)
                elif kind == "V":
                    _, b, t = op
                    eng.wait_ge(s_["v_mm"], tr.done(*op))
                    if not tr.ahead:
                        eng.wait_ge(s_["pv"], tr.done("PV", 2, TT - 1, TT - 1) if b == 0 else tr.before("PV"))
                    eng.activation(v[0][:, b, t, :], mm_banks[tr.bank(op)][:, 0:2 * HD0], ACT.Copy)\
                       .then_inc(s_["v_hi_done"], 1)
                elif kind == "S":
                    _, s, u, h = op
                    n, unit = tr.n[op], s * TT + u
                    w = (u + 1) * P
                    eng.wait_ge(s_["maxed"], tr.done(*op))
                    if h == 0:
                        if unit >= 2:
                            s2, u2 = divmod(unit - 2, TT)
                            eng.wait_ge(s_["turned_mm"], tr.done("T", s2, u2, u2))
                        else:
                            eng.wait_ge(s_["turned_mm"], tr.before("T"))
                    eng.activation(probs[:, unit % 2, h, 0:w], score_banks[n % 3][:, 0:w], ACT.Exp,
                                   bias=negmax[:, n % ring:n % ring + 1],
                                   accum_out=rowsum[:, n % ring:n % ring + 1]).then_inc(s_["exped"], 1)
                elif kind == "T":
                    n = tr.n[op]
                    eng.wait_ge(s_["turned_mm"], tr.done(*op))
                    if n >= 2:
                        eng.wait_ge(s_["pv"], tr.before("PV") + (n - 1))
                    else:
                        eng.wait_ge(s_["pv"], tr.before("PV"))
                    eng.activation(pt[0][:, n % 2, :], turn_banks[n % 2][:, :], ACT.Copy)\
                       .then_inc(s_["pt_hi_done"], 1)
                elif kind == "PV" and op[2] == op[3]:
                    k = tr.n["O", op[1], op[2]]
                    eng.wait_ge(s_["pv"], tr.done(*op))
                    eng.wait_ge(s_["out_mm"], tr.before("OUT") + max(k - 1, 0))
                    eng.activation(o[0][:, k % 2, :], out_bank[:, :], ACT.Copy).then_inc(s_["o_hi_done"], 1)

        def dve_turn(eng, tr):
            lags = {"S": [("max", 0), ("norm", 3)], "T": [("lo", 1)], "PV": [("lo", 1)], "PROJ": [("rotate", 3)],
                    "V": [("lo", 1)], "OUT": [("add", 5)]}
            for part, op in late(tr.ops, lags):
                kind = op[0]
                if kind == "PROJ":
                    n, slot = tr.n[op], rope_slot(tr, op)
                    eng.wait_ge(*tr.evacuated(op))
                    if not (tr.ahead and n == 0):
                        eng.wait_ge(s_["roped"], tr.done(*op) - 1)
                    half = HD0 // 2
                    eng.tensor_tensor(by_cos[:, :], plain[:, slot, :], table[:, 0, :], ALU.mult)
                    for a, z in ((0, half), (half, 0)):
                        last = eng.tensor_tensor(by_sin[z:z + half, :], plain[a:a + half, slot, :],
                                                 table[a:a + half, 1, :], ALU.mult)
                    last.then_inc(s_["rotated"], 1)
                elif kind == "V":
                    _, b, t = op
                    eng.wait_ge(s_["v_hi_done"], tr.done(*op))
                    eng.tensor_tensor(v[1][:, b, t, :], mm_banks[tr.bank(op)][:, 0:2 * HD0],
                                      v[0][:, b, t, :].bitcast(F32), ALU.subtract)\
                       .then_inc(freed[tr.bank(op)], 1)
                elif part == "max":
                    _, s, u, h = op
                    n = tr.n[op]
                    eng.wait_ge(s_["scores"], tr.done(*op))
                    eng.tensor_reduce(negmax[:, n % ring:n % ring + 1], score_banks[n % 3][:, 0:(u + 1) * P],
                                      AX_X, ALU.max, negate=True).then_inc(s_["maxed"], 1)
                elif part == "norm":
                    _, s, u, h = op
                    n, unit = tr.n[op], s * TT + u
                    eng.wait_ge(s_["exped"], tr.done(*op))
                    eng.reciprocal(rsum[:, n % ring:n % ring + 1], rowsum[:, n % ring:n % ring + 1])\
                       .then_inc(s_["rsummed"], 1)
                    eng.wait_ge(s_["rsummed"], tr.done(*op))
                    p_ = probs[:, unit % 2, h, 0:(u + 1) * P]
                    eng.tensor_scalar(p_, p_, rsum[:, n % ring:n % ring + 1], None, ALU.mult)\
                       .then_inc(s_["normed"], 1)
                elif kind == "T":
                    n = tr.n[op]
                    eng.wait_ge(s_["pt_hi_done"], tr.done(*op))
                    eng.tensor_tensor(pt[1][:, n % 2, :], turn_banks[n % 2][:, :], pt[0][:, n % 2, :].bitcast(F32),
                                      ALU.subtract).then_inc(s_["pt_done"], 1)
                elif kind == "PV" and op[2] == op[3]:
                    k = tr.n["O", op[1], op[2]]
                    eng.wait_ge(s_["o_hi_done"], tr.before("O") + (k + 1))
                    eng.tensor_tensor(o[1][:, k % 2, :], out_bank[:, :], o[0][:, k % 2, :].bitcast(F32),
                                      ALU.subtract).then_inc(s_["o_done"], 1)
                elif kind == "OUT":
                    _, s, u = op
                    y = g.y[:, (s % B) * TT + u, :]
                    eng.wait_ge(s_["out_mm"], tr.done(*op))
                    eng.wait_ge(*(tr.evacuated(("OUT", s - 2, u)) if s >= 2 else tr.free(-1)))
                    eng.tensor_tensor(y, mm_banks[tr.bank(op)][:, :], y, ALU.add)\
                       .then_inc(freed[tr.bank(op)], 1)

        def turns(eng, body):
            body(eng, Turn(-1, ahead=True))
            body(eng, Turn(0))
            with eng.Fori(1, PAIRS - 1) as it:
                body(eng, Turn(it))
            body(eng, Turn(PAIRS - 1, more=False))

        block = ctx.enter_context(nc.Block())

        @block.sync
        def _(sync):
            sync.dma_start(table[:, :, :], rope).then_inc(table_in, 16)
            turns(sync, sync_turn)

        @block.gpsimd
        def _(pool):
            turns(pool, pool_turn)

        @block.tensor
        def _(pe):
            turns(pe, pe_turn)

        @block.scalar
        def _(act):
            turns(act, act_turn)

        @block.vector
        def _(dve):
            dve.memset(g.y[:, :, :], 0.0).then_inc(s_["zeroed"], 1)
            dve.wait_ge(s_["zeroed"], 1)
            dve.wait_ge(table_in, 16)
            turns(dve, dve_turn)



class Router:

    def __init__(self, nc, ctx, g, norm, bank, w, b, bias, descend):
        sb = lambda n, s: ctx.enter_context(nc.sbuf_tensor(f"r_{n}", s, F32))
        sem = lambda n: g.sem(f"r_{n}")
        self.g, self.norm, self.bank = g, norm, bank
        self.srcs = (w, b, bias, descend)
        self.w = sb("w", [P, KT, E0])
        self.b, self.bias, self.descend = (sb(n, [P, E0]) for n in ("b", "bias", "descend"))
        self.e, self.p, self.q, self.hit, self.kept = (sb(n, [P, NT, E0]) for n in ("e", "p", "q", "hit", "kept"))
        self.one, self.two = sb("one", [P, NT]), sb("two", [P, NT])
        self.gmax, self.keep, self.ghit, self.gq = (sb(n, [P, NT, GROUPS]) for n in ("gmax", "keep", "ghit", "gq"))
        self.loaded, self.logits, self.chain, self.shifted, self.exped = (
            sem(n) for n in ("loaded", "logits", "chain", "shifted", "exped"))

    def load(self, eng):
        for dst, src in zip((self.w[:, :, :], self.b[:, :], self.bias[:, :], self.descend[:, :]), self.srcs):
            eng.dma_start(dst, src).then_inc(self.loaded, 16)

    def pe(self, pe):
        pe.wait_ge(self.loaded, 64)
        for t in range(NT):
            if t % TT == 0:
                pe.wait_ge(self.norm.affine, (t // TT + 1) * KT)
            for k in range(KT):
                mm = pe.matmul(self.bank[:, t * E0:(t + 1) * E0], self.norm.hf[:, k, t * P:(t + 1) * P],
                               self.w[:, k, :], start=(k == 0), stop=(k == KT - 1))
        mm.then_inc(self.logits, 1)

    def act(self, act):
        act.wait_ge(self.shifted, 1)
        act.activation(self.e[:, :, :], self.e[:, :, :], ACT.Exp).then_inc(self.exped, 1)

    def dve(self, dve):
        g = self.g
        link = Chain(dve, self.chain)
        over = lambda x, n: x.unsqueeze(2).to_broadcast([P, NT, n])
        each = lambda x, n: x.unsqueeze(1).to_broadcast([P, NT, n])
        dve.wait_ge(self.logits, 1)
        dve.wait_ge(self.loaded, 64)
        link(dve.tensor_tensor(self.e[:, :, :], self.bank[:, 0:NT * E0].rearrange("p (t e) -> p t e", e=E0),
                               each(self.b[:, :], E0), ALU.add))
        link(dve.tensor_reduce(self.one[:, :], self.e[:, :, :], AX_X, ALU.max))
        dve.tensor_tensor(self.e[:, :, :], self.e[:, :, :], over(self.one[:, :], E0), ALU.subtract)\
           .then_inc(self.shifted, 1)
        dve.wait_ge(self.exped, 1)
        link(dve.tensor_reduce(self.one[:, :], self.e[:, :, :], AX_X, ALU.add))
        link(dve.reciprocal(self.two[:, :], self.one[:, :]))
        link(dve.tensor_tensor(self.p[:, :, :], self.e[:, :, :], over(self.two[:, :], E0), ALU.mult))
        link(dve.tensor_tensor(self.p[:, :, :], self.p[:, :, :], each(self.bias[:, :], E0), ALU.add))

        def best_two(values, work, hit, kept, n):
            for turn in range(2):
                src = values if turn == 0 else work
                link(dve.tensor_reduce(self.one[:, :], src, AX_X, ALU.max))
                link(dve.tensor_tensor(hit, src, over(self.one[:, :], n), ALU.is_equal))
                link(dve.tensor_tensor(hit, hit, each(self.descend[:, 0:n], n), ALU.mult))
                link(dve.tensor_reduce(self.two[:, :], hit, AX_X, ALU.max))
                link(dve.tensor_tensor(hit, hit, over(self.two[:, :], n), ALU.is_equal))
                if turn == 0:
                    link(dve.tensor_copy(kept, hit))
                    link(dve.scalar_tensor_tensor(out=work, in0=hit, scalar=NEG, in1=src,
                                                  op0=ALU.mult, op1=ALU.add))
                else:
                    link(dve.tensor_tensor(kept, kept, hit, ALU.add))

        link(dve.tensor_reduce(self.gmax[:, :, :].rearrange("p t a -> p (t a)"),
                               self.p[:, :, :].rearrange("p t (a e) -> p (t a) e", a=GROUPS), AX_X, ALU.max))
        best_two(self.gmax[:, :, :], self.gq[:, :, :], self.ghit[:, :, :], self.keep[:, :, :], GROUPS)
        wide = self.keep[:, :, :].rearrange("p t a -> p (t a)").unsqueeze(2).to_broadcast(
            [P, NT * GROUPS, E0 // GROUPS])
        by_group = lambda x: x[:, :, :].rearrange("p t (a e) -> p (t a) e", a=GROUPS)
        link(dve.tensor_tensor(by_group(self.q), by_group(self.p), wide, ALU.mult))
        link(dve.tensor_scalar(self.keep[:, :, :], self.keep[:, :, :], -1.0, -NEG, ALU.add, ALU.mult))
        link(dve.tensor_tensor(by_group(self.q), by_group(self.q), wide, ALU.add))
        best_two(self.q[:, :, :], self.q[:, :, :], self.hit[:, :, :], self.kept[:, :, :], E0)
        link(dve.tensor_tensor(g.gates[:, :, 0:E0], self.p[:, :, :], self.kept[:, :, :], ALU.mult))
        link(dve.memset(g.gates[:, :, E0:EX], 1.0))


def layer0_experts(nc, g, chunks, biases, b3, next_c, next_wmod):
    with ExitStack() as ctx:
        g.sem = semaphores(nc, ctx)
        sb = lambda n, s, t=F32: ctx.enter_context(nc.sbuf_tensor(f"e0_{n}", s, t))
        sem = lambda n: g.sem(f"e0_{n}")
        TURNS, RAW, CH = EX // 2, 3, 3
        raw = sb("raw", [P, RAW, 512])
        w12 = [sb(f"w12_{p}", [P, 2, 2, KT, INTER], F32R) for p in ("hi", "lo")]
        w3 = [sb(f"w3_{p}", [P, 2, D], F32R) for p in ("hi", "lo")]
        bias = sb("bias", [P, EX, 2])
        bias_now = sb("bias_now", [P, 2, 2])
        gate_now = sb("gate_now", [P, NT, 2])
        b3_rows = sb("b3", [EX, D])
        gates_t = sb("gates_t", [EX, NT * P])
        silu = sb("silu", [P, B, T])
        prod = sb("prod", [P, B, T])
        pr = [sb(f"prod_{p}", [P, B, T], F32R) for p in ("hi", "lo")]
        raw_in = [sem(f"raw_in{r}") for r in range(RAW)]
        names = ("small_in", "raw_hi", "split", "turned", "turned_sb", "up_mm", "silu_done", "prod_done", "prod_hi",
                 "prod_lo", "down_mm", "added", "bias_set", "gate_set")
        s_ = {n: sem(n) for n in names}
        mod = Modulation(nc, ctx, g, "m1", next_c, next_wmod, g.bank[0:4])
        UPS, DOWNS = 2 * B, 2 * NT
        order = [("H", 0, 0), ("H", 0, 1), ("Y", 0, 0), ("H", 1, 0), ("Y", 0, 1), ("H", 1, 1), ("Y", 1, 0),
                 ("Y", 1, 1)]

        def tiles(p, b):
            return [((p * B + b) * TT + t, b * TT + t) for t in range(TT)]

        def load_expert(eng, row, n, first):
            for c in range(CH):
                if not first:
                    eng.wait_ge(s_["split"], (n - 1) * CH + (c + 1))
                eng.dma_start(raw[:, c, :], chunks[row * CH + c]).then_inc(raw_in[c], 16)

        def views(p, c):
            if c < 2:
                return *(t[:, p, c, :, :] for t in w12), raw[:, c, :].rearrange("p (k n) -> p k n", k=KT)
            return *(t[:, p, :] for t in w3), raw[:, c, :]

        def hi_expert(act, p, n, used, chunks=range(CH)):
            for c in chunks:
                used(act, c)
                act.wait_ge(raw_in[c], (n + 1) * 16)
                hi, _, src = views(p, c)
                act.activation(hi, src, ACT.Copy).then_inc(s_["raw_hi"], 1)

        def lo_expert(pool, p, n):
            for c in range(CH):
                hi, lo, src = views(p, c)
                pool.wait_ge(s_["raw_hi"], n * CH + (c + 1))
                pool.tensor_tensor(lo, src, hi.bitcast(F32), ALU.subtract).then_inc(s_["split"], 1)

        def hi_product(act, it, p, b):
            act.wait_ge(s_["prod_done"], it * UPS + (p * B + b + 1))
            if p:
                act.wait_ge(s_["down_mm"], it * DOWNS + ((p - 1) * B + b + 1) * TT)
            else:
                act.wait_ge(s_["down_mm"], it * DOWNS)
            act.activation(pr[0][:, b, :], prod[:, b, :], ACT.Copy).then_inc(s_["prod_hi"], 1)

        def lo_product(pool, it, p, b):
            pool.wait_ge(s_["prod_hi"], it * UPS + (p * B + b + 1))
            pool.tensor_tensor(pr[1][:, b, :], prod[:, b, :], pr[0][:, b, :].bitcast(F32), ALU.subtract)\
                .then_inc(s_["prod_lo"], 1)

        def pool_turn(pool, it, more):
            pool.wait_ge(s_["silu_done"], it * UPS)
            pool.wait_ge(s_["small_in"], 32)
            passed(pool, g)
            pool.tensor_copy(bias_now[:, :, :], bias[:, bass.ds(it * 2, 2), :]).then_inc(s_["bias_set"], 1)
            lo_expert(pool, 1, it * 2 + 1)
            lo_product(pool, it, 0, 0)
            lo_product(pool, it, 0, 1)
            lo_product(pool, it, 1, 0)
            if more:
                lo_expert(pool, 0, it * 2 + 2)
            lo_product(pool, it, 1, 1)

        def pe_turn(eng, it, more):
            for kind, p, b in order:
                if kind == "H":
                    n = it * UPS + (p * B + b)
                    if b == 0:
                        eng.wait_ge(s_["split"], it * 2 * CH + (p * CH + 2))
                    if p:
                        eng.wait_ge(s_["prod_done"], n - 1)
                    else:
                        eng.wait_ge(s_["prod_done"], it * UPS)
                    if not more and p == 0:
                        eng.wait_ge(mod.chain, 4)
                    cols = slice(b * T, (b + 1) * T)
                    for c in range(2):
                        for k in range(KT):
                            mm = three_passes(eng, g.bank[2 * b + c][:, :], [t[:, p, c, k, :] for t in w12],
                                              [t[:, k, cols] for t in (g.hh, g.hl)], k, k == 0, k == KT - 1)
                    mm.then_inc(s_["up_mm"], 1)
                else:
                    if b == 0:
                        eng.wait_ge(s_["split"], it * 2 * CH + (p + 1) * CH)
                    eng.wait_ge(s_["prod_lo"], it * UPS + (p * B + b + 1))
                    for (k, t) in tiles(p, b):
                        eng.wait_ge(s_["added"], it * DOWNS + (k + NT - 3))
                        three_passes(eng, g.bank[4 + t % 4][:, :], [x[:, b, (t % TT) * P:(t % TT + 1) * P] for x in pr],
                                     [x[:, p, :] for x in w3], 0, True, True).then_inc(s_["down_mm"], 1)

        def act_turn(act, it, more):
            def used_second(eng, c):
                eng.wait_ge(*((s_["up_mm"], it * UPS) if c < 2 else (s_["down_mm"], it * DOWNS)))

            def used_first(eng, c):
                eng.wait_ge(*((s_["up_mm"], it * UPS + B) if c < 2 else (s_["down_mm"], it * DOWNS + NT)))

            def silu_of(p, b):
                act.wait_ge(s_["up_mm"], it * UPS + (p * B + b + 1))
                if p:
                    act.wait_ge(s_["prod_done"], it * UPS + (b + 1))
                else:
                    act.wait_ge(s_["prod_done"], it * UPS)
                act.activation(silu[:, b, :], g.bank[2 * b][:, :], ACT.Silu, bias=bias_now[:, p, 0:1])\
                   .then_inc(s_["silu_done"], 1)

            act.wait_ge(s_["bias_set"], it + 1)
            hi_expert(act, 1, it * 2 + 1, used_second)
            silu_of(0, 0)
            hi_product(act, it, 0, 0)
            silu_of(0, 1)
            hi_product(act, it, 0, 1)
            silu_of(1, 0)
            hi_product(act, it, 1, 0)
            if more:
                hi_expert(act, 0, it * 2 + 2, used_first)
            silu_of(1, 1)
            hi_product(act, it, 1, 1)

        def dve_turn(eng, it, more):
            eng.wait_ge(s_["added"], it * DOWNS + NT)
            eng.tensor_copy(gate_now[:, :, :], g.gates[:, :, bass.ds(it * 2, 2)]).then_inc(s_["gate_set"], 1)
            eng.wait_ge(s_["gate_set"], it + 1)
            eng.wait_ge(s_["bias_set"], it + 1)
            for kind, p, b in order:
                if kind == "H":
                    n = it * UPS + (p * B + b)
                    eng.wait_ge(s_["silu_done"], n + 1)
                    if p:
                        eng.wait_ge(s_["prod_lo"], n - 1)
                    else:
                        eng.wait_ge(s_["prod_lo"], it * UPS)
                    eng.scalar_tensor_tensor(out=prod[:, b, :], in0=g.bank[2 * b + 1][:, :],
                                             scalar=bias_now[:, p, 1:2], in1=silu[:, b, :],
                                             op0=ALU.add, op1=ALU.mult).then_inc(s_["prod_done"], 1)
                else:
                    for (k, t) in tiles(p, b):
                        eng.wait_ge(s_["down_mm"], it * DOWNS + (k + 1))
                        eng.wait_ge(s_["added"], it * DOWNS + (k + 1))
                        eng.scalar_tensor_tensor(out=g.y[:, t, :], in0=g.bank[4 + t % 4][:, :],
                                                 scalar=gate_now[:, t, p:p + 1], in1=g.y[:, t, :],
                                                 op0=ALU.mult, op1=ALU.add).then_inc(s_["added"], 1)

        def turns(eng, body, between=lambda n: None):
            body(eng, 0, True)
            between(0)
            with eng.Fori(1, TURNS - 1) as it:
                body(eng, it, True)
            between(1)
            body(eng, TURNS - 1, False)

        block = ctx.enter_context(nc.Block())

        @block.sync
        def _(sync):
            sync.dma_start(bias[:, :, :], biases).then_inc(s_["small_in"], 16)
            sync.dma_start(b3_rows[:, :], b3).then_inc(s_["small_in"], 16)
            load_expert(sync, 0, 0, True)

            def body(eng, it, more):
                load_expert(eng, it * 2 + 1, it * 2 + 1, False)
                if more:
                    load_expert(eng, it * 2 + 2, it * 2 + 2, False)
            turns(sync, body)

        @block.gpsimd
        def _(pool):
            lo_expert(pool, 0, 0)
            turns(pool, pool_turn)

        @block.tensor
        def _(pe):
            for t in range(NT):
                mm = pe.transpose(g.bank[t // TT][0:EX, (t % TT) * P:(t % TT + 1) * P], g.gates[:, t, :],
                                  g.ident[:, :])
            mm.then_inc(s_["turned"], 1)
            pe.wait_ge(s_["turned_sb"], 2)
            pe.wait_ge(s_["small_in"], 32)
            for t in range(NT):
                if t >= TT:
                    pe.wait_ge(s_["added"], t - TT + 1)
                pe.matmul(g.bank[4 + t % 4][:, :], gates_t[:, t * P:(t + 1) * P], b3_rows[:, :],
                          start=True, stop=True).then_inc(s_["turned"], 1)

            def modulate(n):
                if n:
                    pe.wait_ge(s_["prod_done"], (TURNS - 1) * UPS)
                    mod.pe_rows(pe, range(4))
                    mod.pe_columns(pe, (0, 1))
                    mod.pe_rows(pe, (4, 5))
                    mod.pe_columns(pe, (4, 5))
            turns(pe, pe_turn, modulate)

        @block.scalar
        def _(act):
            mod.load_c(act)
            hi_expert(act, 0, 0, lambda eng, c: None)

            def load_mod(n):
                if n:
                    mod.act(act)
                    return
                for m in range(6):
                    mod.load(act, m)
            turns(act, act_turn, load_mod)

        @block.vector
        def _(dve):
            dve.wait_ge(s_["turned"], 1)
            for n in range(2):
                dve.tensor_copy(gates_t[:, n * TT * P:(n + 1) * TT * P], g.bank[n][0:EX, :]).then_inc(s_["turned_sb"], 1)
            for t in range(NT):
                dve.wait_ge(s_["turned"], t + 2)
                dve.tensor_copy(g.y[:, t, :], g.bank[4 + t % 4][:, :]).then_inc(s_["added"], 1)

            def modulate(n):
                if n:
                    mod.dve_rows(dve, range(4))
                    mod.dve_columns(dve, 0)
                    mod.dve_rows(dve, (4, 5))
                    mod.dve_columns(dve, 1)
                    mod.dve_gates(dve, g.gate1)
            turns(dve, dve_turn, modulate)



SLOT = 64
STACK = ((0, 2), (0, 1))


def split_weights(pool, g, raw, raw_in, hi_sem, split_sem, items, n=0):
    for hi, lo, view in items:
        src = view(raw[:, n % raw.shape[1], :])
        pool.wait_ge(raw_in[n % raw.shape[1]], (n // raw.shape[1] + 1) * 16)
        pool.tensor_copy(hi, src).then_inc(hi_sem, 1)
        pool.wait_ge(hi_sem, n + 1)
        pool.tensor_tensor(lo, src, hi.bitcast(F32), ALU.subtract).then_inc(split_sem, 1)
        n += 1


def load_weights(sync, raw, raw_in, split_sem, sources):
    ring = raw.shape[1]
    for n, src in enumerate(sources):
        if n >= ring:
            sync.wait_ge(split_sem, n - ring + 1)
        sync.dma_start(raw[:, n % ring, :], src).then_inc(raw_in[n % ring], 16)


def layer1_projections(nc, g, weights, rope1):
    with ExitStack() as ctx:
        g.sem = semaphores(nc, ctx)
        sb = lambda n, s, t=F32: ctx.enter_context(nc.sbuf_tensor(f"p1_{n}", s, t))
        sem = lambda n: g.sem(f"p1_{n}")
        RAW = 2
        raw = sb("raw", [P, RAW, 512])
        w = [sb(f"w_{p}", [P, 3, KT, D], F32R) for p in ("hi", "lo")]
        trig = sb("trig", [P, 2, 2, TT])
        by_cos, by_sin = (sb(n, [P, 2, D]) for n in ("by_cos", "by_sin"))
        raw_in = [sem(f"raw_in{r}") for r in range(RAW)]
        s_ = {n: sem(n) for n in ("trig_in", "raw_hi", "split", "mm", "cos_done",
                                                    "v_done", "even", "odd", "ones")}
        freed = [sem(f"freed{r}") for r in range(4)]
        pieces = [(t, c) for t in range(NT) for c in range(3)]
        rotated = [(t, c) for t, c in pieces if c < 2]
        block = ctx.enter_context(nc.Block())

        @block.sync
        def _(sync):
            sync.dma_start(trig[:, :, :, :], rope1).then_inc(s_["trig_in"], 16)
            load_weights(sync, raw, raw_in, s_["split"], [weights[c * KT + k] for c in range(3) for k in range(KT)])

        @block.gpsimd
        def _(pool):
            items = [(w[0][:, c, k, :], w[1][:, c, k, :], lambda r: r) for c in range(3) for k in range(KT)]
            split_weights(pool, g, raw, raw_in, s_["raw_hi"], s_["split"], items)
            pair = lambda x: x.rearrange("p (i two) -> p i two", two=2)
            for n, (t, c) in enumerate(rotated):
                dst = pair((g.q1 if c == 0 else g.k1)[:, t, :])
                cos, sin = pair(by_cos[:, n % 2, :]), pair(by_sin[:, n % 2, :])
                pool.wait_ge(s_["cos_done"], n + 1)
                m = pieces.index((t, c))
                pool.wait_ge(freed[m % 4], m // 4 + 1)
                pool.tensor_tensor(dst[:, :, 0], cos[:, :, 0], sin[:, :, 1], ALU.subtract).then_inc(s_["even"], 1)
                pool.tensor_tensor(dst[:, :, 1], cos[:, :, 1], sin[:, :, 0], ALU.add).then_inc(s_["odd"], 1)

        @block.tensor
        def _(pe):
            for n, (t, c) in enumerate(pieces):
                if n < 3:
                    pe.wait_ge(s_["split"], (c + 1) * KT)
                if n >= 4:
                    pe.wait_ge(freed[n % 4], n // 4)
                for k in range(KT):
                    mm = three_passes(pe, g.bank[n % 4][:, :], [x[:, k, t * P:(t + 1) * P] for x in (g.hh, g.hl)],
                                      [x[:, c, k, :] for x in w], k, k == 0, k == KT - 1)
                mm.then_inc(s_["mm"], 1)

        @block.scalar
        def _(act):
            act.wait_ge(s_["trig_in"], 16)
            for n, (t, c) in enumerate(pieces):
                if c == 2:
                    continue
                r = rotated.index((t, c))
                act.wait_ge(s_["mm"], n + 1)
                if r >= 2:
                    act.wait_ge(s_["odd"], r - 1)
                act.activation(by_cos[:, r % 2, :], g.bank[n % 4][:, :], ACT.Copy,
                               scale=trig[:, c, 0, t % TT:t % TT + 1]).then_inc(s_["cos_done"], 1)

        @block.vector
        def _(dve):
            dve.memset(g.v1[:, :, :, HD1:VW], 1.0).then_inc(s_["ones"], 1)
            dve.wait_ge(s_["trig_in"], 16)
            for n, (t, c) in enumerate(pieces):
                bank = g.bank[n % 4]
                dve.wait_ge(s_["mm"], n + 1)
                if c == 2:
                    dve.tensor_copy(g.v1[:, t, :, 0:HD1], bank[:, :].rearrange("p (h d) -> p h d", h=H1))\
                       .then_inc(freed[n % 4], 1)
                    continue
                r = rotated.index((t, c))
                dve.wait_ge(s_["cos_done"], r + 1)
                if r >= 2:
                    dve.wait_ge(s_["odd"], r - 1)
                dve.tensor_scalar(by_sin[:, r % 2, :], bank[:, :], trig[:, c, 1, t % TT:t % TT + 1], None, ALU.mult)\
                   .then_inc(freed[n % 4], 1)


def layer1_attention(nc, g, b):
    with ExitStack() as ctx:
        g.sem = semaphores(nc, ctx)
        sb = lambda n, s, t=F32: ctx.enter_context(nc.sbuf_tensor(f"a1{b}_{n}", s, t))
        sem = lambda n: g.sem(f"a1{b}_{n}")
        PR = H1 // 2
        stack = sb("stack", [P, 2, H1, 4, HD1], F32R)
        turned = [sb(n, [P, PR, T], F32R) for n in ("q", "k")]
        probs = sb("probs", [P, 2, TT, T])
        BLOCKS = TT * (TT + 1) // 2
        pt = sb("pt", [P, 2, BLOCKS, P])
        out_t = sb("out_t", [P, TT, P])
        negmax = sb("negmax", [P, 2, TT])
        rsum = sb("rsum", [P, 2, TT, 4])
        names = ("hi", "lo", "turn", "taken_a", "taken_v", "scores", "maxed", "exped", "pt_mm", "pt_a", "pt_v",
                 "pv", "out_t", "back", "rsummed", "normed")
        s_ = {n: sem(n) for n in names}
        SB = 3
        score_banks, back_bank, turn_banks, out_banks = g.bank[0:SB], g.bank[3], g.bank[4:6], g.bank[6:8]
        stacks = [(t, c) for t in range(TT) for c in range(2)]
        STRIPS = [[(j, u) for j in js for u in range(j, TT)] for js in ((0,), (1,), (2, 3))]
        FIRST = [0, 4, 7]
        where = {ju: FIRST[n] + m for n, strip in enumerate(STRIPS) for m, ju in enumerate(strip)}
        HG = 4
        HP = P // HG

        block = ctx.enter_context(nc.Block())

        def copies(c, n, lo):
            s = stack[:, n % 2, :, :, :]
            if c == 0:
                return s[:, :, lo:4:2, :]
            return s[:, :, 2 * lo:2 * lo + 2, :]

        def source(t, c):
            return (g.q1 if c == 0 else g.k1)[:, b * TT + t, :].rearrange("p (h d) -> p h d", h=H1)\
                .unsqueeze(2).to_broadcast([P, H1, 2, HD1])

        def wait_turned_copy(eng, h, n):
            eng.wait_ge(*((s_["pt_a"], h + 1) if n == 2 else (s_["pt_v"], 2 * h + n + 1)))

        @block.tensor
        def _(pe):
            for n, (t, c) in enumerate(stacks):
                pe.wait_ge(s_["lo"], n + 1)
                flat = stack[:, n % 2, :, :, :].rearrange("p h a d -> p (h a d)").bitcast(F32)
                for q in range(4):
                    m = 4 * n + q
                    if m >= 8:
                        pe.wait_ge((s_["taken_a"], s_["taken_v"])[m % 2], (m - 8) // 2 + 1)
                    for r in range(4):
                        mm = pe.transpose(g.bank[m % 8][:, r * P:(r + 1) * P],
                                          flat[:, (q * 4 + r) * P:(q * 4 + r + 1) * P], g.ident[:, :])
                    mm.then_inc(s_["turn"], 1)
            pe.wait_ge(s_["taken_a"], 16)
            pe.wait_ge(s_["taken_v"], 16)

            def score(h, u):
                n = h * TT + u
                if n >= SB:
                    pe.wait_ge(s_["exped"], n - SB + 1)
                rows = slice(SLOT * (h % 2), SLOT * (h % 2 + 1))
                w = max(2, u + 1) * P
                bank = score_banks[n % SB]
                pe.matmul(bank[:, 0:w], turned[0][rows, h // 2, u * P:(u + 1) * P], turned[1][rows, h // 2, 0:w],
                          start=True, stop=False)
                pe.matmul(bank[:, u * P:(u + 1) * P], g.eye16[:, :], g.mask[:, :], start=False, stop=True)\
                    .then_inc(s_["scores"], 1)

            def turn(h, n):
                pe.wait_ge(s_["exped"], (h + 1) * TT)
                k = 3 * h + n
                if k >= 2:
                    wait_turned_copy(pe, *divmod(k - 2, 3))
                for m, (j, u) in enumerate(STRIPS[n]):
                    mm = pe.transpose(turn_banks[k % 2][:, m * P:(m + 1) * P], probs[:, h % 2, u, j * P:(j + 1) * P],
                                      g.ident[:, :])
                mm.then_inc(s_["pt_mm"], 1)

            def values(h, j):
                grp, i = h // HG, h % HG
                wait_turned_copy(pe, h, min(j, 2))
                if j == 0 and i == 0 and grp >= 2:
                    pe.wait_ge(s_["out_t"], grp - 1)
                mm = pe.matmul(out_banks[grp % 2][i * HP:i * HP + VW, j * P:], g.v1[:, b * TT + j, h, :],
                               pt[:, h % 2, where[j, j]:where[j, j] + TT - j, :].rearrange("p a x -> p (a x)"),
                               start=(j == 0), stop=(j == TT - 1))
                if j == TT - 1:
                    mm.then_inc(s_["pv"], 1)

            def back(grp):
                pe.wait_ge(s_["out_t"], grp + 1)
                if grp:
                    pe.wait_ge(s_["normed"], grp)
                for u in range(TT):
                    mm = pe.transpose(back_bank[:, u * P:(u + 1) * P], out_t[:, u, :], g.ident[:, :])
                mm.then_inc(s_["back"], 1)

            for h in range(H1 + 2):
                new, old, oldest = h < H1, 1 <= h <= H1, h >= 2
                if new:
                    score(h, 0)
                if oldest:
                    values(h - 2, 0)
                if new:
                    score(h, 1)
                if oldest:
                    values(h - 2, 1)
                if old:
                    turn(h - 1, 0)
                if new:
                    score(h, 2)
                if old:
                    turn(h - 1, 1)
                if new:
                    score(h, 3)
                if old:
                    turn(h - 1, 2)
                if oldest:
                    values(h - 2, 2)
                    values(h - 2, 3)
                if h >= HG + 2 and (h - 2) % HG == 0:
                    back((h - 2) // HG - 1)
            back(H1 // HG - 1)

        @block.scalar
        def _(act):
            def hi(n):
                if n >= 2:
                    act.wait_ge(s_["turn"], 4 * (n - 1))
                act.activation(copies(stacks[n][1], n, 0), source(*stacks[n]), ACT.Copy).then_inc(s_["hi"], 1)

            hi(0)
            for n, (t, c) in enumerate(stacks):
                if n + 1 < len(stacks):
                    hi(n + 1)
                for q in range(0, 4, 2):
                    m = 4 * n + q
                    act.wait_ge(s_["turn"], m + 1)
                    act.activation(turned[c][:, q * 4:q * 4 + 4, t * P:(t + 1) * P],
                                   g.bank[m % 8][:, :].rearrange("p (a x) -> p a x", a=4), ACT.Copy)\
                       .then_inc(s_["taken_a"], 1)

            def take(h):
                act.wait_ge(s_["pt_mm"], 3 * h + 3)
                if h >= 2:
                    act.wait_ge(s_["pv"], h - 1)
                act.activation(pt[:, h % 2, FIRST[2]:, :], turn_banks[(3 * h + 2) % 2][:, 0:3 * P]
                               .rearrange("p (a x) -> p a x", a=3), ACT.Copy).then_inc(s_["pt_a"], 1)

            def out_of_bank(grp):
                act.wait_ge(s_["pv"], HG * (grp + 1))
                if grp:
                    act.wait_ge(s_["back"], grp)
                act.activation(out_t[:, :, :], out_banks[grp % 2][:, :].rearrange("p (u x) -> p u x", u=TT), ACT.Copy)\
                    .then_inc(s_["out_t"], 1)

            for h in range(H1 + 1):
                for u in range(TT):
                    n = h * TT + u
                    if h < H1:
                        act.wait_ge(s_["maxed"], n + 1)
                        if h >= 2 and u == 0:
                            act.wait_ge(s_["pt_mm"], 3 * (h - 1))
                        act.activation(probs[:, h % 2, u, 0:(u + 1) * P], score_banks[n % SB][:, 0:(u + 1) * P],
                                       ACT.Exp, bias=negmax[:, h % 2, u:u + 1]).then_inc(s_["exped"], 1)
                    if u == 0 and h >= HG + 2 and (h - 2) % HG == 0:
                        out_of_bank((h - 2) // HG - 1)
                    if u == 3 and h:
                        take(h - 1)
            out_of_bank(H1 // HG - 1)

        @block.vector
        def _(dve):
            for n, (t, c) in enumerate(stacks):
                dve.wait_ge(s_["hi"], n + 1)
                hi = stack[:, n % 2, :, 0:1, :].bitcast(F32).to_broadcast([P, H1, 2, HD1])
                dve.tensor_tensor(copies(c, n, 1), source(t, c), hi, ALU.subtract).then_inc(s_["lo"], 1)
                for q in range(1, 4, 2):
                    m = 4 * n + q
                    dve.wait_ge(s_["turn"], m + 1)
                    dve.tensor_copy(turned[c][:, q * 4:q * 4 + 4, t * P:(t + 1) * P],
                                    g.bank[m % 8][:, :].rearrange("p (a x) -> p a x", a=4)).then_inc(s_["taken_v"], 1)

            def take(h, n):
                dve.wait_ge(s_["pt_mm"], 3 * h + n + 1)
                if n == 0 and h >= 2:
                    dve.wait_ge(s_["pv"], h - 1)
                k = len(STRIPS[n])
                dve.tensor_copy(pt[:, h % 2, FIRST[n]:FIRST[n] + k, :],
                                turn_banks[(3 * h + n) % 2][:, 0:k * P].rearrange("p (a x) -> p a x", a=k))\
                   .then_inc(s_["pt_v"], 1)

            def finish(grp):
                out = back_bank[:, :].rearrange("p (u h d) -> p u h d", u=TT, h=HG)
                dve.wait_ge(s_["back"], grp + 1)
                dve.reciprocal(rsum[:, grp % 2, :, :], out[:, :, :, HD1]).then_inc(s_["rsummed"], 1)
                dve.wait_ge(s_["rsummed"], grp + 1)
                dst = g.q1[:, b * TT:(b + 1) * TT, grp * HG * HD1:(grp + 1) * HG * HD1]\
                    .rearrange("p u (h d) -> p u h d", h=HG)
                dve.tensor_tensor(dst, out[:, :, :, 0:HD1],
                                  rsum[:, grp % 2, :, :].unsqueeze(3).to_broadcast([P, TT, HG, HD1]), ALU.mult)\
                   .then_inc(s_["normed"], 1)

            for h in range(H1 + 1):
                for u in range(TT):
                    if h < H1:
                        n = h * TT + u
                        dve.wait_ge(s_["scores"], n + 1)
                        dve.tensor_reduce(negmax[:, h % 2, u:u + 1], score_banks[n % SB][:, 0:(u + 1) * P], AX_X,
                                          ALU.max, negate=True).then_inc(s_["maxed"], 1)
                    if u == 0 and h >= HG + 3 and (h - 3) % HG == 0:
                        finish((h - 3) // HG - 1)
                    if h and u in (1, 2):
                        take(h - 1, u - 1)
            finish(H1 // HG - 1)


def layer1_output(nc, g, weights):
    with ExitStack() as ctx:
        g.sem = semaphores(nc, ctx)
        sb = lambda n, s, t=F32: ctx.enter_context(nc.sbuf_tensor(f"o1_{n}", s, t))
        sem = lambda n: g.sem(f"o1_{n}")
        RAW = 4
        raw = sb("raw", [P, RAW, 512])
        w = [sb(f"w_{p}", [P, KT, D], F32R) for p in ("hi", "lo")]
        o = [sb(f"o_{p}", [P, KT, B * T], F32R) for p in ("hi", "lo")]
        raw_in = [sem(f"raw_in{r}") for r in range(RAW)]
        s_ = {n: sem(n) for n in ("raw_hi", "split", "turn", "hi", "lo", "mm", "out")}
        block = ctx.enter_context(nc.Block())

        @block.sync
        def _(sync):
            load_weights(sync, raw, raw_in, s_["split"], [weights[3 * KT + k] for k in range(KT)])

        @block.gpsimd
        def _(pool):
            split_weights(pool, g, raw, raw_in, s_["raw_hi"], s_["split"],
                          [(w[0][:, k, :], w[1][:, k, :], lambda r: r) for k in range(KT)])

        @block.tensor
        def _(pe):
            def turn(t):
                if t >= 2:
                    pe.wait_ge(s_["lo"], t - 1)
                for k in range(KT):
                    mm = pe.transpose(g.bank[t % 2][:, k * P:(k + 1) * P], g.q1[:, t, k * P:(k + 1) * P], g.ident[:, :])
                mm.then_inc(s_["turn"], 1)

            turn(0)
            turn(1)
            for t in range(NT):
                if t + 2 < NT:
                    turn(t + 2)
                pe.wait_ge(s_["lo"], t + 1)
                if t == 0:
                    pe.wait_ge(s_["split"], KT)
                if t >= 4:
                    pe.wait_ge(s_["out"], t - 3)
                for k in range(KT):
                    mm = three_passes(pe, g.bank[2 + t % 4][:, :], [x[:, k, t * P:(t + 1) * P] for x in o],
                                      [x[:, k, :] for x in w], k, k == 0, k == KT - 1)
                mm.then_inc(s_["mm"], 1)

        @block.scalar
        def _(act):
            for t in range(NT):
                act.wait_ge(s_["turn"], t + 1)
                act.activation(o[0][:, :, t * P:(t + 1) * P], g.bank[t % 2][:, :].rearrange("p (k x) -> p k x", k=KT),
                               ACT.Copy).then_inc(s_["hi"], 1)

        @block.vector
        def _(dve):
            def out(t):
                dve.wait_ge(s_["mm"], t + 1)
                dve.tensor_copy(g.y[:, t, :], g.bank[2 + t % 4][:, :]).then_inc(s_["out"], 1)

            for t in range(NT):
                dve.wait_ge(s_["hi"], t + 1)
                dve.tensor_tensor(o[1][:, :, t * P:(t + 1) * P], g.bank[t % 2][:, :].rearrange("p (k x) -> p k x", k=KT),
                                  o[0][:, :, t * P:(t + 1) * P].bitcast(F32), ALU.subtract).then_inc(s_["lo"], 1)
                if t >= 2:
                    out(t - 2)
            out(NT - 2)
            out(NT - 1)



def layer1_experts(nc, g, norm, rows, weights, a_w, b_w, bias_row, out_dram):
    with ExitStack() as ctx:
        g.sem = semaphores(nc, ctx)
        sb = lambda n, s, t=F32: ctx.enter_context(nc.sbuf_tensor(f"l1_{n}", s, t))
        sem = lambda n: g.sem(f"l1_{n}")
        RAW, ER = 2, E1 * R1
        raw = sb("raw", [P, RAW, 512])
        w = [sb(f"w_{p}", [P, 2, KT, D], F32R) for p in ("hi", "lo")]
        bw = [sb(f"b_{p}", [P, D], F32R) for p in ("hi", "lo")]
        aw = sb("aw", [P, KT, ER])
        bias = sb("bias", [P, D])
        k_sb = sb("k_sb", [P, 2, E1 * DK1])
        qk = sb("qk", [P, 2, E1 * DK1])
        sc, ex, wt = (sb(n, [P, 2, E1]) for n in ("sc", "ex", "wt"))
        mx, sm, rs = (sb(n, [P, 2]) for n in ("mx", "sm", "rs"))
        wh = sb("wh", [P, 2, ER])
        wht = [sb(f"wht_{p}", [P, 2, P], F32R) for p in ("hi", "lo")]
        biased = sb("biased", [P, 2, D])
        gated = sb("gated", [P, 2, D])
        final = sb("final", [P, 2, D])
        raw_in = [sem(f"raw_in{r}") for r in range(RAW)]
        names = ("small_in", "raw_hi", "split", "res_mm", "qk_mm", "a_mm", "k_copied", "chain", "scored", "exped",
                 "rs", "wt", "weighted", "turned", "t_hi", "t_lo", "b_mm", "biased", "gated", "final")
        s_ = {n: sem(n) for n in names}
        stored = [sem(f"stored{r}") for r in range(2)]
        block = ctx.enter_context(nc.Block())

        @block.sync
        def _(sync):
            for dst, src in ((aw[:, :, :], a_w), (bias[:, :], bias_row)):
                sync.dma_start(dst, src).then_inc(s_["small_in"], 16)
            load_weights(sync, raw, raw_in, s_["split"], [weights[(4 + c) * KT + k] for c in (1, 0) for k in range(KT)] + [b_w])
            for t in range(NT):
                sync.wait_ge(s_["final"], t + 1)
                sync.dma_start(out_dram[t * P:(t + 1) * P, :], final[:, t % 2, :]).then_inc(stored[t % 2], 16)
            for slot in stored:
                sync.wait_ge(slot, 16 * (NT // 2))

        @block.gpsimd
        def _(pool):
            items = [(w[0][:, c, k, :], w[1][:, c, k, :], lambda r: r) for c in (1, 0) for k in range(KT)]
            items.append((bw[0][:, :], bw[1][:, :], lambda r: r))
            split_weights(pool, g, raw, raw_in, s_["raw_hi"], s_["split"], items)
            for t in range(NT):
                pool.wait_ge(s_["biased"], t + 1)
                if t >= 2:
                    pool.wait_ge(s_["final"], t - 1)
                pool.tensor_tensor(gated[:, t % 2, :], biased[:, t % 2, :], rows.out[:, 1, t // TT, :], ALU.mult)\
                    .then_inc(s_["gated"], 1)
                pool.wait_ge(s_["gated"], t + 1)
                if t >= 2:
                    pool.wait_ge(stored[t % 2], 16 * (t // 2))
                pool.tensor_tensor(final[:, t % 2, :], gated[:, t % 2, :], g.x[:, t, :], ALU.add).then_inc(s_["final"], 1)

        @block.tensor
        def _(pe):
            def front(t):
                cols = slice(t * P, (t + 1) * P)
                if t == 0:
                    pe.wait_ge(s_["split"], KT)
                if t >= 2:
                    pe.wait_ge(s_["scored"], t - 1)
                for k in range(KT):
                    mm = three_passes(pe, g.bank[3 + t % 2][:, :], [x[:, k, cols] for x in (g.hh, g.hl)],
                                      [x[:, 1, k, :] for x in w], k, k == 0, k == KT - 1)
                mm.then_inc(s_["qk_mm"], 1)
                pe.wait_ge(s_["small_in"], 32)
                if t >= 2:
                    pe.wait_ge(s_["weighted"], t - 1)
                for k in range(KT):
                    mm = pe.matmul(g.bank[5 + t % 2][:, 0:ER], norm.hf[:, k, cols], aw[:, k, :],
                                   start=(k == 0), stop=(k == KT - 1))
                mm.then_inc(s_["a_mm"], 1)
                if t == 0:
                    pe.wait_ge(s_["split"], 2 * KT)
                if t >= 3:
                    pe.wait_ge(s_["biased"], t - 2)
                for k in range(KT):
                    mm = three_passes(pe, g.bank[t % 3][:, :], [x[:, k, cols] for x in (g.hh, g.hl)],
                                      [x[:, 0, k, :] for x in w], k, k == 0, False)

            front(0)
            for t in range(NT):
                if t + 1 < NT:
                    front(t + 1)
                pe.wait_ge(s_["weighted"], t + 1)
                if t >= 1:
                    pe.wait_ge(s_["t_lo"], t)
                pe.transpose(g.bank[7][:, 0:P], wh[:, t % 2, :], g.ident[:, :]).then_inc(s_["turned"], 1)
                pe.wait_ge(s_["t_lo"], t + 1)
                if t == 0:
                    pe.wait_ge(s_["split"], 2 * KT + 1)
                three_passes(pe, g.bank[t % 3][:, :], [x[:, t % 2, :] for x in wht], [x[:, :] for x in bw],
                             0, False, True).then_inc(s_["b_mm"], 1)

        @block.scalar
        def _(act):
            for t in range(NT):
                act.wait_ge(s_["qk_mm"], t + 1)
                if t >= 2:
                    act.wait_ge(s_["scored"], t - 1)
                act.activation(k_sb[:, t % 2, :], g.bank[3 + t % 2][:, E1 * DK1:2 * E1 * DK1], ACT.Copy)\
                    .then_inc(s_["k_copied"], 1)
                act.wait_ge(s_["chain"], 3 * t + 3)
                act.activation(ex[:, t % 2, :], sc[:, t % 2, :], ACT.Exp, bias=mx[:, t % 2:t % 2 + 1],
                               scale=float(DK1) ** -0.5, accum_out=sm[:, t % 2:t % 2 + 1]).then_inc(s_["exped"], 1)
                act.wait_ge(s_["turned"], t + 1)
                if t >= 2:
                    act.wait_ge(s_["b_mm"], t - 1)
                act.activation(wht[0][:, t % 2, :], g.bank[7][:, 0:P], ACT.Copy).then_inc(s_["t_hi"], 1)

        @block.vector
        def _(dve):
            dve.wait_ge(s_["small_in"], 32)

            def last(t):
                dve.wait_ge(s_["t_hi"], t + 1)
                dve.tensor_tensor(wht[1][:, t % 2, :], g.bank[7][:, 0:P], wht[0][:, t % 2, :].bitcast(F32),
                                  ALU.subtract).then_inc(s_["t_lo"], 1)
                dve.wait_ge(s_["b_mm"], t + 1)
                if t >= 2:
                    dve.wait_ge(s_["gated"], t - 1)
                dve.tensor_tensor(biased[:, t % 2, :], g.bank[t % 3][:, :], bias[:, :], ALU.add).then_inc(s_["biased"], 1)

            for t in range(NT):
                p = t % 2
                dve.wait_ge(s_["k_copied"], t + 1)
                dve.tensor_tensor(qk[:, p, :], g.bank[3 + p][:, 0:E1 * DK1], k_sb[:, p, :], ALU.mult).then_inc(s_["scored"], 1)
                dve.wait_ge(s_["scored"], t + 1)
                dve.tensor_reduce(sc[:, p, :], qk[:, p, :].rearrange("p (e d) -> p e d", e=E1), AX_X, ALU.add)\
                   .then_inc(s_["chain"], 1)
                dve.wait_ge(s_["chain"], 3 * t + 1)
                dve.tensor_reduce(mx[:, p:p + 1], sc[:, p, :], AX_X, ALU.max, negate=True).then_inc(s_["chain"], 1)
                dve.wait_ge(s_["chain"], 3 * t + 2)
                dve.tensor_scalar(mx[:, p:p + 1], mx[:, p:p + 1], float(DK1) ** -0.5, None, ALU.mult).then_inc(s_["chain"], 1)
                dve.wait_ge(s_["exped"], t + 1)
                dve.reciprocal(rs[:, p:p + 1], sm[:, p:p + 1]).then_inc(s_["rs"], 1)
                dve.wait_ge(s_["rs"], t + 1)
                dve.tensor_scalar(wt[:, p, :], ex[:, p, :], rs[:, p:p + 1], None, ALU.mult).then_inc(s_["wt"], 1)
                dve.wait_ge(s_["wt"], t + 1)
                dve.wait_ge(s_["a_mm"], t + 1)
                if t >= 2:
                    dve.wait_ge(s_["turned"], t - 1)
                dve.tensor_tensor(wh[:, p, :].rearrange("p (e r) -> p e r", e=E1),
                                  g.bank[5 + p][:, 0:ER].rearrange("p (e r) -> p e r", e=E1),
                                  wt[:, p, :].unsqueeze(2).to_broadcast([P, E1, R1]), ALU.mult).then_inc(s_["weighted"], 1)
                last(t)



def build(nc, a, out, upto=99):
    with ExitStack() as ctx:
        sb = lambda n, s, t=F32: ctx.enter_context(nc.sbuf_tensor(n, s, t))
        g = Shared()
        g.bank = [ctx.enter_context(nc.psum_tensor(f"bank{i}", [P, 512], F32)) for i in range(8)]
        g.y = sb("y", [P, NT, D])

        def operands(scope, name):
            g.hh, g.hl = (scope.enter_context(nc.sbuf_tensor(f"h_{p}_{name}", [P, KT, B * T], F32R))
                          for p in ("hi", "lo"))

        g.mod = sb("mod", [P, 6, KT * B])
        g.pick = sb("pick", [B, B, P])
        g.ident = sb("ident", [P, P])
        g.eye16 = sb("eye16", [P, P], BF16)
        g.mask = sb("mask", [P, P], BF16)
        g.passed = ctx.enter_context(nc.semaphore("passed"))
        g.ready = ctx.enter_context(nc.semaphore("ready"))
        dbg = lambda: None

        part = ctx.enter_context(ExitStack())
        operands(part, "attention0")
        with ExitStack() as ph:
            sem = g.sem = semaphores(nc, ph)
            g.x = ph.enter_context(nc.sbuf_tensor("x_first", [P, NT, D], F32))
            mod = Modulation(nc, ph, g, "m0", a["c0"], a["L0_wmod"], g.bank[4:8])
            norm = Norm(nc, ph, g, "n0", 1, 0, x_dram=a["x"], mod_ready=(mod.chain, 2))
            gate = ph.enter_context(nc.sbuf_tensor("gate_first", [B, 2, D], F32))
            zeroed, eyed, picked, stored = (sem(n) for n in ("zeroed", "eyed", "picked", "stored"))
            block = ph.enter_context(nc.Block())

            @block.sync
            def _(sync):
                mod.load_c(sync)
                norm.load(sync, range(TT))
                mod.load(sync, 0)
                mod.load(sync, 1)
                norm.load(sync, range(TT, NT))
                for n in range(2, 6):
                    mod.load(sync, n)
                sync.wait_ge(mod.chain, 6)
                sync.dma_start(a["gate0"], gate[0:B, :, :]).then_inc(stored, 16)
                sync.wait_ge(stored, 16)

            @block.gpsimd
            def _(pool):
                pool.memset(g.ident[:, :], 0.0).then_inc(zeroed, 1)
                pool.memset(g.eye16[:, :], 0.0).then_inc(zeroed, 1)
                pool.memset(g.mask[:, :], 0.0).then_inc(zeroed, 1)
                pool.wait_ge(zeroed, 3)
                for eye in (g.ident, g.eye16):
                    pool.affine_select(out=eye[:, :], in_=eye[:, :], compare_op=ALU.not_equal, fill=1.0,
                                       base=0, pattern=[[-1, P]], channel_multiplier=1).then_inc(eyed, 1)
                pool.wait_ge(eyed, 2)
                pool.tensor_copy(g.pick[:, :, :], g.ident[0:B, 0:B].unsqueeze(2).to_broadcast([B, B, P])).then_inc(picked, 1)
                pool.affine_select(out=g.mask[:, :], in_=g.mask[:, :], compare_op=ALU.is_ge, fill=NEG,
                                   base=0, pattern=[[-1, P]], channel_multiplier=1).then_inc(g.ready, 1)

            @block.scalar
            def _(act):
                mod.act(act)
                norm.act(act)

            @block.tensor
            def _(pe):
                pe.wait_ge(eyed, 2)
                mod.pe_rows(pe, (0, 1))
                mod.pe_columns(pe, (0, 1))
                norm.pe(pe)
                mod.pe_rows(pe, range(2, 6))
                mod.pe_columns(pe, (4, 5))

            @block.vector
            def _(dve):
                norm.dve_stats(dve)
                mod.dve_rows(dve, (0, 1))
                mod.dve_columns(dve, 0)
                norm.dve_split(dve)
                mod.dve_rows(dve, (2, 3))
                mod.dve_gates(dve, gate)
                mod.dve_rows(dve, (4, 5))
                mod.dve_columns(dve, 1)
        if upto == 0:
            return dump(nc, g, out, g.hh, [[g.hh[:, k, t * P:(t + 1) * P] for k in range(KT)] for t in range(NT)])
        layer0_attention(nc, g, a["chunks"], a["wv_chunks"], a["rope"])
        if upto == 1:
            return dump(nc, g, out, g.y, [[g.y[:, t, k * P:(k + 1) * P] for k in range(KT)] for t in range(NT)])
        part.close()

        g.gate0, g.gate1 = (sb(f"gate{l}", [B, 2, D]) for l in (0, 1))
        g.x = sb("x", [P, NT, D])
        part = ctx.enter_context(ExitStack())
        g.gates = part.enter_context(nc.sbuf_tensor("gates", [P, NT, EX], F32))
        operands(part, "experts")
        with ExitStack() as ph:
            sem = g.sem = semaphores(nc, ph)
            gate_in = sem("gate_in")
            rows = GateRows(nc, ph, g, "rows0", g.gate0, (0,), g.bank[6:8])
            norm = Norm(nc, ph, g, "n1", 4, 3, gate=rows, x_dram=a["x"])
            router = Router(nc, ph, g, norm, g.bank[4], a["router_w"], a["router_b"], a["router_bias"], a["descend"])
            block = ph.enter_context(nc.Block())

            @block.sync
            def _(sync):
                sync.dma_start(g.gate0[0:B, :, :], a["gate0"]).then_inc(gate_in, 16)
                norm.load(sync)

            @block.gpsimd
            def _(pool):
                norm.pool(pool)

            @block.scalar
            def _(act):
                router.load(act)
                norm.act(act)
                router.act(act)

            @block.tensor
            def _(pe):
                pe.wait_ge(gate_in, 16)
                rows.pe(pe)
                norm.pe(pe)
                router.pe(pe)

            @block.vector
            def _(dve):
                rows.dve(dve)
                norm.dve_stats(dve)
                norm.dve_split(dve)
                router.dve(dve)
        if upto == 2:
            return dump(nc, g, out, g.gates, [[g.gates[:, t, 0:16] for k in range(1)] for t in range(NT)])

        layer0_experts(nc, g, a["expert_chunks"], a["expert_biases"], a["expert_b3"], a["c1"], a["L1_wmod"])
        if upto == 3:
            return dump(nc, g, out, g.y, [[g.y[:, t, k * P:(k + 1) * P] for k in range(KT)] for t in range(NT)])
        part.close()

        qkv = ctx.enter_context(ExitStack())
        g.q1 = qkv.enter_context(nc.sbuf_tensor("q1", [P, NT, D], F32))
        g.v1 = qkv.enter_context(nc.sbuf_tensor("v1", [P, NT, H1, VW], F32))
        g.k1 = g.y
        part = ctx.enter_context(ExitStack())
        operands(part, "attention1")
        with ExitStack() as ph:
            g.sem = semaphores(nc, ph)
            rows = GateRows(nc, ph, g, "rows1", g.gate0, (1,), g.bank[6:8])
            norm = Norm(nc, ph, g, "n2", 1, 0, gate=rows)
            block = ph.enter_context(nc.Block())

            @block.gpsimd
            def _(pool):
                norm.pool(pool)

            @block.scalar
            def _(act):
                norm.act(act)

            @block.tensor
            def _(pe):
                rows.pe(pe)
                norm.pe(pe)

            @block.vector
            def _(dve):
                rows.dve(dve)
                norm.dve_stats(dve)
                norm.dve_split(dve)
        if upto == 4:
            return dump(nc, g, out, g.hh, [[g.hh[:, k, t * P:(t + 1) * P] for k in range(KT)] for t in range(NT)])
        layer1_projections(nc, g, a["l1_chunks"], a["rope1"])
        part.close()
        for b in range(B):
            layer1_attention(nc, g, b)
        layer1_output(nc, g, a["l1_chunks"])
        if upto == 5:
            return dump(nc, g, out, g.y, [[g.y[:, t, k * P:(k + 1) * P] for k in range(KT)] for t in range(NT)])
        qkv.close()

        operands(ctx, "experts1")
        g.sem = semaphores(nc, ctx)
        rows = GateRows(nc, ctx, g, "rows2", g.gate1, (0, 1), g.bank[6:8])
        norm = Norm(nc, ctx, g, "n3", 4, 3, gate=rows)
        with nc.Block() as block:
            @block.gpsimd
            def _(pool):
                norm.pool(pool)

            @block.scalar
            def _(act):
                norm.act(act)

            @block.tensor
            def _(pe):
                rows.pe(pe)
                norm.pe(pe)

            @block.vector
            def _(dve):
                rows.dve(dve)
                norm.dve_stats(dve)
                norm.dve_split(dve)
        if upto == 6:
            return dump(nc, g, out, g.hh, [[g.hh[:, k, t * P:(t + 1) * P] for k in range(KT)] for t in range(NT)])
        layer1_experts(nc, g, norm, rows, a["l1_chunks"], a["lora_a"], a["lora_b"], a["l1_bias"], out)


def dump(nc, g, out, src, tiles):
    with nc.semaphore("dumped") as s, nc.Block() as block:
        @block.sync
        def _(sync):
            n = 0
            for t in range(NT):
                for k, v in enumerate(tiles[t]):
                    sync.dma_start(out[t * P:(t + 1) * P, k * P:k * P + v.shape[1]],
                                   v.bitcast(F32) if src.dtype == F32R else v).then_inc(s, 16)
                    n += 16
            sync.wait_ge(s, n)


def lay_out(i):
    n = lambda k: np.asarray(i[k])
    a = {}
    a["x"] = np.ascontiguousarray(n("L0_attn_x").reshape(B * T, D))
    a["L0_wmod"], a["L1_wmod"] = n("L0_wmod"), n("L1_wmod")
    for l in (0, 1):
        a[f"c{l}"] = np.ascontiguousarray(n(f"L{l}_c").reshape(B, KT, P).transpose(2, 1, 0))
    a["rope"] = rope_tables()
    kt = lambda w: w.reshape(KT, P, w.shape[1]).transpose(1, 0, 2)
    wq, wk, wv, wo = (n(f"L0_attn_w{c}") for c in "qkvo")
    chunks = np.empty((KV0, 1 + 2 * REP, P, 512), np.float32)
    for kv in range(KV0):
        chunks[kv, 0] = kt(wk[:, kv * HD0:(kv + 1) * HD0]).reshape(P, 512)
        for r in range(REP):
            h = kv * REP + r
            chunks[kv, 1 + r] = kt(wq[:, h * HD0:(h + 1) * HD0]).reshape(P, 512)
            chunks[kv, 1 + REP + r] = wo[h * HD0:(h + 1) * HD0]
    a["chunks"] = chunks.reshape(KV0 * (1 + 2 * REP), P, 512)
    wvc = np.empty((PAIRS, 2, P, 512), np.float32)
    for pr in range(PAIRS):
        w = kt(wv[:, pr * 2 * HD0:(pr + 1) * 2 * HD0])
        for c in range(2):
            wvc[pr, c] = w[:, 2 * c:2 * c + 2].reshape(P, 512)
    a["wv_chunks"] = wvc.reshape(PAIRS * 2, P, 512)
    f = lambda k: n("L0_ffn_" + k)
    a["router_w"] = np.ascontiguousarray(kt(f("router_w")))
    for k in ("router_b", "router_bias"):
        a[k] = np.ascontiguousarray(np.broadcast_to(f(k), (P, E0)))
    a["descend"] = np.ascontiguousarray(np.broadcast_to(np.arange(E0, 0, -1, dtype=np.float32), (P, E0)))
    ec = np.empty((EX, 3, P, 512), np.float32)
    eb = np.empty((P, EX, 2), np.float32)
    b3 = np.zeros((EX, D), np.float32)
    for e in range(E0):
        ec[e, 0], ec[e, 1] = (kt(f(k)[e]).reshape(P, 512) for k in ("ew1", "ew2"))
        ec[e, 2] = f("ew3")[e]
        eb[:, e, 0], eb[:, e, 1] = f("eb1")[e], f("eb2")[e]
    b3[:E0], b3[E0] = f("eb3"), f("sb3")
    for m in range(2):
        c = slice(m * INTER, (m + 1) * INTER)
        ec[E0 + m, 0], ec[E0 + m, 1] = (kt(f(k)[:, c]).reshape(P, 512) for k in ("sw1", "sw2"))
        ec[E0 + m, 2] = f("sw3")[c]
        eb[:, E0 + m, 0], eb[:, E0 + m, 1] = f("sb1")[c], f("sb2")[c]
    l1 = [n(f"L1_attn_w{c}").T for c in "qkvo"] + [n("L1_ffn_W").T, np.concatenate(
        [n("L1_ffn_Wq").T, n("L1_ffn_Wk").T], axis=1)]
    a["l1_chunks"] = np.ascontiguousarray(np.stack(l1).reshape(6 * KT, P, D))
    a["lora_a"] = np.ascontiguousarray(kt(n("L1_ffn_A").reshape(E1 * R1, D).T))
    a["lora_b"] = np.ascontiguousarray(n("L1_ffn_Bm").transpose(0, 2, 1).reshape(E1 * R1, D))
    a["l1_bias"] = np.ascontiguousarray(np.broadcast_to(n("L1_ffn_b"), (P, D)))
    a["rope1"] = rope1_tables()
    a["expert_chunks"], a["expert_biases"], a["expert_b3"] = ec.reshape(EX * 3, P, 512), eb, b3
    return a


def program(nc, arrays, upto=99):
    a = {k: nc.dram_tensor(f"in_{k}", v.shape, mybir.dt.from_np(v.dtype), kind="ExternalInput").ap()
         for k, v in arrays.items()}
    a["gate0"] = nc.dram_tensor("gate_scratch", (B, 2, D), F32, kind="Internal").ap()
    out = nc.dram_tensor("out", (B * T, D), F32, kind="ExternalOutput").ap()
    build(nc, a, out, upto)


def kernel(**inputs):
    import concourse.bacc as _bacc
    from concourse.bass_utils import run_bass_kernel_spmd as _run

    nc = _bacc.Bacc("TRN2", target_bir_lowering=False, num_devices=1)
    arrays = lay_out(inputs)
    program(nc, arrays)
    r = _run(nc, [{f"in_{k}": v for k, v in arrays.items()}], core_ids=[0])
    return r.results[0]["out"].reshape(B, T, D)
```

```python
from contextlib import ExitStack

import numpy as np

import concourse.bass as bass
from concourse import mybir

F32 = mybir.dt.float32
F32R = mybir.dt.float32r
BF16 = mybir.dt.bfloat16
ALU = mybir.AluOpType
ACT = mybir.ActivationFunctionType
AX_X = mybir.AxisListType.X

P = 128
B, T, D = 2, 512, 512
KT = D // P
TT = T // P
NT = B * TT
EPS = 1e-5

H0, KV0, HD0 = 32, 8, 128
REP = H0 // KV0
PAIRS = KV0 // 2
E0, INTER, GROUPS = 16, 128, 4
EX = E0 + 2
H1, HD1 = 32, 16
VW = HD1 + 1
E1, DK1, R1 = 8, 32, 16
NEG = -1e30
MOD_ORDER = (0, 1, 2, 5, 3, 4)



def rope_tables():
    theta, factor, hi_ff, lo_ff, orig = 500000.0, 8.0, 4.0, 1.0, 1024
    inv = 1.0 / theta ** (np.arange(0, HD0, 2, dtype=np.float64) / HD0)
    wavelen = 2.0 * np.pi / inv
    low_wl, high_wl = orig / lo_ff, orig / hi_ff
    smooth = (orig / wavelen - lo_ff) / (hi_ff - lo_ff)
    scaled = np.where(wavelen > low_wl, inv / factor, inv)
    mid = (wavelen <= low_wl) & (wavelen >= high_wl)
    scaled = np.where(mid, (1 - smooth) * inv / factor + smooth * inv, scaled).astype(np.float32)
    freqs = np.arange(T, dtype=np.float32)[:, None] * scaled[None, :]
    emb = np.concatenate([freqs, freqs], axis=-1)
    cos, sin = np.cos(emb).T, np.sin(emb).T
    sin = np.concatenate([sin[:HD0 // 2], -sin[HD0 // 2:]], axis=0)
    return np.stack([cos, sin], axis=1).astype(np.float32)


def rope1_tables():
    pos = np.arange(T, dtype=np.float32)
    both = np.stack([np.cos(pos), np.sin(pos)]).reshape(2, TT, P)
    both = np.stack([both * float(HD1) ** -0.5, both])
    return np.ascontiguousarray(both.transpose(3, 0, 1, 2)).astype(np.float32)



class Shared:
    pass


def semaphores(nc, scope):
    taken = []

    def give_back():
        nc.clear_and_free_semaphores(taken)
        nc.all_engine_barrier()

    scope.callback(give_back)

    def new(name):
        taken.append(nc.alloc_semaphore(name))
        return taken[-1]
    return new


def three_passes(pe, out, left, right, k, start, stop):
    (lh, ll), (rh, rl) = left, right
    pe.matmul(out, lh, rh, start=start, stop=False)
    pe.matmul(out, lh, rl, start=False, stop=False)
    return pe.matmul(out, ll, rh, start=False, stop=stop)


def passed(pool, g):
    pool.sem_inc(g.passed, 1)


class Chain:

    def __init__(self, eng, sem):
        self.eng, self.sem, self.n = eng, sem, 0

    def __call__(self, ins):
        self.n += 1
        ins.then_inc(self.sem, 1)
        self.eng.wait_ge(self.sem, self.n)


class Modulation:

    SLOTS = 4
    TURNED = (0, 1, 4, 5)

    def __init__(self, nc, ctx, g, name, c_cols, wmod_chunks, banks):
        sb = lambda n, s: ctx.enter_context(nc.sbuf_tensor(f"{name}_{n}", s, F32))
        sem = lambda n: g.sem(f"{name}_{n}")
        self.g, self.c_cols, self.wmod_chunks = g, c_cols, wmod_chunks
        self.row_banks, self.col_banks = banks[0:2], banks[2:4]
        self.c = sb("c", [P, KT, B])
        self.silu_c = sb("silu_c", [P, KT, B])
        self.wmod = sb("wmod", [P, 6 * KT, D])
        self.row = sb("row", [B, self.SLOTS, D])
        self.c_in, self.silu, self.row_mm, self.row_out, self.cols, self.chain = (
            sem(n) for n in ("c_in", "silu", "row_mm", "row_out", "cols", "chain"))
        self.w_in = [sem(f"w_in{n}") for n in range(6)]
        self.all_in = sem("all_in")

    def load_c(self, queue):
        queue.dma_start(self.c[:, :, :], self.c_cols).then_inc(self.c_in, 16)

    def load(self, queue, n):
        part = slice(n * KT, (n + 1) * KT)
        queue.dma_start(self.wmod[:, part, :], self.wmod_chunks[part].rearrange("k p c -> p k c"))\
             .then_inc(self.w_in[n], 16)

    def load_chunk(self, queue, c):
        queue.dma_start(self.wmod[:, bass.ds(c, 1), :], self.wmod_chunks[bass.ds(c, 1)].rearrange("k p c -> p k c"))\
             .then_inc(self.all_in, 16)

    def act(self, act):
        act.wait_ge(self.c_in, 16)
        act.activation(self.silu_c[:, :, :], self.c[:, :, :], ACT.Silu).then_inc(self.silu, 1)

    def pe_rows(self, pe, ns, chunkwise=False):
        for n in ns:
            if n == 0:
                pe.wait_ge(self.silu, 1)
            if not chunkwise:
                pe.wait_ge(self.w_in[n], 16)
            elif n == 0:
                pe.wait_ge(self.all_in, 6 * KT * 16)
            if n >= 2:
                pe.wait_ge(self.row_out, n - 1)
            for k in range(KT):
                mm = pe.matmul(self.row_banks[n % 2][0:B, :], self.silu_c[:, k, :], self.wmod[:, n * KT + k, :],
                               start=(k == 0), stop=(k == KT - 1))
            mm.then_inc(self.row_mm, 1)

    def pe_columns(self, pe, ns):
        for n in ns:
            at = self.TURNED.index(n)
            pe.wait_ge(self.row_out, n + 1)
            for j in range(KT):
                col = (at % 2 * KT + j) * B
                mm = pe.transpose(self.col_banks[at // 2][:, col:col + B],
                                  self.row[0:B, n % self.SLOTS, j * P:(j + 1) * P], self.g.ident[0:B, 0:B])
            mm.then_inc(self.cols, 1)

    def dve_rows(self, dve, ns):
        for n in ns:
            dve.wait_ge(self.row_mm, n + 1)
            if n == self.SLOTS:
                dve.wait_ge(self.cols, 2)
            dve.tensor_copy(self.row[0:B, n % self.SLOTS, :], self.row_banks[n % 2][0:B, :]).then_inc(self.row_out, 1)

    def dve_columns(self, dve, pair):
        if pair == 0:
            self.link = Chain(dve, self.chain)
        link = self.link
        dve.wait_ge(self.cols, 2 * pair + 2)
        mod, m = self.g.mod, 3 * pair
        cols = self.col_banks[pair][:, 0:2 * KT * B].rearrange("p (m n) -> p m n", m=2)
        link(dve.tensor_copy(mod[:, m:m + 2, :], cols))
        link(dve.tensor_scalar(mod[:, m + 1, :], mod[:, m + 1, :], 1.0, None, ALU.add))

    def dve_gates(self, dve, gate):
        link, raw = self.link, self.row[0:B, 2:4, :]
        dve.wait_ge(self.row_out, 4)
        link(dve.tensor_scalar(gate[0:B, :, :], raw, 0.0, 2.0, ALU.is_ge, ALU.mult))
        link(dve.scalar_tensor_tensor(out=raw, in0=raw, scalar=-1.0, in1=raw, op0=ALU.mult, op1=ALU.max))
        link(dve.tensor_scalar(raw, raw, 0.25, None, ALU.max))
        link(dve.scalar_tensor_tensor(out=gate[0:B, :, :], in0=gate[0:B, :, :], scalar=-1.0, in1=raw,
                                      op0=ALU.add, op1=ALU.mult))


class GateRows:

    def __init__(self, nc, ctx, g, name, gate, whichs, banks):
        self.g, self.gate, self.banks, self.whichs = g, gate, banks, whichs
        self.out = ctx.enter_context(nc.sbuf_tensor(f"{name}_out", [P, len(whichs), B, D], F32))
        self.rows, self.rows_out = (g.sem(f"{name}_{n}") for n in ("rows", "rows_out"))
        self.pieces = [(n, b) for n in range(len(whichs)) for b in range(B)]

    def pe(self, pe):
        for m, (n, b) in enumerate(self.pieces):
            if m >= 2:
                pe.wait_ge(self.rows_out, m - 1)
            pe.matmul(self.banks[m % 2][:, :], self.g.pick[0:B, b, :], self.gate[0:B, self.whichs[n], :],
                      start=True, stop=True).then_inc(self.rows, 1)

    def dve(self, dve):
        for m, (n, b) in enumerate(self.pieces):
            dve.wait_ge(self.rows, m + 1)
            dve.tensor_copy(self.out[:, n, b, :], self.banks[m % 2][:, :]).then_inc(self.rows_out, 1)


class Norm:

    def __init__(self, nc, ctx, g, name, scale, shift, gate=None, x_dram=None, mod_ready=None, hf=None, xn=None):
        sb = lambda n, s, t=F32: ctx.enter_context(nc.sbuf_tensor(f"{name}_{n}", s, t))
        sem = lambda n: g.sem(f"{name}_{n}")
        self.g, self.scale, self.shift, self.gate = g, scale, shift, gate
        self.x_dram, self.mod_ready = x_dram, mod_ready
        self.xn = sb("xn", [P, NT, D]) if xn is None else xn
        self.hf = sb("hf", [P, KT, B * T]) if hf is None else hf
        self.stats = sb("stats", [P, NT, 6])
        self.mv = sb("mv", [P, NT, 2])
        self.var = sb("var", [P, NT])
        self.std = sb("std", [P, NT])
        self.rstd = sb("rstd", [P, NT])
        self.fix = sb("fix", [P, NT])
        self.gated, self.summed, self.chain, self.var_ready, self.std_ready = (
            sem(n) for n in ("gated", "summed", "chain", "var_ready", "std_ready"))
        self.normed, self.turned, self.affine, self.split_hi, self.split_lo = (
            sem(n) for n in ("normed", "turned", "affine", "split_hi", "split_lo"))
        self.x_in = [sem(f"x_in{t}") for t in range(NT)] if x_dram is not None else None

    def load(self, sync, tiles=range(NT)):
        for t in tiles:
            sync.dma_start(self.g.x[:, t, :], self.x_dram[t * P:(t + 1) * P, :]).then_inc(self.x_in[t], 16)

    def dve_stats(self, dve):
        g = self.g
        link = Chain(dve, self.chain)
        if self.gate is not None:
            for t in range(NT):
                if t % TT == 0:
                    dve.wait_ge(self.gate.rows_out, t // TT + 1)
                dve.tensor_tensor(self.xn[:, t, :], g.y[:, t, :], self.gate.out[:, 0, t // TT, :],
                                  ALU.mult).then_inc(self.gated, 1)
        for b in range(B):
            tiles = range(b * TT, (b + 1) * TT)
            for t in tiles:
                if self.gate is not None:
                    dve.wait_ge(self.summed, t + 1)
                elif self.x_in is not None:
                    dve.wait_ge(self.x_in[t], 16)
                last = dve.bn_stats(self.stats[:, t, :], g.x[:, t, :])
            link(last)
            for t in tiles:
                last = dve.bn_aggr(self.mv[:, t, :], self.stats[:, t, :])
            link(last)
            h = slice(b * TT, (b + 1) * TT)
            dve.tensor_scalar(self.var[:, h], self.mv[:, h, 1], EPS, None, ALU.add).then_inc(self.var_ready, 1)
            dve.wait_ge(self.std_ready, b + 1)
            link(dve.reciprocal(self.rstd[:, h], self.std[:, h]))
            link(dve.tensor_tensor(self.fix[:, h], self.rstd[:, h], self.rstd[:, h], ALU.mult))
            link(dve.tensor_tensor(self.fix[:, h], self.fix[:, h], self.var[:, h], ALU.mult))
            link(dve.tensor_scalar(self.fix[:, h], self.fix[:, h], -0.5, 1.5, ALU.mult, ALU.add))
            link(dve.tensor_tensor(self.rstd[:, h], self.rstd[:, h], self.fix[:, h], ALU.mult))
            for t in tiles:
                dve.tensor_scalar(self.xn[:, t, :], g.x[:, t, :], self.mv[:, t, 0:1], self.rstd[:, t:t + 1],
                                  ALU.subtract, ALU.mult).then_inc(self.normed, 1)

    def dve_split(self, dve):
        g = self.g
        for b in range(B):
            for k in range(KT):
                dve.wait_ge(self.split_hi, b * KT + k + 1)
                cols = slice(b * T, (b + 1) * T)
                dve.tensor_tensor(g.hl[:, k, cols], self.hf[:, k, cols], g.hh[:, k, cols].bitcast(F32),
                                  ALU.subtract).then_inc(self.split_lo, 1)

    def act(self, act):
        g = self.g
        for b in range(B):
            h = slice(b * TT, (b + 1) * TT)
            act.wait_ge(self.var_ready, b + 1)
            act.activation(self.std[:, h], self.var[:, h], ACT.Sqrt).then_inc(self.std_ready, 1)
        if self.mod_ready is not None:
            act.wait_ge(*self.mod_ready)
        for b in range(B):
            for k in range(KT):
                act.wait_ge(self.turned, b * KT + k + 1)
                act.activation(self.hf[:, k, b * T:(b + 1) * T], g.bank[k][:, :], ACT.Identity,
                               scale=g.mod[:, self.scale, k * B + b:k * B + b + 1],
                               bias=g.mod[:, self.shift, k * B + b:k * B + b + 1]).then_inc(self.affine, 1)
                if b * KT + k:
                    self.act_hi(act, b * KT + k - 1)
        self.act_hi(act, B * KT - 1)

    def pe(self, pe):
        g = self.g
        for b in range(B):
            pe.wait_ge(self.normed, (b + 1) * TT)
            for k in range(KT):
                if b:
                    pe.wait_ge(self.affine, k + 1)
                for t in range(TT):
                    mm = pe.transpose(g.bank[k][:, t * P:(t + 1) * P],
                                      self.xn[:, b * TT + t, k * P:(k + 1) * P], g.ident[:, :])
                mm.then_inc(self.turned, 1)

    def act_hi(self, act, n):
        b, k = divmod(n, KT)
        cols = slice(b * T, (b + 1) * T)
        act.wait_ge(self.affine, n + 1)
        act.activation(self.g.hh[:, k, cols], self.hf[:, k, cols], ACT.Copy).then_inc(self.split_hi, 1)

    def pool(self, pool):
        g = self.g
        if self.gate is not None:
            for t in range(NT):
                if self.x_in is not None:
                    pool.wait_ge(self.x_in[t], 16)
                pool.wait_ge(self.gated, t + 1)
                pool.tensor_tensor(g.x[:, t, :], g.x[:, t, :], self.xn[:, t, :], ALU.add)\
                    .then_inc(self.summed, 1)



CUTS = {0: (0, 0, 0, 0), 2: (1, 1, 2, 2), 4: (0, 2, 2, 4), 6: (0, 2, 4, 5), 8: (0, 2, 5, 6)}
OUT_AT = (1, 1, 1, 1)
PROJ_AT = ((0, 0), (0, 3), (2, 0), (2, 3), (3, 0))
V_AT = ((1, 0), (1, 4), (2, 4), (3, 2))
STEPS = 2 * B
KINDS = ("S", "T", "PV", "O", "OUT", "PROJ", "V")


def attention_order(more):
    ops = []

    def tail(s, u):
        n = u + 1
        seq = [("T", s, u, 0)] + ([("T", s, u, 1)] if n > 1 else [])
        for j in range(n):
            seq.append(("PV", s, u, j))
            if j + 2 < n:
                seq.append(("T", s, u, j + 2))
        return seq

    for s in range(STEPS):
        extra = {}
        if s + 1 < STEPS or more:
            for x, at in zip((4, 0, 1, 2, 3), PROJ_AT):
                extra.setdefault(at, []).append(("PROJ", s + 1, x))
        if s == 0 or (s == STEPS - 1 and more):
            for t, at in enumerate(V_AT):
                extra.setdefault(at, []).append(("V", 1 if s == 0 else 0, t))
        for u in range(TT):
            before = (s, u - 1) if u else (s - 1, TT - 1)
            rest = tail(*before) if before[0] >= 0 else []
            due = (s, u - 2) if u >= 2 else (s - 1, u + 2)
            if due[0] >= 0:
                extra.setdefault((u, OUT_AT[u]), []).insert(0, ("OUT", *due))
            cuts = CUTS[len(rest)]
            for h, (a, z) in enumerate(zip((0, *cuts), (*cuts, len(rest)))):
                if h < REP:
                    ops.append(("S", s, u, h))
                ops += rest[a:z]
                ops += extra.get((u, h), [])
    s = STEPS - 1
    ops.append(("OUT", s, TT - 2))
    ops += tail(s, TT - 1)
    ops.append(("OUT", s, TT - 1))
    return ops


def late(ops, lags):
    due = [[] for _ in range(len(ops) + 16)]
    for at, op in enumerate(ops):
        for part, lag in lags.get(op[0], ()):
            due[at + lag].append((part, op))
    return [x for place in due for x in place]


def layer0_attention(nc, g, chunks, wv_chunks, rope):
    with ExitStack() as ctx:
        g.sem = semaphores(nc, ctx)
        sb = lambda n, s, t=F32: ctx.enter_context(nc.sbuf_tensor(f"a0_{n}", s, t))
        sem = lambda n: g.sem(f"a0_{n}")
        RAW = 4
        raw = sb("raw", [P, RAW, 512])
        wq = [sb(f"wq_{p}", [P, REP, KT, HD0], F32R) for p in ("hi", "lo")]
        wk = [sb(f"wk_{p}", [P, KT, HD0], F32R) for p in ("hi", "lo")]
        wv = [sb(f"wv_{p}", [P, KT, 2 * HD0], F32R) for p in ("hi", "lo")]
        wo = [sb(f"wo_{p}", [P, REP, D], F32R) for p in ("hi", "lo")]
        v = [sb(f"v_{p}", [P, B, TT, 2 * HD0], F32R) for p in ("hi", "lo")]
        qk = [sb(f"qk_{p}", [P, 2, REP + 1, T], F32R) for p in ("hi", "lo")]
        plain = sb("plain", [P, 2, T])
        by_cos = sb("by_cos", [P, T])
        by_sin = sb("by_sin", [P, T])
        turned = sb("turned", [P, 2, T])
        probs = sb("probs", [P, 2, REP, T])
        pt = [sb(f"pt_{p}", [P, 2, REP * P], F32R) for p in ("hi", "lo")]
        o = [sb(f"o_{p}", [P, 2, REP * P], F32R) for p in ("hi", "lo")]
        table = sb("table", [P, 2, T])
        ring = REP * 2
        negmax = sb("negmax", [P, ring])
        rowsum = sb("rowsum", [P, ring])
        rsum = sb("rsum", [P, ring])
        score_banks, turn_banks, out_bank, mm_banks = g.bank[0:3], g.bank[3:5], g.bank[5], g.bank[6:8]

        raw_in = [sem(f"raw_in{r}") for r in range(RAW)]
        table_in = sem("table_in")
        names = ("raw_hi", "split", "scores", "maxed", "exped", "rsummed", "normed", "turned_mm", "pt_hi_done",
                 "pt_done", "pv", "o_hi_done", "o_done", "out_mm", "zeroed", "proj_mm", "rotated", "roped",
                 "qk_hi_done", "qk_done", "v_mm", "v_hi_done")
        s_ = {n: sem(n) for n in names}
        freed = [sem(f"freed{r}") for r in range(2)]

        full = attention_order(True)
        PER = {k: sum(op[0] == k for op in full) for k in KINDS}
        PER["O"] = STEPS * TT
        MM = ("PROJ", "V", "OUT")
        first_ops = [("PROJ", 0, 4), ("PROJ", 0, 0), ("V", 0, 0), ("PROJ", 0, 1), ("V", 0, 1), ("PROJ", 0, 2),
                     ("V", 0, 2), ("PROJ", 0, 3), ("V", 0, 3)]
        AHEAD = {"PROJ": REP + 1, "V": TT}
        MM_AHEAD = len(first_ops)
        MM_PER = sum(PER[k] for k in MM)

        W_AHEAD = [("K", 0), ("Q", 0), ("Vw", 0), ("Vw", 1), ("Q", 1), ("Q", 2), ("Q", 3)]

        def weight_order(more):
            ops = attention_order(more)
            at = {op: n for n, op in enumerate(ops)}
            out = [(2 + 3 * h, ("O", h), 0) for h in range(REP)]
            for s in (0, 2):
                if s == 0 or more:
                    for x in (4, 0, 1, 2, 3):
                        what = ("K", 0) if x == 4 else ("Q", x)
                        out.append((at["PROJ", s + 1, x] + 4, what, (s // 2 + 1)))
            out += [(at["OUT", 1, TT - 1] + 1 + h, ("O", h), 1) for h in range(REP)]
            if more:
                out += [(at["V", 1, 3] + 8 + n, ("Vw", n), 2) for n in range(2)]
            return sorted(out, key=lambda x: x[0])

        W_PER = len(weight_order(True))

        class Turn:

            def __init__(self, it, more=True, ahead=False):
                self.it, self.ahead, self.more = it, ahead, more
                self.ops = first_ops if ahead else attention_order(more)
                self.n = {}
                seen = {}
                m = -MM_AHEAD if ahead else 0
                for op in self.ops:
                    k = op[0]
                    self.n[op] = seen.get(k, 0)
                    seen[k] = self.n[op] + 1
                    if k == "PV" and op[2] == op[3]:
                        self.n["O", op[1], op[2]] = seen.get("O", 0)
                        seen["O"] = seen.get("O", 0) + 1
                    if k in MM:
                        self.n["MM", op] = m
                        m += 1
                self.weights = ([(0, w, 0) for w in W_AHEAD] if ahead else weight_order(more))
                for n, (_, w, kv) in enumerate(self.weights):
                    self.n["W", w, kv] = n - (len(W_AHEAD) if ahead else 0)

            def before(self, kind):
                if self.ahead:
                    return 0
                return self.it * PER[kind] + AHEAD.get(kind, 0)

            def done(self, *op):
                return self.before(op[0]) + (self.n[op] + 1)

            def bank(self, op):
                return self.n["MM", op] % 2

            def free(self, m):
                r = m % 2
                ahead = (MM_AHEAD + (1 if r else 0)) // 2
                n = m // 2 + 1 + ahead
                return freed[r], (n if self.ahead else self.it * (MM_PER // 2) + n)

            def evacuated(self, op):
                return self.free(self.n["MM", op])

            def chunk_in(self, c):
                r = c % RAW
                ahead = sum(x % RAW == r for x in range(-len(W_AHEAD), 0))
                n = c // RAW + 1 + ahead
                return raw_in[r], (n * 16 if self.ahead else self.it * (W_PER // RAW * 16) + n * 16)

            def split_count(self, c):
                n = c + 1 + len(W_AHEAD)
                return n if self.ahead else self.it * W_PER + n

        assert MM_PER % 2 == 0 and W_PER % RAW == 0 and PER["T"] % 2 == 0

        def project_source(tr, op):
            _, s, x = op
            kv = s // 2
            key = ("K", 0) if x == REP else ("Q", x)
            w = [t[:, :, :] if x == REP else t[:, x, :, :] for t in (wk, wq)[x < REP]]
            return w, key, kv


        def sync_turn(eng, tr):
            for n, (_, (what, which), kv) in enumerate(tr.weights):
                c = tr.n["W", (what, which), kv]
                if not (tr.ahead and c < RAW - len(W_AHEAD)):
                    eng.wait_ge(s_["split"], tr.split_count(c - RAW))
                if tr.ahead:
                    pair = 0
                else:
                    pair = tr.it
                if what == "Vw":
                    src = wv_chunks[(pair + kv // 2) * 2 + which]
                else:
                    row = {"K": 0, "Q": 1, "O": 1 + REP}[what] + which
                    src = chunks[(pair * 2 + kv) * (1 + 2 * REP) + row]
                eng.dma_start(raw[:, c % RAW, :], src).then_inc(raw_in[c % RAW], 16)

        def chunk_views(tr, what, which, kv):
            c = tr.n["W", (what, which), kv]
            dst = {"K": lambda t: t[:, :, :], "Q": lambda t: t[:, which, :, :],
                   "O": lambda t: t[:, which, :], "Vw": lambda t: t[:, 2 * which:2 * which + 2, :]}[what]
            hi, lo = (dst(t) for t in {"K": wk, "Q": wq, "O": wo, "Vw": wv}[what])
            src = raw[:, c % RAW, :]
            if what != "O":
                src = src.rearrange("p (k n) -> p k n", k=2 if what == "Vw" else KT)
            return c, hi, lo, src

        def act_split(eng, tr, what, which, kv):
            c, hi, lo, src = chunk_views(tr, what, which, kv)
            if not tr.ahead:
                if what == "K":
                    eng.wait_ge(s_["proj_mm"], tr.done("PROJ", 2 * kv - 1, REP))
                elif what == "Q":
                    eng.wait_ge(s_["proj_mm"], tr.done("PROJ", 2 * kv - 1, which))
                elif what == "Vw":
                    eng.wait_ge(s_["v_mm"], tr.done("V", 1, TT - 1))
                elif kv == 0:
                    eng.wait_ge(s_["out_mm"], tr.before("OUT"))
                else:
                    eng.wait_ge(s_["out_mm"], tr.done("OUT", 1, TT - 1))
            eng.wait_ge(*tr.chunk_in(c))
            eng.activation(hi, src, ACT.Copy).then_inc(s_["raw_hi"], 1)

        def pool_split(eng, tr, what, which, kv):
            c, hi, lo, src = chunk_views(tr, what, which, kv)
            eng.wait_ge(s_["raw_hi"], tr.split_count(c))
            eng.tensor_tensor(lo, src, hi.bitcast(F32), ALU.subtract).then_inc(s_["split"], 1)

        def rope_slot(tr, op):
            return (tr.n[op] + (0 if tr.ahead else 1)) % 2

        def pool_rope(eng, tr, op):
            eng.wait_ge(s_["rotated"], tr.done(*op))
            if not tr.ahead or tr.n[op] >= 2:
                eng.wait_ge(s_["qk_done"], tr.done(*op) - 2)
            eng.tensor_tensor(turned[:, rope_slot(tr, op), :], by_cos[:, :], by_sin[:, :], ALU.add)\
               .then_inc(s_["roped"], 1)

        def act_rope(eng, tr, op):
            _, s, x = op
            if not tr.ahead:
                eng.wait_ge(s_["scores"], tr.before("S") + (s - 1) * TT * REP)
            eng.wait_ge(s_["roped"], tr.done(*op))
            eng.activation(qk[0][:, s % 2, x, :], turned[:, rope_slot(tr, op), :], ACT.Copy)\
               .then_inc(s_["qk_hi_done"], 1)

        def pool_rope_lo(eng, tr, op):
            _, s, x = op
            eng.wait_ge(s_["qk_hi_done"], tr.done(*op))
            eng.tensor_tensor(qk[1][:, s % 2, x, :], turned[:, rope_slot(tr, op), :],
                              qk[0][:, s % 2, x, :].bitcast(F32), ALU.subtract).then_inc(s_["qk_done"], 1)

        def with_weights(tr, pieces):
            items = [(at, 1, part, op) for at, part, op in pieces]
            items += [(n, 0, "split", w) for n, *w in tr.weights]
            return [x[2:] for x in sorted(items, key=lambda x: x[:2])]

        def pool_turn(eng, tr):
            work = [(n + lag, part, op) for n, op in enumerate(tr.ops) if op[0] == "PROJ"
                    for part, lag in (("rope", 2), ("lo", 5))]
            for part, op in with_weights(tr, work):
                if part == "split":
                    pool_split(eng, tr, *op[0], op[1])
                elif part == "rope":
                    pool_rope(eng, tr, op)
                else:
                    pool_rope_lo(eng, tr, op)

        def pe_turn(eng, tr):
            for op in tr.ops:
                kind = op[0]
                if kind in MM:
                    m = tr.n["MM", op]
                    bank = mm_banks[m % 2]
                    if not (tr.ahead and m < 2 - MM_AHEAD):
                        eng.wait_ge(*tr.free(m - 2))
                if kind == "PROJ":
                    _, s, x = op
                    b = s % B
                    w, key, kv = project_source(tr, op)
                    if tr.ahead:
                        eng.wait_ge(s_["split"], tr.split_count(tr.n["W", key, 0]))
                    elif s > 1:
                        eng.wait_ge(s_["split"], tr.split_count(tr.n["W", key, kv]))
                    cols = slice(b * T, (b + 1) * T)
                    for k in range(KT):
                        mm = three_passes(eng, bank[:, :], [t[:, k, :] for t in w],
                                          [t[:, k, cols] for t in (g.hh, g.hl)], k, k == 0, k == KT - 1)
                    mm.then_inc(s_["proj_mm"], 1)
                elif kind == "V":
                    _, b, t = op
                    if tr.ahead:
                        eng.wait_ge(s_["split"], tr.split_count(tr.n["W", ("Vw", 1), 0]))
                    elif b == 0:
                        eng.wait_ge(s_["split"], tr.split_count(tr.n["W", ("Vw", 1), 2]))
                    cols = slice(b * T + t * P, b * T + (t + 1) * P)
                    for k in range(KT):
                        mm = three_passes(eng, bank[:, 0:2 * HD0], [x[:, k, cols] for x in (g.hh, g.hl)],
                                          [x[:, k, :] for x in wv], k, k == 0, k == KT - 1)
                    mm.then_inc(s_["v_mm"], 1)
                elif kind == "OUT":
                    _, s, u = op
                    eng.wait_ge(s_["o_done"], tr.before("O") + tr.n["O", s, u] + 1)
                    eng.wait_ge(s_["split"], tr.split_count(tr.n["W", ("O", REP - 1), s // 2]))
                    slot = tr.n["O", s, u] % 2
                    for h in range(REP):
                        mm = three_passes(eng, bank[:, :], [t[:, slot, h * P:(h + 1) * P] for t in o],
                                          [t[:, h, :] for t in wo], h, h == 0, h == REP - 1)
                    mm.then_inc(s_["out_mm"], 1)
                elif kind == "S":
                    _, s, u, h = op
                    n = tr.n[op]
                    eng.wait_ge(s_["exped"], tr.before("S") + max(n - 2, 0))
                    if s == 0:
                        if u == 0 and h == 0:
                            eng.wait_ge(s_["qk_done"], tr.before("PROJ"))
                    elif u == 0:
                        eng.wait_ge(s_["qk_done"], tr.done("PROJ", s, h))
                    width = max(2 * P, (u + 1) * P)
                    q = [t[:, s % 2, h, u * P:(u + 1) * P] for t in qk]
                    kk = [t[:, s % 2, REP, 0:width] for t in qk]
                    bank = score_banks[n % 3]
                    three_passes(eng, bank[:, 0:width], q, kk, 0, True, False)
                    eng.matmul(bank[:, u * P:(u + 1) * P], g.eye16[:, :], g.mask[:, :], start=False, stop=True)\
                       .then_inc(s_["scores"], 1)
                elif kind == "T":
                    _, s, u, j = op
                    n = tr.n[op]
                    if j == 0:
                        eng.wait_ge(s_["normed"], tr.done("S", s, u, REP - 1))
                    eng.wait_ge(s_["pt_done"], tr.before("T") + max(n - 1, 0))
                    unit = s * TT + u
                    for h in range(REP):
                        mm = eng.transpose(turn_banks[n % 2][:, h * P:(h + 1) * P],
                                           probs[:, unit % 2, h, j * P:(j + 1) * P], g.ident[:, :])
                    mm.then_inc(s_["turned_mm"], 1)
                elif kind == "PV":
                    _, s, u, j = op
                    slot = tr.n["T", s, u, j] % 2
                    b, kv = s % B, s // 2
                    eng.wait_ge(s_["pt_done"], tr.done("T", s, u, j))
                    if j == 0:
                        if u == 0 and s == 0:
                            eng.wait_ge(*tr.free(-2))
                            eng.wait_ge(*tr.free(-1))
                        elif u == 0 and s == 1:
                            eng.wait_ge(*tr.evacuated(("V", 1, TT - 2)))
                            eng.wait_ge(*tr.evacuated(("V", 1, TT - 1)))
                        eng.wait_ge(s_["o_done"], tr.before("O") + tr.n["O", s, u])
                    three_passes(eng, out_bank[:, :], [t[:, b, j, kv * HD0:(kv + 1) * HD0] for t in v],
                                 [t[:, slot, :] for t in pt], 0, j == 0, j == u).then_inc(s_["pv"], 1)

        def act_turn(eng, tr):
            lags = {"S": [("exp", 0)], "T": [("hi", 0)], "PV": [("hi", 0)],
                    "PROJ": [("copy", 0), ("turned", 4)], "V": [("hi", 0)]}
            pieces = sorted((n + lag, m, part, op) for n, op in enumerate(tr.ops)
                            for m, (part, lag) in enumerate(lags.get(op[0], ())))
            for part, op in with_weights(tr, [(n, part, op) for n, _, part, op in pieces]):
                kind = op[0]
                if part == "split":
                    act_split(eng, tr, *op[0], op[1])
                elif part == "turned":
                    act_rope(eng, tr, op)
                elif kind == "PROJ":
                    n, slot = tr.n[op], rope_slot(tr, op)
                    eng.wait_ge(s_["proj_mm"], tr.done(*op))
                    if not (tr.ahead and n < 2):
                        eng.wait_ge(s_["rotated"], tr.done(*op) - 2)
                    eng.activation(plain[:, slot, :], mm_banks[tr.bank(op)][:, :], ACT.Copy,
                                   scale=float(HD0) ** -0.5 if op[2] < REP else 1.0)\
                       .then_inc(freed[tr.bank(op)], 1)
                elif kind == "V":
                    _, b, t = op
                    eng.wait_ge(s_["v_mm"], tr.done(*op))
                    if not tr.ahead:
                        eng.wait_ge(s_["pv"], tr.done("PV", 2, TT - 1, TT - 1) if b == 0 else tr.before("PV"))
                    eng.activation(v[0][:, b, t, :], mm_banks[tr.bank(op)][:, 0:2 * HD0], ACT.Copy)\
                       .then_inc(s_["v_hi_done"], 1)
                elif kind == "S":
                    _, s, u, h = op
                    n, unit = tr.n[op], s * TT + u
                    w = (u + 1) * P
                    eng.wait_ge(s_["maxed"], tr.done(*op))
                    if h == 0:
                        if unit >= 2:
                            s2, u2 = divmod(unit - 2, TT)
                            eng.wait_ge(s_["turned_mm"], tr.done("T", s2, u2, u2))
                        else:
                            eng.wait_ge(s_["turned_mm"], tr.before("T"))
                    eng.activation(probs[:, unit % 2, h, 0:w], score_banks[n % 3][:, 0:w], ACT.Exp,
                                   bias=negmax[:, n % ring:n % ring + 1],
                                   accum_out=rowsum[:, n % ring:n % ring + 1]).then_inc(s_["exped"], 1)
                elif kind == "T":
                    n = tr.n[op]
                    eng.wait_ge(s_["turned_mm"], tr.done(*op))
                    if n >= 2:
                        eng.wait_ge(s_["pv"], tr.before("PV") + (n - 1))
                    else:
                        eng.wait_ge(s_["pv"], tr.before("PV"))
                    eng.activation(pt[0][:, n % 2, :], turn_banks[n % 2][:, :], ACT.Copy)\
                       .then_inc(s_["pt_hi_done"], 1)
                elif kind == "PV" and op[2] == op[3]:
                    k = tr.n["O", op[1], op[2]]
                    eng.wait_ge(s_["pv"], tr.done(*op))
                    eng.wait_ge(s_["out_mm"], tr.before("OUT") + max(k - 1, 0))
                    eng.activation(o[0][:, k % 2, :], out_bank[:, :], ACT.Copy).then_inc(s_["o_hi_done"], 1)

        def dve_turn(eng, tr):
            lags = {"S": [("max", 1), ("norm", 3)], "T": [("lo", 1)], "PV": [("lo", 3)],
                    "PROJ": [("rotate", 3)],
                    "V": [("lo", 3)], "OUT": [("add", 4)]}
            for part, op in late(tr.ops, lags):
                kind = op[0]
                if kind == "PROJ":
                    n, slot = tr.n[op], rope_slot(tr, op)
                    eng.wait_ge(*tr.evacuated(op))
                    if not (tr.ahead and n == 0):
                        eng.wait_ge(s_["roped"], tr.done(*op) - 1)
                    half = HD0 // 2
                    eng.tensor_tensor(by_cos[:, :], plain[:, slot, :], table[:, 0, :], ALU.mult)
                    for a, z in ((0, half), (half, 0)):
                        last = eng.tensor_tensor(by_sin[z:z + half, :], plain[a:a + half, slot, :],
                                                 table[a:a + half, 1, :], ALU.mult)
                    last.then_inc(s_["rotated"], 1)
                elif kind == "V":
                    _, b, t = op
                    eng.wait_ge(s_["v_hi_done"], tr.done(*op))
                    eng.tensor_tensor(v[1][:, b, t, :], mm_banks[tr.bank(op)][:, 0:2 * HD0],
                                      v[0][:, b, t, :].bitcast(F32), ALU.subtract)\
                       .then_inc(freed[tr.bank(op)], 1)
                elif part == "max":
                    _, s, u, h = op
                    n = tr.n[op]
                    eng.wait_ge(s_["scores"], tr.done(*op))
                    eng.tensor_reduce(negmax[:, n % ring:n % ring + 1], score_banks[n % 3][:, 0:(u + 1) * P],
                                      AX_X, ALU.max, negate=True).then_inc(s_["maxed"], 1)
                elif part == "norm":
                    _, s, u, h = op
                    n, unit = tr.n[op], s * TT + u
                    eng.wait_ge(s_["exped"], tr.done(*op))
                    eng.reciprocal(rsum[:, n % ring:n % ring + 1], rowsum[:, n % ring:n % ring + 1])\
                       .then_inc(s_["rsummed"], 1)
                    eng.wait_ge(s_["rsummed"], tr.done(*op))
                    p_ = probs[:, unit % 2, h, 0:(u + 1) * P]
                    eng.tensor_scalar(p_, p_, rsum[:, n % ring:n % ring + 1], None, ALU.mult)\
                       .then_inc(s_["normed"], 1)
                elif kind == "T":
                    n = tr.n[op]
                    eng.wait_ge(s_["pt_hi_done"], tr.done(*op))
                    eng.tensor_tensor(pt[1][:, n % 2, :], turn_banks[n % 2][:, :], pt[0][:, n % 2, :].bitcast(F32),
                                      ALU.subtract).then_inc(s_["pt_done"], 1)
                elif kind == "PV" and op[2] == op[3]:
                    k = tr.n["O", op[1], op[2]]
                    eng.wait_ge(s_["o_hi_done"], tr.before("O") + (k + 1))
                    eng.tensor_tensor(o[1][:, k % 2, :], out_bank[:, :], o[0][:, k % 2, :].bitcast(F32),
                                      ALU.subtract).then_inc(s_["o_done"], 1)
                elif kind == "OUT":
                    _, s, u = op
                    y = g.y[:, (s % B) * TT + u, :]
                    eng.wait_ge(s_["out_mm"], tr.done(*op))
                    eng.wait_ge(*(tr.evacuated(("OUT", s - 2, u)) if s >= 2 else tr.free(-1)))
                    eng.tensor_tensor(y, mm_banks[tr.bank(op)][:, :], y, ALU.add)\
                       .then_inc(freed[tr.bank(op)], 1)

        def turns(eng, body):
            body(eng, Turn(-1, ahead=True))
            body(eng, Turn(0))
            with eng.Fori(1, PAIRS - 1) as it:
                body(eng, Turn(it))
            body(eng, Turn(PAIRS - 1, more=False))

        block = ctx.enter_context(nc.Block())

        @block.sync
        def _(sync):
            sync.dma_start(table[:, :, :], rope).then_inc(table_in, 16)
            turns(sync, sync_turn)

        @block.gpsimd
        def _(pool):
            turns(pool, pool_turn)

        @block.tensor
        def _(pe):
            turns(pe, pe_turn)

        @block.scalar
        def _(act):
            turns(act, act_turn)

        @block.vector
        def _(dve):
            dve.memset(g.y[:, :, :], 0.0).then_inc(s_["zeroed"], 1)
            dve.wait_ge(s_["zeroed"], 1)
            dve.wait_ge(table_in, 16)
            turns(dve, dve_turn)



class Router:

    def __init__(self, nc, ctx, g, norm, bank, w, b, bias, descend):
        sb = lambda n, s: ctx.enter_context(nc.sbuf_tensor(f"r_{n}", s, F32))
        sem = lambda n: g.sem(f"r_{n}")
        self.g, self.norm, self.bank = g, norm, bank
        self.srcs = (w, b, bias, descend)
        self.w = sb("w", [P, KT, E0])
        self.b, self.bias, self.descend = (sb(n, [P, E0]) for n in ("b", "bias", "descend"))
        self.e, self.p, self.q, self.hit, self.kept = (sb(n, [P, NT, E0]) for n in ("e", "p", "q", "hit", "kept"))
        self.one, self.two = sb("one", [P, NT]), sb("two", [P, NT])
        self.gmax, self.keep, self.ghit, self.gq = (sb(n, [P, NT, GROUPS]) for n in ("gmax", "keep", "ghit", "gq"))
        self.loaded, self.logits, self.chain, self.shifted, self.exped = (
            sem(n) for n in ("loaded", "logits", "chain", "shifted", "exped"))

    def load(self, eng):
        for dst, src in zip((self.w[:, :, :], self.b[:, :], self.bias[:, :], self.descend[:, :]), self.srcs):
            eng.dma_start(dst, src).then_inc(self.loaded, 16)

    def pe(self, pe):
        pe.wait_ge(self.loaded, 64)
        for t in range(NT):
            if t % TT == 0:
                pe.wait_ge(self.norm.affine, (t // TT + 1) * KT)
            for k in range(KT):
                mm = pe.matmul(self.bank[:, t * E0:(t + 1) * E0], self.norm.hf[:, k, t * P:(t + 1) * P],
                               self.w[:, k, :], start=(k == 0), stop=(k == KT - 1))
        mm.then_inc(self.logits, 1)

    def act(self, act):
        act.wait_ge(self.shifted, 1)
        act.activation(self.e[:, :, :], self.e[:, :, :], ACT.Exp).then_inc(self.exped, 1)

    def dve(self, dve):
        g = self.g
        link = Chain(dve, self.chain)
        over = lambda x, n: x.unsqueeze(2).to_broadcast([P, NT, n])
        each = lambda x, n: x.unsqueeze(1).to_broadcast([P, NT, n])
        dve.wait_ge(self.logits, 1)
        dve.wait_ge(self.loaded, 64)
        link(dve.tensor_tensor(self.e[:, :, :], self.bank[:, 0:NT * E0].rearrange("p (t e) -> p t e", e=E0),
                               each(self.b[:, :], E0), ALU.add))
        link(dve.tensor_reduce(self.one[:, :], self.e[:, :, :], AX_X, ALU.max))
        dve.tensor_tensor(self.e[:, :, :], self.e[:, :, :], over(self.one[:, :], E0), ALU.subtract)\
           .then_inc(self.shifted, 1)
        dve.wait_ge(self.exped, 1)
        link(dve.tensor_reduce(self.one[:, :], self.e[:, :, :], AX_X, ALU.add))
        link(dve.reciprocal(self.two[:, :], self.one[:, :]))
        link(dve.tensor_tensor(self.p[:, :, :], self.e[:, :, :], over(self.two[:, :], E0), ALU.mult))
        link(dve.tensor_tensor(self.p[:, :, :], self.p[:, :, :], each(self.bias[:, :], E0), ALU.add))

        def best_two(values, work, hit, kept, n):
            for turn in range(2):
                src = values if turn == 0 else work
                link(dve.tensor_reduce(self.one[:, :], src, AX_X, ALU.max))
                link(dve.tensor_tensor(hit, src, over(self.one[:, :], n), ALU.is_equal))
                link(dve.tensor_tensor(hit, hit, each(self.descend[:, 0:n], n), ALU.mult))
                link(dve.tensor_reduce(self.two[:, :], hit, AX_X, ALU.max))
                link(dve.tensor_tensor(hit, hit, over(self.two[:, :], n), ALU.is_equal))
                if turn == 0:
                    link(dve.tensor_copy(kept, hit))
                    link(dve.scalar_tensor_tensor(out=work, in0=hit, scalar=NEG, in1=src,
                                                  op0=ALU.mult, op1=ALU.add))
                else:
                    link(dve.tensor_tensor(kept, kept, hit, ALU.add))

        link(dve.tensor_reduce(self.gmax[:, :, :].rearrange("p t a -> p (t a)"),
                               self.p[:, :, :].rearrange("p t (a e) -> p (t a) e", a=GROUPS), AX_X, ALU.max))
        best_two(self.gmax[:, :, :], self.gq[:, :, :], self.ghit[:, :, :], self.keep[:, :, :], GROUPS)
        wide = self.keep[:, :, :].rearrange("p t a -> p (t a)").unsqueeze(2).to_broadcast(
            [P, NT * GROUPS, E0 // GROUPS])
        by_group = lambda x: x[:, :, :].rearrange("p t (a e) -> p (t a) e", a=GROUPS)
        link(dve.tensor_tensor(by_group(self.q), by_group(self.p), wide, ALU.mult))
        link(dve.tensor_scalar(self.keep[:, :, :], self.keep[:, :, :], -1.0, -NEG, ALU.add, ALU.mult))
        link(dve.tensor_tensor(by_group(self.q), by_group(self.q), wide, ALU.add))
        best_two(self.q[:, :, :], self.q[:, :, :], self.hit[:, :, :], self.kept[:, :, :], E0)
        link(dve.tensor_tensor(g.gates[:, :, 0:E0], self.p[:, :, :], self.kept[:, :, :], ALU.mult))
        link(dve.memset(g.gates[:, :, E0:EX], 1.0))


def layer0_experts(nc, g, chunks, biases, b3, next_c, next_wmod):
    with ExitStack() as ctx:
        g.sem = semaphores(nc, ctx)
        sb = lambda n, s, t=F32: ctx.enter_context(nc.sbuf_tensor(f"e0_{n}", s, t))
        sem = lambda n: g.sem(f"e0_{n}")
        TURNS, RAW, CH = EX // 2, 3, 3
        raw = sb("raw", [P, RAW, 512])
        w12 = [sb(f"w12_{p}", [P, 2, 2, KT, INTER], F32R) for p in ("hi", "lo")]
        w3 = [sb(f"w3_{p}", [P, 2, D], F32R) for p in ("hi", "lo")]
        bias = sb("bias", [P, EX, 2])
        bias_now = sb("bias_now", [P, 2, 2])
        gate_now = sb("gate_now", [P, NT, 2])
        b3_rows = sb("b3", [EX, D])
        gates_t = sb("gates_t", [EX, NT * P])
        silu = sb("silu", [P, B, T])
        prod = sb("prod", [P, B, T])
        pr = [sb(f"prod_{p}", [P, B, T], F32R) for p in ("hi", "lo")]
        raw_in = [sem(f"raw_in{r}") for r in range(RAW)]
        names = ("small_in", "raw_hi", "split", "turned", "turned_sb", "up_mm", "silu_done", "prod_done", "prod_hi",
                 "prod_lo", "down_mm", "added", "bias_set", "gate_set")
        s_ = {n: sem(n) for n in names}
        mod = Modulation(nc, ctx, g, "m1", next_c, next_wmod, g.bank[0:4])
        MOD_CHUNKS = 6 * KT // (TURNS - 1)
        assert MOD_CHUNKS * (TURNS - 1) == 6 * KT
        UPS, DOWNS = 2 * B, 2 * NT
        every, half = range(TT), TT // 2
        order = [("H", 0, 0, None), ("H", 0, 1, None), ("Y", 0, 0, every), ("H", 1, 0, None), ("Y", 0, 1, range(half)),
                 ("H", 1, 1, None), ("Y", 0, 1, range(half, TT)), ("Y", 1, 0, every), ("Y", 1, 1, every)]

        def tiles(p, b, ts):
            return [((p * B + b) * TT + t, b * TT + t) for t in ts]

        def load_expert(eng, row, n, first):
            for c in range(CH):
                if not first:
                    eng.wait_ge(s_["split"], (n - 1) * CH + (c + 1))
                eng.dma_start(raw[:, c, :], chunks[row * CH + c]).then_inc(raw_in[c], 16)

        def views(p, c):
            if c < 2:
                return *(t[:, p, c, :, :] for t in w12), raw[:, c, :].rearrange("p (k n) -> p k n", k=KT)
            return *(t[:, p, :] for t in w3), raw[:, c, :]

        def hi_expert(act, p, n, used, chunks=range(CH)):
            for c in chunks:
                used(act, c)
                act.wait_ge(raw_in[c], (n + 1) * 16)
                hi, _, src = views(p, c)
                act.activation(hi, src, ACT.Copy).then_inc(s_["raw_hi"], 1)

        def lo_expert(pool, p, n):
            for c in range(CH):
                hi, lo, src = views(p, c)
                pool.wait_ge(s_["raw_hi"], n * CH + (c + 1))
                pool.tensor_tensor(lo, src, hi.bitcast(F32), ALU.subtract).then_inc(s_["split"], 1)

        def hi_product(act, it, p, b):
            act.wait_ge(s_["prod_done"], it * UPS + (p * B + b + 1))
            if p:
                act.wait_ge(s_["down_mm"], it * DOWNS + ((p - 1) * B + b + 1) * TT)
            else:
                act.wait_ge(s_["down_mm"], it * DOWNS)
            act.activation(pr[0][:, b, :], prod[:, b, :], ACT.Copy).then_inc(s_["prod_hi"], 1)

        def lo_product(dve, it, p, b):
            dve.wait_ge(s_["prod_hi"], it * UPS + (p * B + b + 1))
            dve.tensor_tensor(pr[1][:, b, :], prod[:, b, :], pr[0][:, b, :].bitcast(F32), ALU.subtract)\
               .then_inc(s_["prod_lo"], 1)

        def pool_turn(pool, it, more):
            pool.wait_ge(s_["silu_done"], it * UPS)
            pool.wait_ge(s_["prod_done"], it * UPS)
            pool.wait_ge(s_["small_in"], 32)
            passed(pool, g)
            pool.tensor_copy(bias_now[:, :, :], bias[:, bass.ds(it * 2, 2), :]).then_inc(s_["bias_set"], 1)
            lo_expert(pool, 1, it * 2 + 1)
            if more:
                lo_expert(pool, 0, it * 2 + 2)

        def pe_turn(eng, it, more):
            for kind, p, b, ts in order:
                if kind == "H":
                    n = it * UPS + (p * B + b)
                    if b == 0:
                        eng.wait_ge(s_["split"], it * 2 * CH + (p * CH + 2))
                    if p:
                        eng.wait_ge(s_["prod_done"], n - 1)
                    else:
                        eng.wait_ge(s_["prod_done"], it * UPS)
                    if not more and p == 0:
                        eng.wait_ge(mod.chain, 4)
                    cols = slice(b * T, (b + 1) * T)
                    for c in range(2):
                        for k in range(KT):
                            mm = three_passes(eng, g.bank[2 * b + c][:, :], [t[:, p, c, k, :] for t in w12],
                                              [t[:, k, cols] for t in (g.hh, g.hl)], k, k == 0, k == KT - 1)
                    mm.then_inc(s_["up_mm"], 1)
                else:
                    if b == 0:
                        eng.wait_ge(s_["split"], it * 2 * CH + (p + 1) * CH)
                    eng.wait_ge(s_["prod_lo"], it * UPS + (p * B + b + 1))
                    for (k, t) in tiles(p, b, ts):
                        eng.wait_ge(s_["added"], it * DOWNS + (k + NT - 3))
                        three_passes(eng, g.bank[4 + t % 4][:, :], [x[:, b, (t % TT) * P:(t % TT + 1) * P] for x in pr],
                                     [x[:, p, :] for x in w3], 0, True, True).then_inc(s_["down_mm"], 1)

        def act_turn(act, it, more):
            def used_second(eng, c):
                eng.wait_ge(*((s_["up_mm"], it * UPS) if c < 2 else (s_["down_mm"], it * DOWNS)))

            def used_first(eng, c):
                eng.wait_ge(*((s_["up_mm"], it * UPS + B) if c < 2 else (s_["down_mm"], it * DOWNS + NT)))

            def silu_of(p, b):
                act.wait_ge(s_["up_mm"], it * UPS + (p * B + b + 1))
                if p:
                    act.wait_ge(s_["prod_done"], it * UPS + (b + 1))
                else:
                    act.wait_ge(s_["prod_done"], it * UPS)
                act.activation(silu[:, b, :], g.bank[2 * b][:, :], ACT.Silu, bias=bias_now[:, p, 0:1])\
                   .then_inc(s_["silu_done"], 1)

            act.wait_ge(s_["bias_set"], it + 1)
            hi_expert(act, 1, it * 2 + 1, used_second)
            silu_of(0, 0)
            hi_product(act, it, 0, 0)
            silu_of(0, 1)
            hi_product(act, it, 0, 1)
            silu_of(1, 0)
            hi_product(act, it, 1, 0)
            if more:
                hi_expert(act, 0, it * 2 + 2, used_first, (0, 1))
            silu_of(1, 1)
            hi_product(act, it, 1, 1)
            if more:
                hi_expert(act, 0, it * 2 + 2, used_first, (2,))

        def dve_turn(eng, it, more):
            eng.wait_ge(s_["added"], it * DOWNS + NT)
            eng.tensor_copy(gate_now[:, :, :], g.gates[:, :, bass.ds(it * 2, 2)]).then_inc(s_["gate_set"], 1)
            eng.wait_ge(s_["gate_set"], it + 1)
            eng.wait_ge(s_["bias_set"], it + 1)
            for kind, p, b, ts in order:
                if kind == "H":
                    n = it * UPS + (p * B + b)
                    eng.wait_ge(s_["silu_done"], n + 1)
                    if p:
                        eng.wait_ge(s_["prod_lo"], n - 1)
                    else:
                        eng.wait_ge(s_["prod_lo"], it * UPS)
                    eng.scalar_tensor_tensor(out=prod[:, b, :], in0=g.bank[2 * b + 1][:, :],
                                             scalar=bias_now[:, p, 1:2], in1=silu[:, b, :],
                                             op0=ALU.add, op1=ALU.mult).then_inc(s_["prod_done"], 1)
                    if (p, b) != (1, 1):
                        lo_product(eng, it, p, b)
                else:
                    for (k, t) in tiles(p, b, ts):
                        eng.wait_ge(s_["down_mm"], it * DOWNS + (k + 1))
                        eng.wait_ge(s_["added"], it * DOWNS + (k + 1))
                        eng.scalar_tensor_tensor(out=g.y[:, t, :], in0=g.bank[4 + t % 4][:, :],
                                                 scalar=gate_now[:, t, p:p + 1], in1=g.y[:, t, :],
                                                 op0=ALU.mult, op1=ALU.add).then_inc(s_["added"], 1)
                    if (p, b) == (0, 1) and ts[0] == half:
                        lo_product(eng, it, 1, 1)

        def turns(eng, body, between=lambda n: None):
            body(eng, 0, True)
            between(0)
            with eng.Fori(1, TURNS - 1) as it:
                body(eng, it, True)
            between(1)
            body(eng, TURNS - 1, False)

        block = ctx.enter_context(nc.Block())

        @block.sync
        def _(sync):
            sync.dma_start(bias[:, :, :], biases).then_inc(s_["small_in"], 16)
            sync.dma_start(b3_rows[:, :], b3).then_inc(s_["small_in"], 16)
            load_expert(sync, 0, 0, True)

            def body(eng, it, more):
                load_expert(eng, it * 2 + 1, it * 2 + 1, False)
                if more:
                    load_expert(eng, it * 2 + 2, it * 2 + 2, False)
                    for c in range(MOD_CHUNKS):
                        mod.load_chunk(eng, it * MOD_CHUNKS + c)
            turns(sync, body)

        @block.gpsimd
        def _(pool):
            lo_expert(pool, 0, 0)
            turns(pool, pool_turn)

        @block.tensor
        def _(pe):
            for t in range(NT):
                mm = pe.transpose(g.bank[t // TT][0:EX, (t % TT) * P:(t % TT + 1) * P], g.gates[:, t, :],
                                  g.ident[:, :])
            mm.then_inc(s_["turned"], 1)
            pe.wait_ge(s_["turned_sb"], 2)
            pe.wait_ge(s_["small_in"], 32)
            for t in range(NT):
                if t >= TT:
                    pe.wait_ge(s_["added"], t - TT + 1)
                pe.matmul(g.bank[4 + t % 4][:, :], gates_t[:, t * P:(t + 1) * P], b3_rows[:, :],
                          start=True, stop=True).then_inc(s_["turned"], 1)

            def modulate(n):
                if n:
                    pe.wait_ge(s_["prod_done"], (TURNS - 1) * UPS)
                    mod.pe_rows(pe, range(4), chunkwise=True)
                    mod.pe_columns(pe, (0, 1))
                    mod.pe_rows(pe, (4, 5), chunkwise=True)
                    mod.pe_columns(pe, (4, 5))
            turns(pe, pe_turn, modulate)

        @block.scalar
        def _(act):
            mod.load_c(act)
            hi_expert(act, 0, 0, lambda eng, c: None)

            turns(act, act_turn, lambda n: mod.act(act) if n else None)

        @block.vector
        def _(dve):
            dve.wait_ge(s_["turned"], 1)
            for n in range(2):
                dve.tensor_copy(gates_t[:, n * TT * P:(n + 1) * TT * P], g.bank[n][0:EX, :])\
                   .then_inc(s_["turned_sb"], 1)
            for t in range(NT):
                dve.wait_ge(s_["turned"], t + 2)
                dve.tensor_copy(g.y[:, t, :], g.bank[4 + t % 4][:, :]).then_inc(s_["added"], 1)

            def modulate(n):
                if n:
                    mod.dve_rows(dve, range(4))
                    mod.dve_columns(dve, 0)
                    mod.dve_rows(dve, (4, 5))
                    mod.dve_columns(dve, 1)
                    mod.dve_gates(dve, g.gate1)
            turns(dve, dve_turn, modulate)



SLOT = 64


class Weights:

    def __init__(self, nc, ctx, g, name, items, ring):
        self.items, self.ring = items, ring
        self.raw = ctx.enter_context(nc.sbuf_tensor(f"{name}_raw", [P, ring, 512], F32))
        self.raw_in = [g.sem(f"{name}_raw_in{r}") for r in range(ring)]
        self.hi_done, self.split = g.sem(f"{name}_hi_done"), g.sem(f"{name}_split")

    def load(self, sync):
        for n, (src, _, _) in enumerate(self.items):
            if n >= self.ring:
                sync.wait_ge(self.split, n - self.ring + 1)
            sync.dma_start(self.raw[:, n % self.ring, :], src).then_inc(self.raw_in[n % self.ring], 16)

    def act(self, act, ns):
        for n in ns:
            act.wait_ge(self.raw_in[n % self.ring], (n // self.ring + 1) * 16)
            act.activation(self.items[n][1], self.raw[:, n % self.ring, :], ACT.Copy).then_inc(self.hi_done, 1)

    def pool(self, pool, ns):
        for n in ns:
            _, hi, lo = self.items[n]
            pool.wait_ge(self.hi_done, n + 1)
            pool.tensor_tensor(lo, self.raw[:, n % self.ring, :], hi.bitcast(F32), ALU.subtract).then_inc(self.split, 1)


def layer1_projections(nc, g, weights, rope1):
    with ExitStack() as ctx:
        g.sem = semaphores(nc, ctx)
        sb = lambda n, s, t=F32: ctx.enter_context(nc.sbuf_tensor(f"p1_{n}", s, t))
        sem = lambda n: g.sem(f"p1_{n}")
        rows = GateRows(nc, ctx, g, "rows1", g.gate0, (1,), g.bank[6:8])
        norm = Norm(nc, ctx, g, "n2", 1, 0, gate=rows, hf=g.q1[:, :, :].rearrange("p (k a) d -> p k (a d)", k=KT))
        w = [sb(f"w_{p}", [P, 3, KT, D], F32R) for p in ("hi", "lo")]
        chunks = Weights(nc, ctx, g, "p1", [(weights[c * KT + k], w[0][:, c, k, :], w[1][:, c, k, :])
                                            for c in range(3) for k in range(KT)], 4)
        trig = sb("trig", [P, 2, 2, TT])
        by_cos, by_sin = (sb(n, [P, 2, D]) for n in ("by_cos", "by_sin"))
        s_ = {n: sem(n) for n in ("trig_in", "mm", "cos_done", "even", "odd", "ones")}
        freed = [sem(f"freed{r}") for r in range(4)]
        pieces = [(t, c) for b in range(B) for c in range(3) for t in range(b * TT, (b + 1) * TT)]
        rotated = [(t, c) for t, c in pieces if c < 2]
        block = ctx.enter_context(nc.Block())

        @block.sync
        def _(sync):
            sync.dma_start(trig[:, :, :, :], rope1).then_inc(s_["trig_in"], 16)
            chunks.load(sync)

        @block.gpsimd
        def _(pool):
            norm.pool(pool)
            chunks.pool(pool, range(3 * KT))
            pool.wait_ge(norm.split_lo, B * KT)
            pair = lambda x: x.rearrange("p (i two) -> p i two", two=2)
            for n, (t, c) in enumerate(rotated):
                dst = pair((g.q1 if c == 0 else g.k1)[:, t, :])
                cos, sin = pair(by_cos[:, n % 2, :]), pair(by_sin[:, n % 2, :])
                pool.wait_ge(s_["cos_done"], n + 1)
                m = pieces.index((t, c))
                pool.wait_ge(freed[m % 4], m // 4 + 1)
                pool.tensor_tensor(dst[:, :, 0], cos[:, :, 0], sin[:, :, 1], ALU.subtract).then_inc(s_["even"], 1)
                pool.tensor_tensor(dst[:, :, 1], cos[:, :, 1], sin[:, :, 0], ALU.add).then_inc(s_["odd"], 1)

        @block.tensor
        def _(pe):
            rows.pe(pe)
            norm.pe(pe)
            for n, (t, c) in enumerate(pieces):
                if t % TT == 0:
                    pe.wait_ge(norm.split_lo, (t // TT + 1) * KT)
                    pe.wait_ge(chunks.split, (c + 1) * KT)
                if n >= 4:
                    pe.wait_ge(freed[n % 4], n // 4)
                for k in range(KT):
                    mm = three_passes(pe, g.bank[4 + n % 4][:, :], [x[:, k, t * P:(t + 1) * P] for x in (g.hh, g.hl)],
                                      [x[:, c, k, :] for x in w], k, k == 0, k == KT - 1)
                mm.then_inc(s_["mm"], 1)

        @block.scalar
        def _(act):
            chunks.act(act, range(KT))
            norm.act(act)
            chunks.act(act, range(KT, 3 * KT))
            act.wait_ge(s_["trig_in"], 16)
            for n, (t, c) in enumerate(pieces):
                if c == 2:
                    continue
                r = rotated.index((t, c))
                act.wait_ge(s_["mm"], n + 1)
                if r >= 2:
                    act.wait_ge(s_["odd"], r - 1)
                act.activation(by_cos[:, r % 2, :], g.bank[4 + n % 4][:, :], ACT.Copy,
                               scale=trig[:, c, 0, t % TT:t % TT + 1]).then_inc(s_["cos_done"], 1)

        @block.vector
        def _(dve):
            rows.dve(dve)
            norm.dve_stats(dve)
            norm.dve_split(dve)
            dve.memset(g.v1[:, :, :, HD1:VW], 1.0).then_inc(s_["ones"], 1)
            dve.wait_ge(s_["trig_in"], 16)
            for n, (t, c) in enumerate(pieces):
                bank = g.bank[4 + n % 4]
                dve.wait_ge(s_["mm"], n + 1)
                if c == 2:
                    dve.tensor_copy(g.v1[:, t, :, 0:HD1], bank[:, :].rearrange("p (h d) -> p h d", h=H1))\
                       .then_inc(freed[n % 4], 1)
                    continue
                r = rotated.index((t, c))
                dve.wait_ge(s_["cos_done"], r + 1)
                if r >= 2:
                    dve.wait_ge(s_["odd"], r - 1)
                dve.tensor_scalar(by_sin[:, r % 2, :], bank[:, :], trig[:, c, 1, t % TT:t % TT + 1], None, ALU.mult)\
                   .then_inc(freed[n % 4], 1)


def layer1_attention(nc, g, b):
    with ExitStack() as ctx:
        g.sem = semaphores(nc, ctx)
        sb = lambda n, s, t=F32: ctx.enter_context(nc.sbuf_tensor(f"a1{b}_{n}", s, t))
        sem = lambda n: g.sem(f"a1{b}_{n}")
        PR = H1 // 2
        stack = sb("stack", [P, 2, H1, 4, HD1], F32R)
        turned = [sb(n, [P, PR, T], F32R) for n in ("q", "k")]
        probs = sb("probs", [P, 2, TT, T])
        BLOCKS = TT * (TT + 1) // 2
        pt = sb("pt", [P, 2, BLOCKS, P])
        out_t = sb("out_t", [P, TT, P])
        negmax = sb("negmax", [P, 2, TT])
        rsum = sb("rsum", [P, 2, TT, 4])
        names = ("hi", "lo", "turn", "taken_a", "taken_v", "scores", "maxed", "exped", "pt_mm", "pt_a", "pt_v",
                 "pv", "out_t", "back", "rsummed", "normed")
        s_ = {n: sem(n) for n in names}
        SB = 3
        score_banks, back_bank, turn_banks, out_banks = g.bank[0:SB], g.bank[3], g.bank[4:6], g.bank[6:8]
        stacks = [(t, c) for t in range(TT) for c in range(2)]
        STRIPS = [[(j, u) for j in js for u in range(j, TT)] for js in ((0,), (1,), (2, 3))]
        FIRST = [0, 4, 7]
        where = {ju: FIRST[n] + m for n, strip in enumerate(STRIPS) for m, ju in enumerate(strip)}
        HG = 4
        HP = P // HG

        block = ctx.enter_context(nc.Block())

        def copies(c, n, lo):
            s = stack[:, n % 2, :, :, :]
            if c == 0:
                return s[:, :, lo:4:2, :]
            return s[:, :, 2 * lo:2 * lo + 2, :]

        def source(t, c):
            return (g.q1 if c == 0 else g.k1)[:, b * TT + t, :].rearrange("p (h d) -> p h d", h=H1)\
                .unsqueeze(2).to_broadcast([P, H1, 2, HD1])

        def wait_turned_copy(eng, h, n):
            eng.wait_ge(*((s_["pt_a"], h + 1) if n == 2 else (s_["pt_v"], 2 * h + n + 1)))

        @block.tensor
        def _(pe):
            for n, (t, c) in enumerate(stacks):
                pe.wait_ge(s_["lo"], n + 1)
                flat = stack[:, n % 2, :, :, :].rearrange("p h a d -> p (h a d)").bitcast(F32)
                for q in range(4):
                    m = 4 * n + q
                    if m >= 8:
                        pe.wait_ge((s_["taken_a"], s_["taken_v"])[m % 2], (m - 8) // 2 + 1)
                    for r in range(4):
                        mm = pe.transpose(g.bank[m % 8][:, r * P:(r + 1) * P],
                                          flat[:, (q * 4 + r) * P:(q * 4 + r + 1) * P], g.ident[:, :])
                    mm.then_inc(s_["turn"], 1)
            pe.wait_ge(s_["taken_a"], 16)
            pe.wait_ge(s_["taken_v"], 16)

            def score(h, u):
                n = h * TT + u
                if n >= SB:
                    pe.wait_ge(s_["exped"], n - SB + 1)
                rows = slice(SLOT * (h % 2), SLOT * (h % 2 + 1))
                w = max(2, u + 1) * P
                bank = score_banks[n % SB]
                pe.matmul(bank[:, 0:w], turned[0][rows, h // 2, u * P:(u + 1) * P], turned[1][rows, h // 2, 0:w],
                          start=True, stop=False)
                pe.matmul(bank[:, u * P:(u + 1) * P], g.eye16[:, :], g.mask[:, :], start=False, stop=True)\
                    .then_inc(s_["scores"], 1)

            def turn(h, n):
                pe.wait_ge(s_["exped"], (h + 1) * TT)
                k = 3 * h + n
                if k >= 2:
                    wait_turned_copy(pe, *divmod(k - 2, 3))
                for m, (j, u) in enumerate(STRIPS[n]):
                    mm = pe.transpose(turn_banks[k % 2][:, m * P:(m + 1) * P], probs[:, h % 2, u, j * P:(j + 1) * P],
                                      g.ident[:, :])
                mm.then_inc(s_["pt_mm"], 1)

            def values(h, j):
                grp, i = h // HG, h % HG
                wait_turned_copy(pe, h, min(j, 2))
                if j == 0 and i == 0 and grp >= 2:
                    pe.wait_ge(s_["out_t"], grp - 1)
                mm = pe.matmul(out_banks[grp % 2][i * HP:i * HP + VW, j * P:], g.v1[:, b * TT + j, h, :],
                               pt[:, h % 2, where[j, j]:where[j, j] + TT - j, :].rearrange("p a x -> p (a x)"),
                               start=(j == 0), stop=(j == TT - 1))
                if j == TT - 1:
                    mm.then_inc(s_["pv"], 1)

            def back(grp):
                pe.wait_ge(s_["out_t"], grp + 1)
                if grp:
                    pe.wait_ge(s_["normed"], grp)
                for u in range(TT):
                    mm = pe.transpose(back_bank[:, u * P:(u + 1) * P], out_t[:, u, :], g.ident[:, :])
                mm.then_inc(s_["back"], 1)

            for h in range(H1 + 2):
                new, old, oldest = h < H1, 1 <= h <= H1, h >= 2
                if new:
                    score(h, 0)
                if oldest:
                    values(h - 2, 0)
                if new:
                    score(h, 1)
                if oldest:
                    values(h - 2, 1)
                if old:
                    turn(h - 1, 0)
                if new:
                    score(h, 2)
                if new:
                    score(h, 3)
                if old:
                    turn(h - 1, 1)
                if oldest:
                    values(h - 2, 2)
                if old:
                    turn(h - 1, 2)
                if oldest:
                    values(h - 2, 3)
                if h >= HG + 2 and (h - 2) % HG == 0:
                    back((h - 2) // HG - 1)
            back(H1 // HG - 1)

        @block.scalar
        def _(act):
            def hi(n):
                if n >= 2:
                    act.wait_ge(s_["turn"], 4 * (n - 1))
                act.activation(copies(stacks[n][1], n, 0), source(*stacks[n]), ACT.Copy).then_inc(s_["hi"], 1)

            hi(0)
            for n, (t, c) in enumerate(stacks):
                if n + 1 < len(stacks):
                    hi(n + 1)
                for q in range(0, 4, 2):
                    m = 4 * n + q
                    act.wait_ge(s_["turn"], m + 1)
                    act.activation(turned[c][:, q * 4:q * 4 + 4, t * P:(t + 1) * P],
                                   g.bank[m % 8][:, :].rearrange("p (a x) -> p a x", a=4), ACT.Copy)\
                       .then_inc(s_["taken_a"], 1)

            def take(h):
                act.wait_ge(s_["pt_mm"], 3 * h + 3)
                if h >= 2:
                    act.wait_ge(s_["pv"], h - 1)
                act.activation(pt[:, h % 2, FIRST[2]:, :], turn_banks[(3 * h + 2) % 2][:, 0:3 * P]
                               .rearrange("p (a x) -> p a x", a=3), ACT.Copy).then_inc(s_["pt_a"], 1)

            def out_of_bank(grp):
                act.wait_ge(s_["pv"], HG * (grp + 1))
                if grp:
                    act.wait_ge(s_["back"], grp)
                act.activation(out_t[:, :, :], out_banks[grp % 2][:, :].rearrange("p (u x) -> p u x", u=TT), ACT.Copy)\
                    .then_inc(s_["out_t"], 1)

            for h in range(H1 + 1):
                for u in range(TT):
                    n = h * TT + u
                    if h < H1:
                        act.wait_ge(s_["maxed"], n + 1)
                        if h >= 2 and u == 0:
                            act.wait_ge(s_["pt_mm"], 3 * (h - 1))
                        act.activation(probs[:, h % 2, u, 0:(u + 1) * P], score_banks[n % SB][:, 0:(u + 1) * P],
                                       ACT.Exp, bias=negmax[:, h % 2, u:u + 1]).then_inc(s_["exped"], 1)
                    if u == 0 and h >= HG + 2 and (h - 2) % HG == 0:
                        out_of_bank((h - 2) // HG - 1)
                    if u == 3 and h:
                        take(h - 1)
            out_of_bank(H1 // HG - 1)

        @block.vector
        def _(dve):
            def lo(n):
                dve.wait_ge(s_["hi"], n + 1)
                hi = stack[:, n % 2, :, 0:1, :].bitcast(F32).to_broadcast([P, H1, 2, HD1])
                dve.tensor_tensor(copies(stacks[n][1], n, 1), source(*stacks[n]), hi, ALU.subtract)\
                   .then_inc(s_["lo"], 1)

            lo(0)
            for n, (t, c) in enumerate(stacks):
                if n + 1 < len(stacks):
                    lo(n + 1)
                for q in range(1, 4, 2):
                    m = 4 * n + q
                    dve.wait_ge(s_["turn"], m + 1)
                    dve.tensor_copy(turned[c][:, q * 4:q * 4 + 4, t * P:(t + 1) * P],
                                    g.bank[m % 8][:, :].rearrange("p (a x) -> p a x", a=4)).then_inc(s_["taken_v"], 1)

            def take(h, n):
                dve.wait_ge(s_["pt_mm"], 3 * h + n + 1)
                if n == 0 and h >= 2:
                    dve.wait_ge(s_["pv"], h - 1)
                k = len(STRIPS[n])
                dve.tensor_copy(pt[:, h % 2, FIRST[n]:FIRST[n] + k, :],
                                turn_banks[(3 * h + n) % 2][:, 0:k * P].rearrange("p (a x) -> p a x", a=k))\
                   .then_inc(s_["pt_v"], 1)

            def finish(grp):
                out = back_bank[:, :].rearrange("p (u h d) -> p u h d", u=TT, h=HG)
                dve.wait_ge(s_["back"], grp + 1)
                dve.reciprocal(rsum[:, grp % 2, :, :], out[:, :, :, HD1]).then_inc(s_["rsummed"], 1)
                dve.wait_ge(s_["rsummed"], grp + 1)
                dst = g.q1[:, b * TT:(b + 1) * TT, grp * HG * HD1:(grp + 1) * HG * HD1]\
                    .rearrange("p u (h d) -> p u h d", h=HG)
                dve.tensor_tensor(dst, out[:, :, :, 0:HD1],
                                  rsum[:, grp % 2, :, :].unsqueeze(3).to_broadcast([P, TT, HG, HD1]), ALU.mult)\
                   .then_inc(s_["normed"], 1)

            for h in range(H1 + 1):
                for u in range(TT):
                    if h < H1:
                        n = h * TT + u
                        dve.wait_ge(s_["scores"], n + 1)
                        dve.tensor_reduce(negmax[:, h % 2, u:u + 1], score_banks[n % SB][:, 0:(u + 1) * P], AX_X,
                                          ALU.max, negate=True).then_inc(s_["maxed"], 1)
                    if u == 0 and h >= HG + 3 and (h - 3) % HG == 0:
                        finish((h - 3) // HG - 1)
                    if h and u == 1:
                        take(h - 1, 0)
                    if h and u == 3:
                        take(h - 1, 1)
            finish(H1 // HG - 1)


def layer1_output(nc, outer, g, weights):
    with ExitStack() as ctx:
        g.sem = semaphores(nc, ctx)
        sb = lambda n, s, t=F32: ctx.enter_context(nc.sbuf_tensor(f"o1_{n}", s, t))
        sem = lambda n: g.sem(f"o1_{n}")
        rows = GateRows(nc, outer, g, "rows2", g.gate1, (0, 1), g.bank[6:8])
        gated = sb("gated", [P, 2, D])
        w = [sb(f"w_{p}", [P, KT, D], F32R) for p in ("hi", "lo")]
        chunks = Weights(nc, ctx, g, "o1", [(weights[3 * KT + k], w[0][:, k, :], w[1][:, k, :]) for k in range(KT)], KT)
        o = [sb(f"o_{p}", [P, KT, B * T], F32R) for p in ("hi", "lo")]
        s_ = {n: sem(n) for n in ("turn", "hi", "lo", "mm", "gated", "summed")}
        block = ctx.enter_context(nc.Block())

        @block.sync
        def _(sync):
            chunks.load(sync)

        @block.gpsimd
        def _(pool):
            chunks.pool(pool, range(KT))
            for t in range(NT):
                pool.wait_ge(s_["gated"], t + 1)
                pool.tensor_tensor(g.x[:, t, :], g.x[:, t, :], gated[:, t % 2, :], ALU.add).then_inc(s_["summed"], 1)

        @block.tensor
        def _(pe):
            def turn(t):
                if t >= 2:
                    pe.wait_ge(s_["lo"], t - 1)
                for k in range(KT):
                    mm = pe.transpose(g.bank[t % 2][:, k * P:(k + 1) * P], g.q1[:, t, k * P:(k + 1) * P], g.ident[:, :])
                mm.then_inc(s_["turn"], 1)

            turn(0)
            turn(1)
            rows.pe(pe)
            for t in range(NT):
                if t + 2 < NT:
                    turn(t + 2)
                pe.wait_ge(s_["lo"], t + 1)
                if t == 0:
                    pe.wait_ge(chunks.split, KT)
                if t >= 4:
                    pe.wait_ge(s_["gated"], t - 3)
                for k in range(KT):
                    mm = three_passes(pe, g.bank[2 + t % 4][:, :], [x[:, k, t * P:(t + 1) * P] for x in o],
                                      [x[:, k, :] for x in w], k, k == 0, k == KT - 1)
                mm.then_inc(s_["mm"], 1)

        @block.scalar
        def _(act):
            for t in range(NT):
                if t == 2:
                    chunks.act(act, range(KT))
                act.wait_ge(s_["turn"], t + 1)
                act.activation(o[0][:, :, t * P:(t + 1) * P], g.bank[t % 2][:, :].rearrange("p (k x) -> p k x", k=KT),
                               ACT.Copy).then_inc(s_["hi"], 1)

        @block.vector
        def _(dve):
            def out(t):
                dve.wait_ge(s_["mm"], t + 1)
                if t >= 2:
                    dve.wait_ge(s_["summed"], t - 1)
                dve.tensor_tensor(gated[:, t % 2, :], g.bank[2 + t % 4][:, :], rows.out[:, 0, t // TT, :], ALU.mult)\
                   .then_inc(s_["gated"], 1)

            for t in range(NT):
                dve.wait_ge(s_["hi"], t + 1)
                dve.tensor_tensor(o[1][:, :, t * P:(t + 1) * P], g.bank[t % 2][:, :].rearrange("p (k x) -> p k x", k=KT),
                                  o[0][:, :, t * P:(t + 1) * P].bitcast(F32), ALU.subtract).then_inc(s_["lo"], 1)
                if t == 1:
                    rows.dve(dve)
                if t >= 2:
                    out(t - 2)
            out(NT - 2)
            out(NT - 1)
        return rows



def layer1_experts(nc, g, rows, weights, a_w, b_w, bias_row, out_dram):
    with ExitStack() as ctx:
        g.sem = semaphores(nc, ctx)
        sb = lambda n, s, t=F32: ctx.enter_context(nc.sbuf_tensor(f"l1_{n}", s, t))
        sem = lambda n: g.sem(f"l1_{n}")
        ER = E1 * R1
        norm = Norm(nc, ctx, g, "n3", 4, 3, hf=g.q1[:, :, :].rearrange("p (k a) d -> p k (a d)", k=KT), xn=g.y)
        w = [sb(f"w_{p}", [P, 2, KT, D], F32R) for p in ("hi", "lo")]
        bw = [sb(f"b_{p}", [P, D], F32R) for p in ("hi", "lo")]
        chunks = Weights(nc, ctx, g, "l1", [(weights[(4 + c) * KT + k], w[0][:, c, k, :], w[1][:, c, k, :])
                                            for c in (1, 0) for k in range(KT)]
                         + [(b_w, bw[0][:, :], bw[1][:, :])], KT + 2)
        aw = sb("aw", [P, KT, ER])
        bias = sb("bias", [P, D])
        k_sb = sb("k_sb", [P, 2, E1 * DK1])
        qk = sb("qk", [P, 2, E1 * DK1])
        sc, ex, wt = (sb(n, [P, 2, E1]) for n in ("sc", "ex", "wt"))
        mx, sm, rs = (sb(n, [P, 2]) for n in ("mx", "sm", "rs"))
        wh = sb("wh", [P, 2, ER])
        wht = [sb(f"wht_{p}", [P, 2, P], F32R) for p in ("hi", "lo")]
        gated_bias = sb("gated_bias", [P, B, D])
        gated = sb("gated", [P, 2, D])
        final = sb("final", [P, 2, D])
        names = ("small_in", "qk_mm", "a_mm", "k_copied", "chain", "scored", "exped",
                 "rs", "wt", "weighted", "turned", "t_hi", "t_lo", "b_mm", "bias_gated", "based", "gated", "final")
        s_ = {n: sem(n) for n in names}
        stored = [sem(f"stored{r}") for r in range(2)]
        block = ctx.enter_context(nc.Block())

        @block.sync
        def _(sync):
            for dst, src in ((aw[:, :, :], a_w), (bias[:, :], bias_row)):
                sync.dma_start(dst, src).then_inc(s_["small_in"], 16)
            chunks.load(sync)
            for t in range(NT):
                sync.wait_ge(s_["final"], t + 1)
                sync.dma_start(out_dram[t * P:(t + 1) * P, :], final[:, t % 2, :]).then_inc(stored[t % 2], 16)
            for slot in stored:
                sync.wait_ge(slot, 16 * (NT // 2))

        @block.gpsimd
        def _(pool):
            chunks.pool(pool, range(2 * KT + 1))
            pool.wait_ge(s_["small_in"], 32)
            for b in range(B):
                pool.tensor_tensor(gated_bias[:, b, :], bias[:, :], rows.out[:, 1, b, :], ALU.mult)\
                    .then_inc(s_["bias_gated"], 1)
            pool.wait_ge(s_["bias_gated"], B)
            for t in range(NT):
                pool.wait_ge(norm.normed, t + 1)
                pool.tensor_tensor(g.x[:, t, :], g.x[:, t, :], gated_bias[:, t // TT, :], ALU.add)\
                    .then_inc(s_["based"], 1)

        @block.tensor
        def _(pe):
            def query_keys(t):
                cols = slice(t * P, (t + 1) * P)
                if t == 0:
                    pe.wait_ge(chunks.split, KT)
                    pe.wait_ge(norm.affine, B * KT)
                if t % TT == 0:
                    pe.wait_ge(norm.split_lo, (t // TT + 1) * KT)
                if t >= 2:
                    pe.wait_ge(s_["scored"], t - 1)
                for k in range(KT):
                    mm = three_passes(pe, g.bank[3 + t % 2][:, :], [x[:, k, cols] for x in (g.hh, g.hl)],
                                      [x[:, 1, k, :] for x in w], k, k == 0, k == KT - 1)
                mm.then_inc(s_["qk_mm"], 1)

            def down_and_whole(t):
                cols = slice(t * P, (t + 1) * P)
                pe.wait_ge(s_["small_in"], 32)
                if t >= 2:
                    pe.wait_ge(s_["weighted"], t - 1)
                for k in range(KT):
                    mm = pe.matmul(g.bank[5 + t % 2][:, 0:ER], norm.hf[:, k, cols], aw[:, k, :],
                                   start=(k == 0), stop=(k == KT - 1))
                mm.then_inc(s_["a_mm"], 1)
                if t == 0:
                    pe.wait_ge(chunks.split, 2 * KT)
                if t >= 3:
                    pe.wait_ge(s_["gated"], t - 2)
                for k in range(KT):
                    mm = three_passes(pe, g.bank[t % 3][:, :], [x[:, k, cols] for x in (g.hh, g.hl)],
                                      [x[:, 0, k, :] for x in w], k, k == 0, False)

            norm.pe(pe)
            query_keys(0)
            down_and_whole(0)
            for t in range(NT):
                if t + 1 < NT:
                    query_keys(t + 1)
                pe.wait_ge(s_["weighted"], t + 1)
                if t >= 1:
                    pe.wait_ge(s_["t_lo"], t)
                pe.transpose(g.bank[7][:, 0:P], wh[:, t % 2, :], g.ident[:, :]).then_inc(s_["turned"], 1)
                if t + 1 < NT:
                    down_and_whole(t + 1)
                pe.wait_ge(s_["t_lo"], t + 1)
                if t == 0:
                    pe.wait_ge(chunks.split, 2 * KT + 1)
                three_passes(pe, g.bank[t % 3][:, :], [x[:, t % 2, :] for x in wht], [x[:, :] for x in bw],
                             0, False, True).then_inc(s_["b_mm"], 1)

        @block.scalar
        def _(act):
            chunks.act(act, range(KT))
            norm.act(act)
            chunks.act(act, range(KT, 2 * KT + 1))
            for t in range(NT):
                act.wait_ge(s_["qk_mm"], t + 1)
                if t >= 2:
                    act.wait_ge(s_["scored"], t - 1)
                act.activation(k_sb[:, t % 2, :], g.bank[3 + t % 2][:, E1 * DK1:2 * E1 * DK1], ACT.Copy)\
                    .then_inc(s_["k_copied"], 1)
                act.wait_ge(s_["chain"], 3 * t + 3)
                act.activation(ex[:, t % 2, :], sc[:, t % 2, :], ACT.Exp, bias=mx[:, t % 2:t % 2 + 1],
                               scale=float(DK1) ** -0.5, accum_out=sm[:, t % 2:t % 2 + 1]).then_inc(s_["exped"], 1)
                act.wait_ge(s_["turned"], t + 1)
                if t >= 2:
                    act.wait_ge(s_["b_mm"], t - 1)
                act.activation(wht[0][:, t % 2, :], g.bank[7][:, 0:P], ACT.Copy).then_inc(s_["t_hi"], 1)

        @block.vector
        def _(dve):
            norm.dve_stats(dve)
            norm.dve_split(dve)
            dve.wait_ge(s_["small_in"], 32)

            def split_turned(t):
                dve.wait_ge(s_["t_hi"], t + 1)
                dve.tensor_tensor(wht[1][:, t % 2, :], g.bank[7][:, 0:P], wht[0][:, t % 2, :].bitcast(F32),
                                  ALU.subtract).then_inc(s_["t_lo"], 1)

            def finish(t):
                dve.wait_ge(s_["b_mm"], t + 1)
                dve.tensor_tensor(gated[:, t % 2, :], g.bank[t % 3][:, :], rows.out[:, 1, t // TT, :], ALU.mult)\
                   .then_inc(s_["gated"], 1)
                dve.wait_ge(s_["gated"], t + 1)
                dve.wait_ge(s_["based"], t + 1)
                if t >= 2:
                    dve.wait_ge(stored[t % 2], 16 * (t // 2))
                dve.tensor_tensor(final[:, t % 2, :], gated[:, t % 2, :], g.x[:, t, :], ALU.add)\
                   .then_inc(s_["final"], 1)

            for t in range(NT):
                p = t % 2
                dve.wait_ge(s_["k_copied"], t + 1)
                dve.tensor_tensor(qk[:, p, :], g.bank[3 + p][:, 0:E1 * DK1], k_sb[:, p, :], ALU.mult)\
                   .then_inc(s_["scored"], 1)
                dve.wait_ge(s_["scored"], t + 1)
                dve.tensor_reduce(sc[:, p, :], qk[:, p, :].rearrange("p (e d) -> p e d", e=E1), AX_X, ALU.add)\
                   .then_inc(s_["chain"], 1)
                dve.wait_ge(s_["chain"], 3 * t + 1)
                dve.tensor_reduce(mx[:, p:p + 1], sc[:, p, :], AX_X, ALU.max, negate=True).then_inc(s_["chain"], 1)
                dve.wait_ge(s_["chain"], 3 * t + 2)
                dve.tensor_scalar(mx[:, p:p + 1], mx[:, p:p + 1], float(DK1) ** -0.5, None, ALU.mult)\
                   .then_inc(s_["chain"], 1)
                dve.wait_ge(s_["exped"], t + 1)
                dve.reciprocal(rs[:, p:p + 1], sm[:, p:p + 1]).then_inc(s_["rs"], 1)
                dve.wait_ge(s_["rs"], t + 1)
                dve.tensor_scalar(wt[:, p, :], ex[:, p, :], rs[:, p:p + 1], None, ALU.mult).then_inc(s_["wt"], 1)
                dve.wait_ge(s_["wt"], t + 1)
                dve.wait_ge(s_["a_mm"], t + 1)
                if t >= 2:
                    dve.wait_ge(s_["turned"], t - 1)
                dve.tensor_tensor(wh[:, p, :].rearrange("p (e r) -> p e r", e=E1),
                                  g.bank[5 + p][:, 0:ER].rearrange("p (e r) -> p e r", e=E1),
                                  wt[:, p, :].unsqueeze(2).to_broadcast([P, E1, R1]), ALU.mult)\
                   .then_inc(s_["weighted"], 1)
                split_turned(t)
                if t:
                    finish(t - 1)
            finish(NT - 1)



def build(nc, a, out):
    with ExitStack() as ctx:
        sb = lambda n, s, t=F32: ctx.enter_context(nc.sbuf_tensor(n, s, t))
        g = Shared()
        g.bank = [ctx.enter_context(nc.psum_tensor(f"bank{i}", [P, 512], F32)) for i in range(8)]
        g.y = sb("y", [P, NT, D])

        def operands(scope, name):
            g.hh, g.hl = (scope.enter_context(nc.sbuf_tensor(f"h_{p}_{name}", [P, KT, B * T], F32R))
                          for p in ("hi", "lo"))

        g.mod = sb("mod", [P, 6, KT * B])
        g.pick = sb("pick", [B, B, P])
        g.ident = sb("ident", [P, P])
        g.eye16 = sb("eye16", [P, P], BF16)
        g.mask = sb("mask", [P, P], BF16)
        g.passed = ctx.enter_context(nc.semaphore("passed"))
        g.ready = ctx.enter_context(nc.semaphore("ready"))

        part = ctx.enter_context(ExitStack())
        operands(part, "attention0")
        with ExitStack() as ph:
            sem = g.sem = semaphores(nc, ph)
            g.x = ph.enter_context(nc.sbuf_tensor("x_first", [P, NT, D], F32))
            mod = Modulation(nc, ph, g, "m0", a["c0"], a["wmod0"], g.bank[4:8])
            norm = Norm(nc, ph, g, "n0", 1, 0, x_dram=a["x"], mod_ready=(mod.chain, 2))
            gate = ph.enter_context(nc.sbuf_tensor("gate_first", [B, 2, D], F32))
            zeroed, eyed, picked, stored = (sem(n) for n in ("zeroed", "eyed", "picked", "stored"))
            block = ph.enter_context(nc.Block())

            @block.sync
            def _(sync):
                mod.load_c(sync)
                norm.load(sync, range(TT))
                mod.load(sync, 0)
                mod.load(sync, 1)
                norm.load(sync, range(TT, NT))
                for n in range(2, 6):
                    mod.load(sync, n)
                sync.wait_ge(mod.chain, 6)
                sync.dma_start(a["gate0"], gate[0:B, :, :]).then_inc(stored, 16)
                sync.wait_ge(stored, 16)

            @block.gpsimd
            def _(pool):
                pool.memset(g.ident[:, :], 0.0).then_inc(zeroed, 1)
                pool.memset(g.eye16[:, :], 0.0).then_inc(zeroed, 1)
                pool.memset(g.mask[:, :], 0.0).then_inc(zeroed, 1)
                pool.wait_ge(zeroed, 3)
                for eye in (g.ident, g.eye16):
                    pool.affine_select(out=eye[:, :], in_=eye[:, :], compare_op=ALU.not_equal, fill=1.0,
                                       base=0, pattern=[[-1, P]], channel_multiplier=1).then_inc(eyed, 1)
                pool.wait_ge(eyed, 2)
                pool.tensor_copy(g.pick[:, :, :], g.ident[0:B, 0:B].unsqueeze(2).to_broadcast([B, B, P]))\
                    .then_inc(picked, 1)
                pool.affine_select(out=g.mask[:, :], in_=g.mask[:, :], compare_op=ALU.is_ge, fill=NEG,
                                   base=0, pattern=[[-1, P]], channel_multiplier=1).then_inc(g.ready, 1)

            @block.scalar
            def _(act):
                mod.act(act)
                norm.act(act)

            @block.tensor
            def _(pe):
                pe.wait_ge(eyed, 2)
                mod.pe_rows(pe, (0, 1))
                mod.pe_columns(pe, (0, 1))
                norm.pe(pe)
                mod.pe_rows(pe, range(2, 6))
                mod.pe_columns(pe, (4, 5))

            @block.vector
            def _(dve):
                norm.dve_stats(dve)
                mod.dve_rows(dve, (0, 1))
                mod.dve_columns(dve, 0)
                norm.dve_split(dve)
                mod.dve_rows(dve, (2, 3))
                mod.dve_gates(dve, gate)
                mod.dve_rows(dve, (4, 5))
                mod.dve_columns(dve, 1)
        layer0_attention(nc, g, a["chunks"], a["wv_chunks"], a["rope"])
        part.close()

        g.gate0, g.gate1 = (sb(f"gate{l}", [B, 2, D]) for l in (0, 1))
        g.x = sb("x", [P, NT, D])
        part = ctx.enter_context(ExitStack())
        g.gates = part.enter_context(nc.sbuf_tensor("gates", [P, NT, EX], F32))
        operands(part, "experts")
        with ExitStack() as ph:
            sem = g.sem = semaphores(nc, ph)
            gate_in = sem("gate_in")
            rows = GateRows(nc, ph, g, "rows0", g.gate0, (0,), g.bank[6:8])
            norm = Norm(nc, ph, g, "n1", 4, 3, gate=rows, x_dram=a["x"])
            router = Router(nc, ph, g, norm, g.bank[4], a["router_w"], a["router_b"], a["router_bias"], a["descend"])
            block = ph.enter_context(nc.Block())

            @block.sync
            def _(sync):
                sync.dma_start(g.gate0[0:B, :, :], a["gate0"]).then_inc(gate_in, 16)
                norm.load(sync)

            @block.gpsimd
            def _(pool):
                norm.pool(pool)

            @block.scalar
            def _(act):
                router.load(act)
                norm.act(act)
                router.act(act)

            @block.tensor
            def _(pe):
                pe.wait_ge(gate_in, 16)
                rows.pe(pe)
                norm.pe(pe)
                router.pe(pe)

            @block.vector
            def _(dve):
                rows.dve(dve)
                norm.dve_stats(dve)
                norm.dve_split(dve)
                router.dve(dve)

        layer0_experts(nc, g, a["expert_chunks"], a["expert_biases"], a["expert_b3"], a["c1"], a["wmod1"])
        part.close()

        g.q1 = sb("q1", [P, NT, D])
        g.v1 = sb("v1", [P, NT, H1, VW])
        g.k1 = g.y
        part = ctx.enter_context(ExitStack())
        operands(part, "attention1")
        layer1_projections(nc, g, a["l1_chunks"], a["rope1"])
        part.close()
        for b in range(B):
            layer1_attention(nc, g, b)
        rows = layer1_output(nc, ctx, g, a["l1_chunks"])

        operands(ctx, "experts1")
        layer1_experts(nc, g, rows, a["l1_chunks"], a["lora_a"], a["lora_b"], a["l1_bias"], out)


def lay_out(i):
    n = lambda k: np.asarray(i[k])
    a = {}
    a["x"] = np.ascontiguousarray(n("L0_attn_x").reshape(B * T, D))
    for l in (0, 1):
        w = n(f"L{l}_wmod").reshape(KT, P, 6, D).transpose(2, 0, 1, 3)[list(MOD_ORDER)]
        a[f"wmod{l}"] = np.ascontiguousarray(w).reshape(6 * KT, P, D)
        a[f"c{l}"] = np.ascontiguousarray(n(f"L{l}_c").reshape(B, KT, P).transpose(2, 1, 0))
    a["rope"] = rope_tables()
    kt = lambda w: w.reshape(KT, P, w.shape[1]).transpose(1, 0, 2)
    wq, wk, wv, wo = (n(f"L0_attn_w{c}") for c in "qkvo")
    chunks = np.empty((KV0, 1 + 2 * REP, P, 512), np.float32)
    for kv in range(KV0):
        chunks[kv, 0] = kt(wk[:, kv * HD0:(kv + 1) * HD0]).reshape(P, 512)
        for r in range(REP):
            h = kv * REP + r
            chunks[kv, 1 + r] = kt(wq[:, h * HD0:(h + 1) * HD0]).reshape(P, 512)
            chunks[kv, 1 + REP + r] = wo[h * HD0:(h + 1) * HD0]
    a["chunks"] = chunks.reshape(KV0 * (1 + 2 * REP), P, 512)
    wvc = np.empty((PAIRS, 2, P, 512), np.float32)
    for pr in range(PAIRS):
        w = kt(wv[:, pr * 2 * HD0:(pr + 1) * 2 * HD0])
        for c in range(2):
            wvc[pr, c] = w[:, 2 * c:2 * c + 2].reshape(P, 512)
    a["wv_chunks"] = wvc.reshape(PAIRS * 2, P, 512)
    f = lambda k: n("L0_ffn_" + k)
    a["router_w"] = np.ascontiguousarray(kt(f("router_w")))
    for k in ("router_b", "router_bias"):
        a[k] = np.ascontiguousarray(np.broadcast_to(f(k), (P, E0)))
    a["descend"] = np.ascontiguousarray(np.broadcast_to(np.arange(E0, 0, -1, dtype=np.float32), (P, E0)))
    ec = np.empty((EX, 3, P, 512), np.float32)
    eb = np.empty((P, EX, 2), np.float32)
    b3 = np.zeros((EX, D), np.float32)
    for e in range(E0):
        ec[e, 0], ec[e, 1] = (kt(f(k)[e]).reshape(P, 512) for k in ("ew1", "ew2"))
        ec[e, 2] = f("ew3")[e]
        eb[:, e, 0], eb[:, e, 1] = f("eb1")[e], f("eb2")[e]
    b3[:E0], b3[E0] = f("eb3"), f("sb3")
    for m in range(2):
        c = slice(m * INTER, (m + 1) * INTER)
        ec[E0 + m, 0], ec[E0 + m, 1] = (kt(f(k)[:, c]).reshape(P, 512) for k in ("sw1", "sw2"))
        ec[E0 + m, 2] = f("sw3")[c]
        eb[:, E0 + m, 0], eb[:, E0 + m, 1] = f("sb1")[c], f("sb2")[c]
    l1 = [n(f"L1_attn_w{c}").T for c in "qkvo"] + [n("L1_ffn_W").T, np.concatenate(
        [n("L1_ffn_Wq").T, n("L1_ffn_Wk").T], axis=1)]
    a["l1_chunks"] = np.ascontiguousarray(np.stack(l1).reshape(6 * KT, P, D))
    a["lora_a"] = np.ascontiguousarray(kt(n("L1_ffn_A").reshape(E1 * R1, D).T))
    a["lora_b"] = np.ascontiguousarray(n("L1_ffn_Bm").transpose(0, 2, 1).reshape(E1 * R1, D))
    a["l1_bias"] = np.ascontiguousarray(np.broadcast_to(n("L1_ffn_b"), (P, D)))
    a["rope1"] = rope1_tables()
    a["expert_chunks"], a["expert_biases"], a["expert_b3"] = ec.reshape(EX * 3, P, 512), eb, b3
    return a


def program(nc, arrays):
    a = {k: nc.dram_tensor(f"in_{k}", v.shape, mybir.dt.from_np(v.dtype), kind="ExternalInput").ap()
         for k, v in arrays.items()}
    a["gate0"] = nc.dram_tensor("gate_scratch", (B, 2, D), F32, kind="Internal").ap()
    out = nc.dram_tensor("out", (B * T, D), F32, kind="ExternalOutput").ap()
    build(nc, a, out)


def kernel(**inputs):
    import concourse.bacc as _bacc
    from concourse.bass_utils import run_bass_kernel_spmd as _run

    nc = _bacc.Bacc("TRN2", target_bir_lowering=False, num_devices=1)
    arrays = lay_out(inputs)
    program(nc, arrays)
    r = _run(nc, [{f"in_{k}": v for k, v in arrays.items()}], core_ids=[0])
    return r.results[0]["out"].reshape(B, T, D)
```
